# Optimizing a Trainium2 kernel written in Bass

```python
import numpy as np
import jax
import jax.numpy as jnp

def _softmax(x, axis=-1):
    return jax.nn.softmax(x, axis=axis)

def _gelu(x):
    return jax.nn.gelu(x, approximate=True)

def _silu(x):
    return jax.nn.silu(x)

def _sigmoid(x):
    return jax.nn.sigmoid(x)

def _layernorm(x, axis=-1, eps=1e-05):
    m = jnp.mean(x, axis=axis, keepdims=True)
    v = jnp.var(x, axis=axis, keepdims=True)
    return (x - m) / jnp.sqrt(v + eps)

def _scatter_add(tgt, idx, src, axis=0):
    return tgt.at[idx].add(src)

def _segment_sum(src, seg, n):
    return jax.ops.segment_sum(src, seg, n)
kernel_name = 'mk_seq_postln_d1_jaxref_r4_554610'

def setup_inputs(seed: int=0):
    np.random.seed(seed)
    _w = jnp.asarray

    def _L0_attn_setup():
        import jax, jax.numpy as jnp
        import numpy as np
        NUM_HEADS = 16
        ROPE_BASE = 10000.0
        QK_GAIN_INIT = 12.0
        EPS = 1e-06
        ROPE_MASK = jnp.asarray(np.tile([1.0, 0.0], NUM_HEADS // 2), dtype=jnp.float32)

        def _rope_cos_sin(seqlen, head_dim, dtype):
            half = head_dim // 2
            inv_freq = ROPE_BASE ** (-jnp.arange(0, half, dtype=jnp.float32) / half)
            theta = jnp.arange(seqlen, dtype=jnp.float32)[:, None] * inv_freq[None, :]
            return (jnp.cos(theta).astype(dtype), jnp.sin(theta).astype(dtype))

        def _apply_rope(t, cos, sin):
            d2 = t.shape[-1] // 2
            t1, t2 = (t[..., :d2], t[..., d2:])
            c = cos[None, :, None, :]
            s = sin[None, :, None, :]
            return jnp.concatenate([t1 * c - t2 * s, t1 * s + t2 * c], axis=-1)

        def _unit_norm(t):
            return t * jax.lax.rsqrt(jnp.sum(t * t, axis=-1, keepdims=True) + EPS)
        key = jax.random.key(seed)
        k0, k1, k2 = jax.random.split(key, 3)
        B, S, Dm = (2, 512, 512)
        x = jax.random.normal(k0, (B, S, Dm), dtype=jnp.float32)
        w_qkv = jax.random.normal(k1, (Dm, 3 * Dm), dtype=jnp.float32) * Dm ** (-0.5)
        w_out = jax.random.normal(k2, (Dm, Dm), dtype=jnp.float32) * Dm ** (-0.5)
        q_gain = jnp.full((NUM_HEADS,), QK_GAIN_INIT, dtype=jnp.float32)
        return {'x': x, 'w_qkv': w_qkv, 'w_out': w_out, 'q_gain': q_gain}
    _L0_attn_in = _L0_attn_setup()

    def _L0_ffn_setup():
        import jax, jax.numpy as jnp
        import numpy as np
        B, S, D = (4, 128, 512)
        E, K, H = (8, 2, 352)
        HS = 2 * 352
        ALPHA = 0.001
        W_SCALE = 0.02

        def _moe_forward(hidden_states, gate_w, w_gate, w_up, w_down, sw_gate, sw_up, sw_down):
            b, s, d = hidden_states.shape
            x = hidden_states.reshape(-1, d)
            T = x.shape[0]
            logits = x @ gate_w
            scores = jax.nn.softmax(logits, axis=-1)
            topk_w, topk_idx = jax.lax.top_k(scores, K)
            mask = jax.nn.one_hot(topk_idx, E, dtype=scores.dtype).sum(axis=1)
            ce = mask.mean(axis=0)
            Pi = scores.mean(axis=0)
            aux_loss = (Pi * ce * E).sum() * ALPHA
            comb = jnp.zeros((T, E), dtype=x.dtype)
            comb = comb.at[jnp.arange(T)[:, None], topk_idx].add(topk_w)
            g = jax.nn.silu(jnp.einsum('td,edh->teh', x, w_gate)) * jnp.einsum('td,edh->teh', x, w_up)
            routed = jnp.einsum('teh,ehd,te->td', g, w_down, comb)
            shared = jax.nn.silu(x @ sw_gate) * (x @ sw_up) @ sw_down
            out = (routed + shared).reshape(b, s, d)
            return (out, aux_loss)
        key = jax.random.key(seed)
        ks = jax.random.split(key, 8)
        rn = lambda k, sh: jax.random.normal(k, sh, dtype=jnp.float32)
        return {'hidden_states': rn(ks[0], (B, S, D)), 'gate_w': rn(ks[1], (D, E)) * W_SCALE, 'w_gate': rn(ks[2], (E, D, H)) * W_SCALE, 'w_up': rn(ks[3], (E, D, H)) * W_SCALE, 'w_down': rn(ks[4], (E, H, D)) * W_SCALE, 'sw_gate': rn(ks[5], (D, HS)) * W_SCALE, 'sw_up': rn(ks[6], (D, HS)) * W_SCALE, 'sw_down': rn(ks[7], (HS, D)) * W_SCALE}
    _L0_ffn_in = _L0_ffn_setup()
    _d = {'L0_attn_x': _L0_attn_in['x'], 'L0_attn_w_qkv': _L0_attn_in['w_qkv'], 'L0_attn_w_out': _L0_attn_in['w_out'], 'L0_attn_q_gain': _L0_attn_in['q_gain'], 'L0_ffn_gate_w': _L0_ffn_in['gate_w'], 'L0_ffn_w_gate': _L0_ffn_in['w_gate'], 'L0_ffn_w_up': _L0_ffn_in['w_up'], 'L0_ffn_w_down': _L0_ffn_in['w_down'], 'L0_ffn_sw_gate': _L0_ffn_in['sw_gate'], 'L0_ffn_sw_up': _L0_ffn_in['sw_up'], 'L0_ffn_sw_down': _L0_ffn_in['sw_down']}
    _x0 = _d['L0_attn_x']
    _d['L0_attn_x'] = jax.random.normal(jax.random.fold_in(jax.random.key(seed), 1), (1, 2048, 512), dtype=_x0.dtype)
    del _x0
    return _d

def reference(L0_attn_x, L0_attn_w_qkv, L0_attn_w_out, L0_attn_q_gain, L0_ffn_gate_w, L0_ffn_w_gate, L0_ffn_w_up, L0_ffn_w_down, L0_ffn_sw_gate, L0_ffn_sw_up, L0_ffn_sw_down):

    def _L0_attn_ref(x, w_qkv, w_out, q_gain):
        import jax, jax.numpy as jnp
        import numpy as np
        NUM_HEADS = 16
        ROPE_BASE = 10000.0
        QK_GAIN_INIT = 12.0
        EPS = 1e-06
        ROPE_MASK = jnp.asarray(np.tile([1.0, 0.0], NUM_HEADS // 2), dtype=jnp.float32)

        def _rope_cos_sin(seqlen, head_dim, dtype):
            half = head_dim // 2
            inv_freq = ROPE_BASE ** (-jnp.arange(0, half, dtype=jnp.float32) / half)
            theta = jnp.arange(seqlen, dtype=jnp.float32)[:, None] * inv_freq[None, :]
            return (jnp.cos(theta).astype(dtype), jnp.sin(theta).astype(dtype))

        def _apply_rope(t, cos, sin):
            d2 = t.shape[-1] // 2
            t1, t2 = (t[..., :d2], t[..., d2:])
            c = cos[None, :, None, :]
            s = sin[None, :, None, :]
            return jnp.concatenate([t1 * c - t2 * s, t1 * s + t2 * c], axis=-1)

        def _unit_norm(t):
            return t * jax.lax.rsqrt(jnp.sum(t * t, axis=-1, keepdims=True) + EPS)
        B, S, Dm = x.shape
        H = NUM_HEADS
        D = Dm // H
        qkv = (x @ w_qkv).reshape(B, S, 3, H, D)
        q, k, v = (qkv[:, :, 0], qkv[:, :, 1], qkv[:, :, 2])
        q = _unit_norm(q)
        k = _unit_norm(k)
        cos, sin = _rope_cos_sin(S, D, x.dtype)
        m = ROPE_MASK[None, None, :, None]
        q = m * _apply_rope(q, cos, sin) + (1.0 - m) * q
        k = m * _apply_rope(k, cos, sin) + (1.0 - m) * k
        logits = jnp.einsum('bshd,bthd->bhst', q, k) * q_gain[None, :, None, None]
        causal = jnp.tril(jnp.ones((S, S), dtype=bool))
        logits = jnp.where(causal[None, None], logits, jnp.finfo(logits.dtype).min)
        attn = jax.nn.softmax(logits, axis=-1)
        y = jnp.einsum('bhst,bthd->bshd', attn, v).reshape(B, S, Dm)
        return y @ w_out

    def _L0_ffn_ref(hidden_states, gate_w, w_gate, w_up, w_down, sw_gate, sw_up, sw_down):
        import jax, jax.numpy as jnp
        import numpy as np
        B, S, D = (4, 128, 512)
        E, K, H = (8, 2, 352)
        HS = 2 * 352
        ALPHA = 0.001
        W_SCALE = 0.02

        def _moe_forward(hidden_states, gate_w, w_gate, w_up, w_down, sw_gate, sw_up, sw_down):
            b, s, d = hidden_states.shape
            x = hidden_states.reshape(-1, d)
            T = x.shape[0]
            logits = x @ gate_w
            scores = jax.nn.softmax(logits, axis=-1)
            topk_w, topk_idx = jax.lax.top_k(scores, K)
            mask = jax.nn.one_hot(topk_idx, E, dtype=scores.dtype).sum(axis=1)
            ce = mask.mean(axis=0)
            Pi = scores.mean(axis=0)
            aux_loss = (Pi * ce * E).sum() * ALPHA
            comb = jnp.zeros((T, E), dtype=x.dtype)
            comb = comb.at[jnp.arange(T)[:, None], topk_idx].add(topk_w)
            g = jax.nn.silu(jnp.einsum('td,edh->teh', x, w_gate)) * jnp.einsum('td,edh->teh', x, w_up)
            routed = jnp.einsum('teh,ehd,te->td', g, w_down, comb)
            shared = jax.nn.silu(x @ sw_gate) * (x @ sw_up) @ sw_down
            out = (routed + shared).reshape(b, s, d)
            return (out, aux_loss)
        out, _aux = _moe_forward(hidden_states, gate_w, w_gate, w_up, w_down, sw_gate, sw_up, sw_down)
        return out
    x = L0_attn_x
    x = _layernorm(x + _L0_attn_ref(x, L0_attn_w_qkv, L0_attn_w_out, L0_attn_q_gain), axis=-1)
    x = _layernorm(x + _L0_ffn_ref(x, L0_ffn_gate_w, L0_ffn_w_gate, L0_ffn_w_up, L0_ffn_w_down, L0_ffn_sw_gate, L0_ffn_sw_up, L0_ffn_sw_down), axis=-1)
    return x

_drawn_inputs = setup_inputs


def setup_inputs(seed=0):
    import zlib

    import numpy as np

    out = dict(_drawn_inputs(seed))
    spreads = {'L0_attn_q_gain': (12.0, 0.2)}
    factors = {'L0_ffn_gate_w': 5.569,
     'L0_ffn_w_gate': 4.955,
     'L0_ffn_w_up': 4.85,
     'L0_ffn_w_down': 4.837,
     'L0_ffn_sw_gate': 3.861,
     'L0_ffn_sw_up': 3.774,
     'L0_ffn_sw_down': 3.781}
    for name, (base, spread) in spreads.items():
        noise = np.random.default_rng([zlib.crc32(name.encode()), seed]).standard_normal(out[name].shape)
        drawn = base * np.exp(spread * noise) if base else spread * noise
        out[name] = jnp.asarray(drawn.astype(out[name].dtype))
    for name, factor in factors.items():
        out[name] = (out[name] * factor).astype(out[name].dtype)
    return out
```

```python
from contextlib import ExitStack

import numpy as np

import concourse.bass as bass
import concourse.mybir as mybir

F32 = mybir.dt.float32
F32R = mybir.dt.float32r
BF16 = mybir.dt.bfloat16
I32 = mybir.dt.int32
U32 = mybir.dt.uint32
ALU = mybir.AluOpType
ACT = mybir.ActivationFunctionType
AX = mybir.AxisListType.X

P = 128
T, D = 2048, 512
NT, KC = T // P, D // P
HEADS, HD = 16, 32
HG = 4
NG = HEADS // HG
CH = 512
NC, TPC = T // CH, CH // P
E, TOPK, FH, FS = 8, 2, 352, 704
UNIT_EPS, LN_EPS = 1e-6, 1e-5
MASKED = -1.0e30
RSQRT_GUESS = float(0x5F3759DF)
EXP_SAFE = 80.0

STEP_AT = [0, 4, 12, 24, 40]
SLOTS = STEP_AT[-1]
PROJECT_AT = {(2, 0): 2, (2, 1): 3, (2, 2): 4, (2, 3): 5,
              (3, 0): 10, (3, 1): 11, (3, 2): 12, (3, 3): 13,
              (0, 0): 25, (0, 1): 26, (0, 2): 27, (0, 3): 28,
              (1, 0): 33, (1, 1): 34, (1, 2): 35, (1, 3): 36}
NORMALISE_AT = {(2, 0): 6, (2, 1): 7, (2, 2): 8,
                (3, 0): 14, (3, 1): 15, (3, 2): 18,
                (0, 0): 29, (0, 1): 30, (0, 2): 32,
                (1, 0): 37, (1, 1): 38, (1, 2): 0}
TURN_AT = {(1, 0): 1, (1, 1): 2, (1, 2): 3, (1, 3): 3,
           (2, 0): 9, (2, 1): 10, (2, 2): 11, (2, 3): 11,
           (3, 0): 19, (3, 1): 20, (3, 2): 21, (3, 3): 22,
           (0, 0): 33, (0, 1): 34, (0, 2): 35, (0, 3): 36}
SPLIT_W_AT = 22
DIRECT = set(range(STEP_AT[2])) | {14, 15, 18, 29, 30, 32, 37, 38}


def work_at(table, slot, g):
    for (c, part), at in table.items():
        ahead = c < 2 and slot >= STEP_AT[3]
        if at == slot and g + ahead < NG:
            yield g + ahead, c, part


def step_of(slot):
    i = max(n for n in range(NC) if STEP_AT[n] <= slot)
    return i, slot - STEP_AT[i]


def build(nc, x, w_qkv, w_out, q_gain, gate_w, w_gate, w_up, w_down, sw_gate, sw_up, sw_down,
          rope_cos, rope_sin, out):
    with ExitStack() as ctx:
        def sem(name):
            return ctx.enter_context(nc.semaphore(name))

        BASE = -(-nc.sbuf_base // 32) * 32
        TOP = 229344

        def at(name, offset, shape, dt):
            size = int(np.prod(shape[1:])) * (2 if dt == BF16 else 4)
            assert BASE + offset + size <= TOP, (name, offset, size)
            return nc.alloc_sbuf_tensor_at(name, shape, dt, offset=BASE + offset)

        xT_h = at("xT_h", 0, [P, KC, T], F32R)
        xT_l = at("xT_l", 32768, [P, KC, T], F32R)
        k_stack = at("k_stack", 65536, [P, HG, T], F32R)
        q_stack = at("q_stack", 98304, [P, 2, HG, CH], F32R)
        v_sb = at("v_sb", 114688, [P, NT, P], F32)
        wqkv_h = at("wqkv_h", 122880, [P, KC, 3 * P], F32R)
        wqkv_l = at("wqkv_l", 129024, [P, KC, 3 * P], F32R)
        probs = at("probs", 135168, [P, 4, HG, CH], F32)
        x_in = at("x_in", 135168, [P, 4, D], F32)
        key_sum = at("key_sum", 167936, [P, HG, CH], F32)
        qk = at("qk", 176128, [P, 2, TPC, HG, HD], F32)
        squares = at("squares", 180224, [P, 2, TPC, HG, HD], F32)
        rope_prod = at("rope_prod", 180224, [P, 4, 2 * TPC, HG // 2, HD // 2], F32)
        wqkv_raw = at("wqkv_raw", 176128, [P, KC, 3 * P], F32)
        split = at("split", 184320, [P, 2, TPC, HG, 3, HD], F32R)
        y_norm = at("y_norm", 196608, [P, 2, CH], F32)
        inv_sum = at("inv_sum", 200704, [P, CH], F32)
        cos = at("cos", 202752, [P, NC, 2, TPC, HD // 2], F32)
        sin = at("sin", 204800, [P, NC, 2, TPC, HD // 2], F32)
        ident = at("ident", 208896, [P, P], F32)
        ident_r = at("ident_r", 206848, [P, P], F32R)
        ident_b = at("ident_b", 209408, [P, P], BF16)
        mask_b = at("mask_b", 209664, [P, P], BF16)
        ones = at("ones", 209920, [P, HD], F32)
        gain = at("gain", 210048, [P, HEADS], F32)
        gain_abs = at("gain_abs", 210112, [P, HEADS], F32)
        shift = at("shift", 210176, [P, HEADS // 2], F32)
        sq_sum = at("sq_sum", 210208, [P, 2, TPC, HG], F32)
        inv_norm = at("inv_norm", 210464, [P, 2, TPC, HG], F32)
        newton = at("newton", 210592, [P, 2, TPC, HG], F32)
        inv_col = at("inv_col", 210720, [P, CH // 32], F32)

        scores = ctx.enter_context(nc.psum_tensor("scores", [P, 2, 2, CH], F32))
        bank = [ctx.enter_context(nc.psum_tensor(f"bank{n}", [P, CH], F32)) for n in range(4)]
        y_ps, sums_ps, qkv_ps, turn_ps = bank

        y_dram = nc.dram_tensor("y_scratch", [NG, P, T], F32, kind="Internal").ap()

        consts_ready, ident_ready, mask_filled = sem("consts_ready"), sem("ident_ready"), sem("mask_filled")
        tables_loaded = sem("tables_loaded")
        shift_steps = sem("shift_steps")
        x_loaded = [sem(f"x_loaded{n}") for n in range(4)]
        x_turned, xT_high, xT_low = sem("x_turned"), sem("xT_high"), sem("xT_low")
        w_loaded, w_high, w_low = sem("w_loaded"), sem("w_high"), sem("w_low")
        qkv_done, qkv_copied = sem("qkv_done"), sem("qkv_copied")
        norm_steps, inv_normed, sums_inverted = sem("norm_steps"), sem("inv_normed"), sem("sums_inverted")
        normed, rope_products, roped = sem("normed"), sem("rope_products"), sem("roped")
        split_high, split_low = sem("split_high"), sem("split_low")
        turned, q_ready, k_ready = sem("turned"), sem("q_ready"), sem("k_ready")
        scores_ready, exp_done, pv_done = sem("scores_ready"), sem("exp_done"), sem("pv_done")
        sum_dve, sum_pool = sem("sum_dve"), sem("sum_pool")
        sums_done, sums_read = sem("sums_done"), sem("sums_read")
        y_copied, y_ready = sem("y_copied"), sem("y_ready")
        y_stored = [sem(f"y_stored{n}") for n in range(2)]


        x1T_h = at("x1T_h", 0, [P, KC, T], F32R)
        x1T_l = at("x1T_l", 32768, [P, KC, T], F32R)
        x1 = at("x1", 65536, [P, NT, D], F32)
        wo_h = at("wo_h", 98304, [P, NG, D], F32R)
        wo_l = at("wo_l", 106496, [P, NG, D], F32R)
        wo_raw = at("wo_raw", 122880, [P, NG, D], F32)
        gw_raw = at("gw_raw", 131072, [P, KC, E], F32)
        gw_h = at("gw_h", 131200, [P, KC, E], F32R)
        gw_l = at("gw_l", 131328, [P, KC, E], F32R)
        y_raw = at("y_raw", 135168, [P, 4, NG, P], F32)
        y_h = at("y_h", 143360, [P, 2, NG, P], F32R)
        y_l = at("y_l", 147456, [P, 2, NG, P], F32R)
        x_res = at("x_res", 151552, [P, 4, D], F32)
        rows = at("rows", 159744, [P, 4, D], F32)
        stats = at("stats", 207360, [P, TPC, 6], F32)
        moments = at("moments", 207456, [P, TPC, 2], F32)
        var_eps = at("var_eps", 207488, [P, TPC], F32)
        rstd = at("rstd", 207520, [P, TPC], F32)
        ln_work = at("ln_work", 207552, [P, TPC], F32)
        comb = at("comb", 207872, [P, NT, E], F32)
        experts_iota = at("experts_iota", 208384, [P, E], F32)
        logits = at("logits", 185344, [P, NT, E], F32)
        shares = at("shares", 185856, [P, NT, E], F32)
        top_values = at("top_values", 186368, [P, NT, E], F32)
        top_index = at("top_index", 186880, [P, NT, E], U32)
        top_float = at("top_float", 187392, [P, NT, TOPK], F32)
        row_max = at("row_max", 187520, [P, NT], F32)
        row_sum = at("row_sum", 187584, [P, NT], F32)
        chosen = at("chosen", 187648, [P, NT, E], F32)
        chosen2 = at("chosen2", 188160, [P, NT, E], F32)
        HC = [(0, P), (P, P), (2 * P, FH - 2 * P)]
        wg, wu, wd = [], [], []
        for n in range(2):
            o = 98304 + 34816 * n
            wg.append([at(f"wg_h{n}", o, [P, KC, FH], F32R), at(f"wg_l{n}", o + 5632, [P, KC, FH], F32R)])
            wu.append([at(f"wu_h{n}", o + 11264, [P, KC, FH], F32R), at(f"wu_l{n}", o + 16896, [P, KC, FH], F32R)])
            wd.append([at(f"wd_h{n}", o + 22528, [P, 3, D], F32R), at(f"wd_l{n}", o + 28672, [P, 3, D], F32R)])
        raw_gate = at("raw_gate", 167936, [P, KC, FH], F32)
        raw_up = at("raw_up", 173568, [P, KC, FH], F32)
        raw_down = at("raw_down", 179200, [P, 3, D], F32)
        silu = at("silu", 185344, [P, 2, CH], F32)
        hidden = at("hidden", 189440, [P, 2, CH], F32)
        hid_h = at("hid_h", 193536, [P, 3, CH], F32R)
        hid_l = at("hid_l", 199680, [P, 3, CH], F32R)

        wo_loaded, wo_high, wo_low = sem("wo_loaded"), sem("wo_high"), sem("wo_low")
        y_loaded = [sem(f"y_loaded{n}") for n in range(4)]
        y_high, y_low = sem("y_high"), sem("y_low")
        projected, res_added, ln_steps, x1_ready = sem("projected"), sem("res_added"), sem("ln_steps"), sem("x1_ready")
        x1_turned, x1T_high, x1T_low = sem("x1_turned"), sem("x1T_high"), sem("x1T_low")
        logits_done, router_steps, router_exp, iota_ready = sem("logits_done"), sem("router_steps"), sem("router_exp"), sem("iota_ready")
        ffn_loaded, ffn_high, ffn_low = sem("ffn_loaded"), sem("ffn_high"), sem("ffn_low")
        gated_ps, silu_done, hidden_done = sem("gated_ps"), sem("silu_done"), sem("hidden_done")
        hid_high, hid_low, down_done, down_added = sem("hid_high"), sem("hid_low"), sem("down_done"), sem("down_added")
        out_ready, out_stored = sem("out_ready"), sem("out_stored")
        EXPERTS = E + 2
        out_rows = out.rearrange("b s d -> (b s) d")
        z_ps = [scores[:, 0, 0], scores[:, 0, 1]]
        x1T_ps = [scores[:, 1, 0], scores[:, 1, 1]]
        logits_ps = turn_ps

        def weights_of(e):
            if e < E:
                return w_gate[e], w_up[e], w_down[e]
            half = slice((e - E) * FH, (e - E + 1) * FH)
            return sw_gate[:, half], sw_up[:, half], sw_down[half, :]

        def tail_sync(sp):
            sp.wait_ge(qkv_done, 16 * NG)
            sp.dma_start(wo_raw[:], w_out.rearrange("(g p) n -> p g n", p=P)).then_inc(wo_loaded, 16)
            sp.dma_start(gw_raw[:], gate_w.rearrange("(k p) n -> p k n", p=P)).then_inc(wo_loaded, 16)
            sp.wait_ge(pv_done, SLOTS * NG)
            sp.wait_ge(sum_dve, added(NG - 1, SLOTS - 1))
            sp.wait_ge(sum_pool, added(NG - 1, SLOTS - 1))
            sp.wait_ge(exp_done, 2 * SLOTS * NG)
            for n in range(2):
                sp.wait_ge(y_stored[n], 16 * NC * NG // 2)
            for t in range(NT):
                if t >= 4:
                    sp.wait_ge(y_low, t - 3)
                    sp.wait_ge(y_high, t - 3)
                    sp.wait_ge(res_added, t - 3)
                sp.dma_start(y_raw[:, t % 4], y_dram[:, :, t * P:(t + 1) * P].rearrange("g p t -> p g t")).then_inc(y_loaded[t % 4], 16)
                sp.dma_start(x_res[:, t % 4], x_rows[t * P:(t + 1) * P, :]).then_inc(y_loaded[t % 4], 16)
            for e in range(EXPERTS):
                if e == 0:
                    sp.wait_ge(sums_done, 2 * NG)
                    sp.wait_ge(y_ready, NC * NG)
                    sp.wait_ge(split_low, 2 * NC * NG)
                else:
                    sp.wait_ge(ffn_high, e)
                    sp.wait_ge(ffn_low, e)
                gate, up, down = weights_of(e)
                sp.dma_start(raw_gate[:], gate.rearrange("(k p) n -> p k n", p=P)).then_inc(ffn_loaded, 16)
                sp.dma_start(raw_up[:], up.rearrange("(k p) n -> p k n", p=P)).then_inc(ffn_loaded, 16)
                sp.dma_start(raw_down[:, 0:2], down[0:2 * P].rearrange("(k p) n -> p k n", p=P)).then_inc(ffn_loaded, 16)
                sp.dma_start(raw_down[0:FH - 2 * P, 2], down[2 * P:FH]).then_inc(ffn_loaded, 16)
            for t in range(NT):
                sp.wait_ge(out_ready, t + 1)
                sp.dma_start(out_rows[t * P:(t + 1) * P, :], x1[:, t]).then_inc(out_stored, 16)
            sp.wait_ge(out_stored, 16 * NT)

        def tail_tensor(pe):
            pe.wait_ge(wo_high, 2)
            pe.wait_ge(wo_low, 2)
            for t in range(NT + 6):
                if t < NT:
                    pe.wait_ge(y_high, t + 1)
                    pe.wait_ge(y_low, t + 1)
                    if t >= 2:
                        pe.wait_ge(res_added, t - 1)
                    for m, (ys, ws) in enumerate(((y_h, wo_h), (y_h, wo_l), (y_l, wo_h))):
                        for g in range(NG):
                            mm = nc.tensor.matmul(z_ps[t % 2], ys[:, t % 2, g, :], ws[:, g, :],
                                                  start=(m == 0 and g == 0), stop=(m == 2 and g == NG - 1))
                    mm.then_inc(projected, 1)
                s = t - 4
                if 0 <= s < NT:
                    pe.wait_ge(x1_ready, s + 1)
                    if s >= 2:
                        pe.wait_ge(x1T_low, s - 1)
                    for k in range(KC):
                        mm = nc.tensor.transpose(x1T_ps[s % 2][:, k * P:(k + 1) * P], x1[:, s, k * P:(k + 1) * P], ident[:])
                    mm.then_inc(x1_turned, 1)
                s = t - 5
                if 0 <= s < NT:
                    pe.wait_ge(x1T_high, s + 1)
                    pe.wait_ge(x1T_low, s + 1)
                    for m, (xs, ws) in enumerate(((x1T_h, gw_h), (x1T_h, gw_l), (x1T_l, gw_h))):
                        for k in range(KC):
                            mm = nc.tensor.matmul(logits_ps[:, s * E:(s + 1) * E], xs[:, k, s * P:(s + 1) * P], ws[:, k, :],
                                                  start=(m == 0 and k == 0), stop=(m == 2 and k == KC - 1))
                    mm.then_inc(logits_done, 1)
            for e in range(EXPERTS):
                pe.wait_ge(ffn_high, e + 1)
                pe.wait_ge(ffn_low, e + 1)
                for c in range(NC + 1):
                    for hc, (h0, hn) in enumerate(HC):
                        if c < NC:
                            n = (e * NC + c) * 3 + hc
                            if n >= 2:
                                pe.wait_ge(hidden_done, n - 1)
                            for which, w in enumerate((wg, wu)):
                                for m, (xs, ws) in enumerate(((x1T_h, 0), (x1T_l, 0), (x1T_h, 1))):
                                    for k in range(KC):
                                        mm = nc.tensor.matmul(scores[0:hn, which, n % 2, :], w[e % 2][ws][:, k, h0:h0 + hn],
                                                              xs[:, k, c * CH:(c + 1) * CH],
                                                              start=(m == 0 and k == 0), stop=(m == 2 and k == KC - 1))
                                mm.then_inc(gated_ps, 1)
                        if hc == 0 and c:
                            b = e * NC + c - 1
                            pe.wait_ge(hid_high, 3 * (b + 1))
                            pe.wait_ge(hid_low, 3 * (b + 1))
                            for tt in range(TPC):
                                n = 4 * b + tt
                                if n >= 2:
                                    pe.wait_ge(down_added, n - 1)
                                for m, (hs, ws) in enumerate(((hid_h, 0), (hid_l, 0), (hid_h, 1))):
                                    for k, (k0, kn) in enumerate(HC):
                                        mm = nc.tensor.matmul(bank[n % 2][:], hs[0:kn, k, tt * P:(tt + 1) * P], wd[e % 2][ws][0:kn, k, :],
                                                              start=(m == 0 and k == 0), stop=(m == 2 and k == 2))
                                mm.then_inc(down_done, 1)

        def tail_scalar(act):
            for t in range(NT + 4):
                if t < NT:
                    act.wait_ge(y_loaded[t % 4], 32 * (t // 4 + 1))
                    if t >= 2:
                        act.wait_ge(projected, t - 1)
                    nc.scalar.copy(y_h[:, t % 2], y_raw[:, t % 4]).then_inc(y_high, 1)
                s = t - 4
                if s >= 0:
                    act.wait_ge(x1_turned, s + 1)
                    nc.scalar.copy(x1T_h[:, :, s * P:(s + 1) * P],
                                   x1T_ps[s % 2].rearrange("p (k n) -> p k n", k=KC)).then_inc(x1T_high, 1)
            act.wait_ge(router_steps, 3)
            nc.scalar.activation(shares[:], shares[:], ACT.Exp).then_inc(router_exp, 1)
            for e in range(EXPERTS):
                act.wait_ge(ffn_loaded, 64 * (e + 1))
                if e >= 2:
                    act.wait_ge(down_done, 4 * NC * (e - 1))
                nc.scalar.copy(wg[e % 2][0][:], raw_gate[:])
                nc.scalar.copy(wu[e % 2][0][:], raw_up[:])
                nc.scalar.copy(wd[e % 2][0][:, 0:2], raw_down[:, 0:2])
                nc.scalar.copy(wd[e % 2][0][0:FH - 2 * P, 2], raw_down[0:FH - 2 * P, 2]).then_inc(ffn_high, 1)
                for c in range(NC):
                    for hc, (h0, hn) in enumerate(HC):
                        n = (e * NC + c) * 3 + hc
                        if n == 0:
                            act.wait_ge(router_steps, R_STEPS)
                        act.wait_ge(gated_ps, 2 * n + 1)
                        if n >= 2:
                            act.wait_ge(hidden_done, n - 1)
                        nc.scalar.activation(silu[0:hn, n % 2], scores[0:hn, 0, n % 2, :], ACT.Silu).then_inc(silu_done, 1)
                        act.wait_ge(hidden_done, n + 1)
                        if e * NC + c:
                            act.wait_ge(down_done, 4 * (e * NC + c))
                        nc.scalar.copy(hid_h[0:hn, hc], hidden[0:hn, n % 2]).then_inc(hid_high, 1)

        def layernorm(tiles, src, steps, dst, done):
            n = steps
            for i in range(TPC):
                nc.vector.bn_aggr(moments[:, i], stats[:, i]).then_inc(ln_steps, 1)
            nc.vector.wait_ge(ln_steps, n + 4)
            nc.vector.tensor_scalar(var_eps[:], moments[:, :, 1], LN_EPS, None, ALU.add).then_inc(ln_steps, 1)
            nc.vector.wait_ge(ln_steps, n + 5)
            dve_rsqrt(rstd[:], ln_work[:], var_eps[:], ln_steps, n + 5)
            for i in range(TPC):
                nc.vector.tensor_scalar(dst[i], src[i], moments[:, i, 0:1], rstd[:, i:i + 1],
                                        ALU.subtract, ALU.mult).then_inc(done, 1)

        LN_STEPS = 4 + 1 + 11 + 4
        R_STEPS = 13

        def tail_vector(dve):
            dve.wait_ge(wo_loaded, 32)
            dve.wait_ge(scores_ready, 2 * SLOTS * NG)
            nc.vector.tensor_copy(wo_h[:], wo_raw[:]).then_inc(wo_high, 1)
            nc.vector.tensor_copy(gw_h[:], gw_raw[:]).then_inc(wo_high, 1)
            dve.wait_ge(wo_high, 2)
            nc.vector.tensor_tensor(wo_l[:], wo_raw[:], wo_h[:].bitcast(F32), ALU.subtract).then_inc(wo_low, 1)
            nc.vector.tensor_tensor(gw_l[:], gw_raw[:], gw_h[:].bitcast(F32), ALU.subtract).then_inc(wo_low, 1)

            def lower_y(t):
                dve.wait_ge(y_high, t + 1)
                if t >= 2:
                    dve.wait_ge(projected, t - 1)
                nc.vector.tensor_tensor(y_l[:, t % 2], y_raw[:, t % 4], y_h[:, t % 2].bitcast(F32), ALU.subtract).then_inc(y_low, 1)

            lower_y(0)
            for t in range(NT + 4):
                if t + 1 < NT:
                    lower_y(t + 1)
                if t < NT:
                    dve.wait_ge(projected, t + 1)
                    if t >= 4:
                        dve.wait_ge(x1_ready, t - 3)
                    nc.vector.tensor_tensor(rows[:, t % 4], z_ps[t % 2], x_res[:, t % 4], ALU.add).then_inc(res_added, 1)
                    dve.wait_ge(res_added, t + 1)
                    nc.vector.bn_stats(stats[:, t % TPC], rows[:, t % 4]).then_inc(ln_steps, 1)
                s = t - 4
                if s >= 0:
                    dve.wait_ge(x1T_high, s + 1)
                    nc.vector.tensor_tensor(x1T_l[:, :, s * P:(s + 1) * P],
                                            x1T_ps[s % 2].rearrange("p (k n) -> p k n", k=KC),
                                            x1T_h[:, :, s * P:(s + 1) * P].bitcast(F32), ALU.subtract).then_inc(x1T_low, 1)
                if t < NT and t % TPC == TPC - 1:
                    c = t // TPC
                    dve.wait_ge(ln_steps, LN_STEPS * c + 4)
                    layernorm(range(TPC), [rows[:, i] for i in range(TPC)], LN_STEPS * c + 4,
                              [x1[:, t - 3 + i] for i in range(TPC)], x1_ready)
            step = [0]

            def done(inst):
                inst.then_inc(router_steps, 1)
                step[0] += 1
                nc.vector.wait_ge(router_steps, step[0])

            dve.wait_ge(logits_done, NT)
            done(nc.vector.tensor_copy(logits[:], logits_ps[:, 0:NT * E].rearrange("p (t e) -> p t e", e=E)))
            done(nc.vector.tensor_reduce(row_max[:], logits[:], AX, ALU.max))
            done(nc.vector.tensor_tensor(shares[:], logits[:], row_max[:].unsqueeze(2).broadcast_to([P, NT, E]), ALU.subtract))
            for t in range(NT):
                top = nc.vector.max(top_values[:, t], logits[:, t])
            done(top)
            for t in range(NT):
                top = nc.vector.max_index(top_index[:, t], top_values[:, t], logits[:, t])
            done(top)
            done(nc.vector.tensor_copy(top_float[:], top_index[:, :, 0:TOPK]))
            dve.wait_ge(iota_ready, E)
            for k, to in enumerate((chosen, chosen2)):
                done(nc.vector.tensor_tensor(to[:], experts_iota[:].unsqueeze(1).broadcast_to([P, NT, E]),
                                             top_float[:, :, k:k + 1].broadcast_to([P, NT, E]), ALU.is_equal))
            done(nc.vector.tensor_tensor(chosen[:], chosen[:], chosen2[:], ALU.add))
            dve.wait_ge(router_exp, 1)
            done(nc.vector.tensor_reduce(row_sum[:], shares[:], AX, ALU.add))
            done(nc.vector.reciprocal(row_sum[:], row_sum[:]))
            done(nc.vector.tensor_tensor(chosen[:], chosen[:], shares[:], ALU.mult))
            done(nc.vector.tensor_tensor(comb[:], chosen[:], row_sum[:].unsqueeze(2).broadcast_to([P, NT, E]), ALU.mult))
            assert step[0] == R_STEPS
            def split_low_w(e):
                dve.wait_ge(ffn_high, e + 1)
                nc.vector.tensor_tensor(wg[e % 2][1][:], raw_gate[:], wg[e % 2][0][:].bitcast(F32), ALU.subtract)
                nc.vector.tensor_tensor(wu[e % 2][1][:], raw_up[:], wu[e % 2][0][:].bitcast(F32), ALU.subtract)
                nc.vector.tensor_tensor(wd[e % 2][1][:, 0:2], raw_down[:, 0:2], wd[e % 2][0][:, 0:2].bitcast(F32), ALU.subtract)
                nc.vector.tensor_tensor(wd[e % 2][1][0:FH - 2 * P, 2], raw_down[0:FH - 2 * P, 2],
                                        wd[e % 2][0][0:FH - 2 * P, 2].bitcast(F32), ALU.subtract).then_inc(ffn_low, 1)

            def add_down(b):
                e = b // NC
                for tt in range(TPC):
                    n = 4 * b + tt
                    t = n % NT
                    dve.wait_ge(down_done, n + 1)
                    if n >= NT:
                        dve.wait_ge(down_added, n - NT + 1)
                    scale = comb[:, t, e:e + 1] if e < E else 1.0
                    nc.vector.scalar_tensor_tensor(x1[:, t], bank[n % 2][:], scale, x1[:, t], ALU.mult, ALU.add).then_inc(down_added, 1)

            for e in range(EXPERTS):
                split_low_w(e)
                for c in range(NC):
                    b = e * NC + c
                    for hc, (h0, hn) in enumerate(HC):
                        n = b * 3 + hc
                        dve.wait_ge(gated_ps, 2 * n + 2)
                        dve.wait_ge(silu_done, n + 1)
                        if n >= 2:
                            dve.wait_ge(hid_low, n - 1)
                            dve.wait_ge(hid_high, n - 1)
                        nc.vector.tensor_tensor(hidden[0:hn, n % 2], silu[0:hn, n % 2], scores[0:hn, 1, n % 2, :], ALU.mult).then_inc(hidden_done, 1)
                        dve.wait_ge(hidden_done, n + 1)
                        dve.wait_ge(hid_high, n + 1)
                        nc.vector.tensor_tensor(hid_l[0:hn, hc], hidden[0:hn, n % 2], hid_h[0:hn, hc].bitcast(F32), ALU.subtract).then_inc(hid_low, 1)
                        if hc == 0 and b:
                            pass
                    add_down(b)
            for c in range(NC):
                dve.wait_ge(down_added, 4 * NC * (EXPERTS - 1) + 4 * (c + 1))
                if c:
                    dve.wait_ge(out_ready, 4 * c)
                for i in range(TPC):
                    nc.vector.bn_stats(stats[:, i], x1[:, TPC * c + i]).then_inc(ln_steps, 1)
                n = LN_STEPS * (NC + c) + 4
                dve.wait_ge(ln_steps, n)
                layernorm(None, [x1[:, TPC * c + i] for i in range(TPC)], n, [x1[:, TPC * c + i] for i in range(TPC)], out_ready)

        def tail_gpsimd(pool):
            for e in range(E):
                nc.gpsimd.memset(experts_iota[:, e:e + 1], float(e)).then_inc(iota_ready, 1)

        x_rows = x.rearrange("b s d -> (b s) d")
        block = ctx.enter_context(nc.Block())

        def added(g, slot):
            return (SLOTS - len(DIRECT)) * g + sum(n not in DIRECT for n in range(slot + 1))

        def load_w(sp, g):
            for part in range(3):
                col = part * D + g * P
                sp.dma_start(wqkv_raw[:, :, part * P:(part + 1) * P],
                             w_qkv.rearrange("(k p) n -> p k n", p=P)[:, :, col:col + P]).then_inc(w_loaded, 16)

        @block.sync
        def _(sp):
            for t in range(NT):
                if t >= 4:
                    sp.wait_ge(x_turned, t - 3)
                sp.dma_start(x_in[:, t % 4, :], x_rows[t * P:(t + 1) * P, :]).then_inc(x_loaded[t % 4], 16)
                if t == 3:
                    load_w(sp, 0)
                    for which in range(2):
                        for to, of in ((cos, rope_cos), (sin, rope_sin)):
                            for c in range(NC):
                                sp.dma_start(to[:, c, which], of[c * CH:(c + 1) * CH, :].rearrange("(t p) f -> p t f", p=P)).then_inc(tables_loaded, 16)
                    sp.dma_start(gain[:], q_gain.rearrange("(a h) -> a h", a=1).broadcast_to([P, HEADS])).then_inc(tables_loaded, 16)
            for g in range(NG):
                for i in range(NC):
                    if i == 2 and g + 1 < NG:
                        sp.wait_ge(split_high, 4 * g + 4)
                        sp.wait_ge(split_low, 2 * (4 * g + 4))
                        load_w(sp, g + 1)
                    step = NC * g + i
                    sp.wait_ge(y_ready, step + 1)
                    sp.dma_start(y_dram[g, :, i * CH:(i + 1) * CH], y_norm[:, step % 2, :]).then_inc(y_stored[step % 2], 16)
            tail_sync(sp)

        def pe_project(g, c, tt):
            n = 4 * (NC * g + c) + tt
            if tt == 0 and c == 0:
                nc.tensor.wait_ge(w_high, g + 1)
                nc.tensor.wait_ge(w_low, g + 1)
            if n >= 1:
                nc.tensor.wait_ge(qkv_copied, n)
            tok = slice((TPC * c + tt) * P, (TPC * c + tt + 1) * P)
            parts = [(xT_h, wqkv_h), (xT_h, wqkv_l), (xT_l, wqkv_h)]
            for m, (xs, ws) in enumerate(parts):
                for k in range(KC):
                    mm = nc.tensor.matmul(qkv_ps[:, 0:3 * P], xs[:, k, tok], ws[:, k, :],
                                          start=(m == 0 and k == 0), stop=(m == 2 and k == KC - 1))
            mm.then_inc(qkv_done, 1)

        def pe_turn(g, c, h, which):
            C = NC * g + c
            if h == 0 and which:
                nc.tensor.wait_ge(split_high, C + 1)
                nc.tensor.wait_ge(split_low, 2 * (C + 1))
            if not which:
                nc.tensor.wait_ge(k_ready, 4 * C + h + 1)
            elif 4 * C + h > 0:
                nc.tensor.wait_ge(q_ready, 4 * C + h)
            for tt in range(TPC):
                mm = nc.tensor.matmul(turn_ps[0:3 * HD, tt * P:(tt + 1) * P],
                                      split[:, which, tt, h, :, :].rearrange("p s d -> p (s d)"), ident_r[:],
                                      start=True, stop=True)
            mm.then_inc(turned, 1)

        def pe_scores(g, slot):
            i, j = step_of(slot)
            n = SLOTS * g + slot
            if j == 0:
                nc.tensor.wait_ge(q_ready, 4 * (NC * g + i + 1))
                nc.tensor.wait_ge(k_ready, 4 * (NC * g + i + 1))
            lo = max(0, (j - TPC * i) * P)
            for p in range(2):
                if n >= 1:
                    nc.tensor.wait_ge(exp_done, 2 * n + p - 1)
                for hh in range(2):
                    h = 2 * p + hh
                    diagonal = j >= TPC * i
                    mm = nc.tensor.matmul(scores[:, p, hh, lo:CH], k_stack[0:3 * HD, h, j * P:(j + 1) * P],
                                          q_stack[0:3 * HD, i % 2, h, lo:CH], start=True, stop=not diagonal)
                    if diagonal:
                        mm = nc.tensor.matmul(scores[:, p, hh, lo:lo + P], ident_b[:], mask_b[:],
                                              start=False, stop=True)
                mm.then_inc(scores_ready, 1)

        def pe_values(g, slot):
            i, j = step_of(slot)
            n, step = SLOTS * g + slot, NC * g + i
            nc.tensor.wait_ge(exp_done, 2 * n + 2)
            if j == 0 and step >= 1:
                nc.tensor.wait_ge(y_copied, step)
            lo = max(0, (j - TPC * i) * P)
            last = TPC * (i + 1) - 1
            if slot in DIRECT:
                first = min(DIRECT & set(range(STEP_AT[i], STEP_AT[i + 1]))) == slot
                if first and step >= 1:
                    nc.tensor.wait_ge(sums_read, step)
                for h in range(HG):
                    nc.tensor.matmul(sums_ps[HD * h:HD * (h + 1), lo:CH], ones[:], probs[:, n % 4, h, lo:CH],
                                     start=first, stop=(j == last))
            for h in range(HG):
                mm = nc.tensor.matmul(y_ps[HD * h:HD * (h + 1), lo:CH],
                                      v_sb[:, j, HD * h:HD * (h + 1)], probs[:, n % 4, h, lo:CH],
                                      start=(j == 0), stop=(j == last))
            mm.then_inc(pv_done, 1)

        def pe_sums(g, i):
            nc.tensor.wait_ge(sum_dve, added(g, STEP_AT[i + 1] - 1))
            nc.tensor.wait_ge(sum_pool, added(g, STEP_AT[i + 1] - 1))
            for h in range(HG):
                mm = nc.tensor.matmul(sums_ps[HD * h:HD * (h + 1), :], ones[:], key_sum[:, h, :], start=False, stop=True)
            mm.then_inc(sums_done, 1)

        @block.tensor
        def _(pe):
            pe.wait_ge(consts_ready, 1)
            for t in range(NT):
                pe.wait_ge(x_loaded[t % 4], 16 * (t // 4 + 1))
                if t >= 4:
                    pe.wait_ge(xT_low, t - 3)
                for k in range(KC):
                    mm = nc.tensor.transpose(scores[:, (t % 4) // 2, t % 2, k * P:(k + 1) * P],
                                             x_in[:, t % 4, k * P:(k + 1) * P], ident[:])
                mm.then_inc(x_turned, 1)
            pe.wait_ge(xT_low, NT)
            pe.wait_ge(xT_high, NT)
            pe.wait_ge(ident_ready, 1)
            for tt in range(TPC):
                pe_project(0, 0, tt)
            for tt in range(TPC):
                pe_project(0, 1, tt)
            for h in range(HG):
                pe_turn(0, 0, h, 1)
                pe_turn(0, 0, h, 0)
            for g in range(NG):
                for slot in range(SLOTS):
                    pe_scores(g, slot)
                    for work in work_at(PROJECT_AT, slot, g):
                        pe_project(*work)
                    turns = list(work_at(TURN_AT, slot, g))
                    for n, work in enumerate(turns):
                        pe_turn(*work, 1)
                        if n + 1 < len(turns):
                            pe_turn(*work, 0)
                    if slot or g:
                        pe_values(g if slot else g - 1, (slot - 1) % SLOTS)
                        if slot in STEP_AT:
                            i = STEP_AT.index(slot)
                            if (i - 1) % NC >= 2:
                                pe_sums(g if i else g - 1, (i - 1) % NC)
                    for work in turns[-1:]:
                        pe_turn(*work, 0)
            pe_values(NG - 1, SLOTS - 1)
            pe_sums(NG - 1, NC - 1)
            tail_tensor(pe)

        def act_copy_qkv(g, c, tt):
            C = NC * g + c
            n = 4 * C + tt
            nc.scalar.wait_ge(qkv_done, n + 1)
            if tt == 0 and C >= 1:
                nc.scalar.wait_ge(split_high, C)
                nc.scalar.wait_ge(split_low, 2 * C)
            if tt == 0 and c == 0:
                nc.scalar.wait_ge(w_high, g + 1)
                nc.scalar.wait_ge(w_low, g + 1)
            rows = qkv_ps[:, 0:2 * P].rearrange("p (w h d) -> p w h d", w=2, h=HG)
            nc.scalar.copy(qk[:, :, tt], rows)
            if tt == 0 and C >= 1:
                nc.scalar.wait_ge(roped, 2 * C)
            nc.scalar.activation(squares[:, :, tt], rows, ACT.Square)
            if g >= 1:
                nc.scalar.wait_ge(pv_done, SLOTS * (g - 1) + STEP_AT[3] + 4 * c + tt + 1)
            nc.scalar.copy(v_sb[:, TPC * c + tt, :], qkv_ps[:, 2 * P:3 * P]).then_inc(qkv_copied, 1)

        def act_copy_q(g, c, h):
            C = NC * g + c
            nc.scalar.wait_ge(turned, 8 * C + 2 * h + 2)
            if C >= 2 and h == 0:
                nc.scalar.wait_ge(scores_ready, 2 * (SLOTS * ((C - 2) // 4) + STEP_AT[(C - 2) % 4 + 1]))
            nc.scalar.copy(q_stack[0:3 * HD, c % 2, h, :], turn_ps[0:3 * HD, :]).then_inc(q_ready, 1)

        def act_copy_y(g, i):
            step = NC * g + i
            nc.scalar.wait_ge(pv_done, SLOTS * g + STEP_AT[i + 1])
            if step >= 2:
                nc.scalar.wait_ge(y_stored[step % 2], 16 * (step // 2))
            nc.scalar.copy(y_norm[:, step % 2, :], y_ps[:]).then_inc(y_copied, 1)

        def act_exp(g, slot):
            i, j = step_of(slot)
            n = SLOTS * g + slot
            lo = max(0, (j - TPC * i) * P)
            if n == 0:
                nc.scalar.wait_ge(shift_steps, 5)
                nc.scalar.wait_ge(x_turned, NT)
            if n >= 4:
                nc.scalar.wait_ge(pv_done, n - 3)
                before = added((n - 4) // SLOTS, (n - 4) % SLOTS)
                if before:
                    nc.scalar.wait_ge(sum_dve, before)
                    nc.scalar.wait_ge(sum_pool, before)
            for p in range(2):
                nc.scalar.wait_ge(scores_ready, 2 * n + p + 1)
                nc.scalar.activation(probs[:, n % 4, 2 * p:2 * p + 2, lo:CH], scores[:, p, :, lo:CH], ACT.Exp,
                                     bias=shift[:, 2 * g + p:2 * g + p + 1]).then_inc(exp_done, 1)

        @block.scalar
        def _(act):
            for t in range(NT):
                act.wait_ge(x_turned, t + 1)
                nc.scalar.copy(xT_h[:, :, t * P:(t + 1) * P],
                               scores[:, (t % 4) // 2, t % 2, :].rearrange("p (k n) -> p k n", k=KC)).then_inc(xT_high, 1)
            for tt in range(TPC):
                act_copy_qkv(0, 0, tt)
            for tt in range(TPC):
                act_copy_qkv(0, 1, tt)
            for h in range(HG):
                act_copy_q(0, 0, h)
            for g in range(NG):
                for slot in range(SLOTS):
                    act_exp(g, slot)
                    if slot in STEP_AT and (slot or g):
                        i = STEP_AT.index(slot)
                        act_copy_y(g if i else g - 1, (i - 1) % NC)
                    for work in work_at(PROJECT_AT, slot, g):
                        act_copy_qkv(*work)
                    for work in work_at(TURN_AT, slot, g):
                        act_copy_q(*work)
            act_copy_y(NG - 1, NC - 1)
            tail_scalar(act)

        def dve_split_w(g):
            nc.vector.wait_ge(w_loaded, 48 * (g + 1))
            if g:
                nc.vector.wait_ge(qkv_done, 16 * g)
            nc.vector.tensor_copy(wqkv_h[:], wqkv_raw[:]).then_inc(w_high, 1)

        def dve_rsqrt(out, work, arg, ready, steps):
            n = steps
            for do in range(2):
                if do == 0:
                    nc.vector.tensor_scalar(out.bitcast(I32), arg.bitcast(I32), 1, None, ALU.arith_shift_right).then_inc(ready, 1)
                else:
                    nc.vector.tensor_scalar(out.bitcast(I32), out.bitcast(I32), -1.0, RSQRT_GUESS, ALU.mult, ALU.add).then_inc(ready, 1)
                n += 1
                nc.vector.wait_ge(ready, n)
            for _ in range(3):
                nc.vector.scalar_tensor_tensor(work, out, -0.5, out, ALU.mult, ALU.mult).then_inc(ready, 1)
                nc.vector.wait_ge(ready, n + 1)
                nc.vector.tensor_tensor(work, work, arg, ALU.mult).then_inc(ready, 1)
                nc.vector.wait_ge(ready, n + 2)
                nc.vector.scalar_tensor_tensor(out, work, 1.5, out, ALU.add, ALU.mult).then_inc(ready, 1)
                nc.vector.wait_ge(ready, n + 3)
                n += 3

        def dve_norms(g, c):
            C = NC * g + c
            nc.vector.wait_ge(qkv_copied, 4 * (C + 1))
            nc.vector.tensor_reduce(sq_sum[:], squares[:], AX, ALU.add).then_inc(norm_steps, 1)
            nc.vector.wait_ge(norm_steps, 13 * C + 1)
            nc.vector.tensor_scalar(sq_sum[:], sq_sum[:], UNIT_EPS, None, ALU.add).then_inc(norm_steps, 1)
            nc.vector.wait_ge(norm_steps, 13 * C + 2)
            if C:
                nc.vector.wait_ge(normed, C)
            dve_rsqrt(inv_norm[:], newton[:], sq_sum[:], norm_steps, 13 * C + 2)
            nc.vector.tensor_tensor(inv_norm[:, 0], inv_norm[:, 0],
                                    gain[:, HG * g:HG * (g + 1)].unsqueeze(1).broadcast_to([P, TPC, HG]),
                                    ALU.mult).then_inc(inv_normed, 1)
            nc.vector.wait_ge(inv_normed, C + 1)
            rows = qk[:].rearrange("p w t h d -> p (w t h) d")
            nc.vector.tensor_tensor(rows, rows, inv_norm[:].rearrange("p w t h -> p (w t h)").unsqueeze(2)
                                    .broadcast_to([P, 2 * TPC * HG, HD]), ALU.mult).then_inc(normed, 1)

        def dve_split(g, c):
            C = NC * g + c
            nc.vector.wait_ge(roped, 2 * (C + 1))
            if C:
                nc.vector.wait_ge(turned, 8 * C)
            rows = [qk[:, w].rearrange("p t h d -> p (t h) d") for w in range(2)]
            parts = [split[:, w].rearrange("p t h s d -> p (t h) s d") for w in range(2)]
            twice = [r.unsqueeze(2).broadcast_to([P, TPC * HG, 2, HD]) for r in rows]
            nc.vector.tensor_copy(parts[0][:, :, 0:2, :], twice[0])
            nc.vector.tensor_copy(parts[1][:, :, 0::2, :], twice[1]).then_inc(split_high, 1)
            nc.vector.wait_ge(split_high, C + 1)
            for w, low in ((0, 2), (1, 1)):
                nc.vector.tensor_tensor(parts[w][:, :, low, :], rows[w], parts[w][:, :, 0, :].bitcast(F32),
                                        ALU.subtract).then_inc(split_low, 1)

        def dve_copy_k(g, c, h):
            C = NC * g + c
            nc.vector.wait_ge(turned, 8 * C + 2 * h + 1)
            if g and h == 0:
                nc.vector.wait_ge(scores_ready, 2 * (SLOTS * (g - 1) + STEP_AT[3] + TPC * (c + 1)))
            nc.vector.tensor_copy(k_stack[0:3 * HD, h, c * CH:(c + 1) * CH], turn_ps[0:3 * HD, :]).then_inc(k_ready, 1)

        def dve_add_keys(g, slot):
            i, j = step_of(slot)
            n = SLOTS * g + slot
            lo = max(0, (j - TPC * i) * P)
            nc.vector.wait_ge(exp_done, 2 * n + 2)
            if added(g, slot) > 1:
                nc.vector.wait_ge(sum_dve, added(g, slot) - 1)
            if j == 0:
                if 2 * g + i > 2:
                    nc.vector.wait_ge(sums_done, 2 * g + i - 2)
                nc.vector.tensor_copy(key_sum[:, 0:3, :], probs[:, n % 4, 0:3, :]).then_inc(sum_dve, 1)
            else:
                nc.vector.tensor_tensor(key_sum[:, 0:3, lo:CH], key_sum[:, 0:3, lo:CH], probs[:, n % 4, 0:3, lo:CH],
                                        ALU.add).then_inc(sum_dve, 1)

        def dve_outputs(g, i):
            step = NC * g + i
            if i < 2:
                nc.vector.wait_ge(pv_done, SLOTS * g + STEP_AT[i + 1])
            else:
                nc.vector.wait_ge(sums_done, 2 * g + i - 1)
            if step:
                nc.vector.wait_ge(y_ready, step)
            nc.vector.transpose(inv_sum[:], sums_ps[:]).then_inc(sums_read, 1)
            nc.vector.wait_ge(sums_read, step + 1)
            nc.vector.reciprocal(inv_col[:], inv_sum[:].rearrange("p (b n) -> p b n", n=32)[:, :, 0]).then_inc(sums_inverted, 1)
            nc.vector.wait_ge(sums_inverted, 2 * step + 1)
            nc.vector.transpose(inv_sum[:], inv_col[:].unsqueeze(2).broadcast_to([P, CH // 32, 32])).then_inc(sums_inverted, 1)
            nc.vector.wait_ge(sums_inverted, 2 * step + 2)
            nc.vector.wait_ge(y_copied, step + 1)
            nc.vector.tensor_tensor(y_norm[:, step % 2, :], y_norm[:, step % 2, :], inv_sum[:], ALU.mult).then_inc(y_ready, 1)

        @block.vector
        def _(dve):
            dve.wait_ge(consts_ready, 1)
            nc.vector.tensor_copy(ident_r[:], ident[:]).then_inc(ident_ready, 1)
            dve.wait_ge(tables_loaded, 16 * 17)
            nc.vector.tensor_scalar(gain_abs[:], gain[:], -1.0, None, ALU.mult).then_inc(shift_steps, 1)
            dve.wait_ge(shift_steps, 1)
            nc.vector.tensor_tensor(gain_abs[:], gain_abs[:], gain[:], ALU.max).then_inc(shift_steps, 1)
            dve.wait_ge(shift_steps, 2)
            pairs = gain_abs[:].rearrange("p (a b) -> p a b", b=2)
            nc.vector.tensor_tensor(shift[:], pairs[:, :, 0], pairs[:, :, 1], ALU.max).then_inc(shift_steps, 1)
            dve.wait_ge(shift_steps, 3)
            nc.vector.tensor_scalar(shift[:], shift[:], EXP_SAFE, 0.0, ALU.subtract, ALU.max).then_inc(shift_steps, 1)
            dve.wait_ge(shift_steps, 4)
            nc.vector.tensor_scalar(shift[:], shift[:], -1.0, None, ALU.mult).then_inc(shift_steps, 1)
            for t in range(NT):
                dve.wait_ge(xT_high, t + 1)
                nc.vector.tensor_tensor(xT_l[:, :, t * P:(t + 1) * P],
                                        scores[:, (t % 4) // 2, t % 2, :].rearrange("p (k n) -> p k n", k=KC),
                                        xT_h[:, :, t * P:(t + 1) * P].bitcast(F32), ALU.subtract).then_inc(xT_low, 1)
                if t == 3:
                    dve_split_w(0)
            for c in range(2):
                dve_norms(0, c)
                if c == 0:
                    dve_split(0, c)
                    for h in range(HG):
                        dve_copy_k(0, 0, h)
            for g in range(NG):
                for slot in range(SLOTS):
                    for work in work_at(TURN_AT, slot, g):
                        dve_copy_k(*work)
                    if slot in STEP_AT and (slot or g):
                        i = STEP_AT.index(slot)
                        dve_outputs(g if i else g - 1, (i - 1) % NC)
                    if slot not in DIRECT:
                        dve_add_keys(g, slot)
                    for gg, c, stage in work_at(NORMALISE_AT, slot, g):
                        if stage == 0:
                            dve_norms(gg, c)
                        if stage == 2:
                            dve_split(gg, c)
                    if slot == SPLIT_W_AT and g + 1 < NG:
                        dve_split_w(g + 1)
            dve_outputs(NG - 1, NC - 1)
            tail_vector(dve)

        def pool_split_w(g):
            nc.gpsimd.wait_ge(w_high, g + 1)
            nc.gpsimd.tensor_tensor(wqkv_l[:], wqkv_raw[:], wqkv_h[:].bitcast(F32), ALU.subtract).then_inc(w_low, 1)

        def rope_views(c):
            half, shape = HD // 2, [P, 2 * TPC, HG // 2, HD // 2]
            rows = qk[:].rearrange("p w t h d -> p (w t) h d")[:, :, 0::2, :]
            angles = [m[:, c].rearrange("p w t f -> p (w t) f").unsqueeze(2).broadcast_to(shape) for m in (cos, sin)]
            return rows[:, :, :, 0:half], rows[:, :, :, half:HD], *angles

        def pool_rotate(g, c):
            C = NC * g + c
            first, second, cs, sn = rope_views(c)
            nc.gpsimd.wait_ge(normed, C + 1)
            nc.gpsimd.tensor_tensor(rope_prod[:, 0], first, cs, ALU.mult)
            nc.gpsimd.tensor_tensor(rope_prod[:, 1], second, sn, ALU.mult)
            nc.gpsimd.tensor_tensor(rope_prod[:, 2], first, sn, ALU.mult)
            nc.gpsimd.tensor_tensor(rope_prod[:, 3], second, cs, ALU.mult).then_inc(rope_products, 1)
            nc.gpsimd.wait_ge(rope_products, C + 1)
            nc.gpsimd.tensor_tensor(first, rope_prod[:, 0], rope_prod[:, 1], ALU.subtract).then_inc(roped, 1)
            nc.gpsimd.tensor_tensor(second, rope_prod[:, 2], rope_prod[:, 3], ALU.add).then_inc(roped, 1)

        def pool_add_keys(g, slot):
            i, j = step_of(slot)
            n = SLOTS * g + slot
            lo = max(0, (j - TPC * i) * P)
            nc.gpsimd.wait_ge(exp_done, 2 * n + 2)
            if added(g, slot) > 1:
                nc.gpsimd.wait_ge(sum_pool, added(g, slot) - 1)
            if j == 0 and 2 * g + i > 2:
                nc.gpsimd.wait_ge(sums_done, 2 * g + i - 2)
            new = probs[:, n % 4, 3, lo:CH]
            if j == 0:
                nc.gpsimd.tensor_tensor(key_sum[:, 3, :], new, ones[:, 0:1].broadcast_to([P, CH]), ALU.mult).then_inc(sum_pool, 1)
            else:
                nc.gpsimd.tensor_tensor(key_sum[:, 3, lo:CH], key_sum[:, 3, lo:CH], new, ALU.add).then_inc(sum_pool, 1)

        @block.gpsimd
        def _(pool):
            nc.gpsimd.memset(ident[:], 0.0)
            nc.gpsimd.memset(mask_b[:], 0.0)
            nc.gpsimd.memset(ident_b[:], 0.0)
            nc.gpsimd.memset(ones[:], 1.0).then_inc(mask_filled, 1)
            pool.wait_ge(mask_filled, 1)
            for m in (ident_b, ident):
                nc.gpsimd.affine_select(out=m[:], in_=m[:], compare_op=ALU.not_equal, fill=1.0, base=0,
                                        pattern=[[-1, P]], channel_multiplier=1)
            nc.gpsimd.affine_select(out=mask_b[:], in_=mask_b[:], compare_op=ALU.is_ge, fill=MASKED, base=0,
                                    pattern=[[1, P]], channel_multiplier=-1).then_inc(consts_ready, 1)
            pool.wait_ge(tables_loaded, 16 * 17)
            pool_split_w(0)
            for c in range(2):
                pool_rotate(0, c)
            for g in range(NG):
                for slot in range(SLOTS):
                    if slot not in DIRECT:
                        pool_add_keys(g, slot)
                    for gg, c, stage in work_at(NORMALISE_AT, slot, g):
                        if stage == 1:
                            pool_rotate(gg, c)
                    if slot == SPLIT_W_AT and g + 1 < NG:
                        pool_split_w(g + 1)
            tail_gpsimd(pool)


def kernel(L0_attn_x, L0_attn_w_qkv, L0_attn_w_out, L0_attn_q_gain, L0_ffn_gate_w, L0_ffn_w_gate, L0_ffn_w_up,
           L0_ffn_w_down, L0_ffn_sw_gate, L0_ffn_sw_up, L0_ffn_sw_down):
    import concourse.bacc as bacc
    from concourse.bass_utils import run_bass_kernel_spmd

    half = HD // 2
    inv_freq = np.float32(10000.0) ** (-np.arange(half, dtype=np.float32) / np.float32(half))
    theta = np.arange(T, dtype=np.float32)[:, None] * inv_freq.astype(np.float32)[None, :]
    arrays = dict(x=L0_attn_x, w_qkv=L0_attn_w_qkv, w_out=L0_attn_w_out, q_gain=L0_attn_q_gain,
                  gate_w=L0_ffn_gate_w, w_gate=L0_ffn_w_gate, w_up=L0_ffn_w_up, w_down=L0_ffn_w_down,
                  sw_gate=L0_ffn_sw_gate, sw_up=L0_ffn_sw_up, sw_down=L0_ffn_sw_down,
                  rope_cos=np.cos(theta), rope_sin=np.sin(theta))
    arrays = {name: np.ascontiguousarray(a) for name, a in arrays.items()}
    nc = bacc.Bacc("TRN2", target_bir_lowering=False, num_devices=1)
    args = [nc.dram_tensor(name, a.shape, mybir.dt.from_np(a.dtype), kind="ExternalInput").ap()
            for name, a in arrays.items()]
    out = nc.dram_tensor("out", L0_attn_x.shape, F32, kind="ExternalOutput").ap()
    build(nc, *args, out)
    result = run_bass_kernel_spmd(nc, [arrays], core_ids=[0])
    return result.results[0]["out"]
```

```python
from contextlib import ExitStack

import numpy as np

import concourse.bass as bass
import concourse.mybir as mybir

F32 = mybir.dt.float32
F32R = mybir.dt.float32r
BF16 = mybir.dt.bfloat16
I32 = mybir.dt.int32
U32 = mybir.dt.uint32
ALU = mybir.AluOpType
ACT = mybir.ActivationFunctionType
AX = mybir.AxisListType.X

P = 128
T, D = 2048, 512
NT, KC = T // P, D // P
HEADS, HD = 16, 32
HG = 4
NG = HEADS // HG
CH = 512
NC, TPC = T // CH, CH // P
E, TOPK, FH, FS = 8, 2, 352, 704
MAX_TILES = TOPK * T // P + E - 1
UNIT_EPS, LN_EPS = 1e-6, 1e-5
MASKED = -1.0e30
RSQRT_GUESS = float(0x5F3759DF)
EXP_SAFE = 80.0

STEP_AT = [0, 4, 12, 24, 40]
SLOTS = STEP_AT[-1]
PROJECT_AT = {(2, 0): 0, (2, 1): 1, (2, 2): 2, (2, 3): 3,
              (3, 0): 8, (3, 1): 9, (3, 2): 10, (3, 3): 11,
              (0, 0): 25, (0, 1): 26, (0, 2): 27, (0, 3): 28,
              (1, 0): 32, (1, 1): 33, (1, 2): 34, (1, 3): 35}
NORMALISE_AT = {(2, 0): 4, (2, 1): 5, (2, 2): 7,
                (3, 0): 12, (3, 1): 13, (3, 2): 15,
                (0, 0): 29, (0, 1): 30, (0, 2): 31,
                (1, 0): 36, (1, 1): 37, (1, 2): 39}
TURN_AT = {(1, 0): 0, (1, 1): 1, (1, 2): 2, (1, 3): 3,
           (2, 0): 8, (2, 1): 9, (2, 2): 10, (2, 3): 11,
           (3, 0): 16, (3, 1): 17, (3, 2): 18, (3, 3): 19,
           (0, 0): 32, (0, 1): 33, (0, 2): 34, (0, 3): 35}
SPLIT_W_AT = 20
SPLIT_WO_AT = 26
DIRECT = set(range(STEP_AT[2])) | {13, 14, 15, 22, 23, 29, 30, 31, 36, 37, 38, 39}


def work_at(table, slot, g):
    for (c, part), at in table.items():
        ahead = c < 2 and slot >= STEP_AT[3]
        if at == slot and g + ahead < NG:
            yield g + ahead, c, part


def step_of(slot):
    i = max(n for n in range(NC) if STEP_AT[n] <= slot)
    return i, slot - STEP_AT[i]


def build(nc, x, w_qkv, w_out, q_gain, gate_w, w_gate, w_up, w_down, sw_gate, sw_up, sw_down,
          rope_cos, rope_sin, numbers, out):
    with ExitStack() as ctx:
        def sem(name):
            return ctx.enter_context(nc.semaphore(name))

        BASE = -(-nc.sbuf_base // 32) * 32
        TOP = 229344

        def at(name, offset, shape, dt):
            size = int(np.prod(shape[1:])) * (2 if dt == BF16 else 4)
            assert BASE + offset + size <= TOP, (name, offset, size)
            return nc.alloc_sbuf_tensor_at(name, shape, dt, offset=BASE + offset)

        xT_h = at("xT_h", 0, [P, KC, T], F32R)
        xT_l = at("xT_l", 32768, [P, KC, T], F32R)
        k_stack = at("k_stack", 65536, [P, HG, T], F32R)
        q_stack = at("q_stack", 98304, [P, 2, HG, CH], F32R)
        v_sb = at("v_sb", 114688, [P, NT, P], F32)
        wqkv_h = at("wqkv_h", 122880, [P, KC, 3 * P], F32R)
        wqkv_l = at("wqkv_l", 129024, [P, KC, 3 * P], F32R)
        probs = at("probs", 135168, [P, 4, HG, CH], F32)
        x_in = at("x_in", 135168, [P, 4, D], F32)
        key_sum = at("key_sum", 167936, [P, HG, CH], F32)
        qk = at("qk", 176128, [P, 2, TPC, HG, HD], F32)
        squares = at("squares", 180224, [P, 2, TPC, HG, HD], F32)
        rope_prod = at("rope_prod", 180224, [P, 2, 4, TPC, HG // 2, HD // 2], F32)
        wqkv_raw = at("wqkv_raw", 176128, [P, KC, 3 * P], F32)
        split = at("split", 184320, [P, 2, TPC, HG, 3, HD], F32R)
        y_norm = at("y_norm", 196608, [P, 2, CH], F32)
        inv_sum = at("inv_sum", 200704, [P, CH], F32)
        cos = at("cos", 202752, [P, NC, TPC, HD // 2], F32)
        sin = at("sin", 204800, [P, NC, TPC, HD // 2], F32)
        ident = at("ident", 208896, [P, P], F32)
        ident_r = at("ident_r", 206848, [P, P], F32R)
        ident_b = at("ident_b", 209408, [P, P], BF16)
        mask_b = at("mask_b", 209664, [P, P], BF16)
        ones = at("ones", 209920, [P, HD], F32)
        gain = at("gain", 210048, [P, HEADS], F32)
        gain_abs = at("gain_abs", 210112, [P, HEADS], F32)
        shift = at("shift", 210176, [P, HEADS // 2], F32)
        sq_sum = at("sq_sum", 210208, [P, 2, TPC, HG], F32)
        inv_norm = at("inv_norm", 210464, [P, 2, TPC, HG], F32)
        newton = at("newton", 210592, [P, 2, TPC, HG], F32)
        inv_col = at("inv_col", 210720, [P, CH // 32], F32)

        scores = ctx.enter_context(nc.psum_tensor("scores", [P, 2, 2, CH], F32))
        bank = [ctx.enter_context(nc.psum_tensor(f"bank{n}", [P, CH], F32)) for n in range(4)]
        y_ps, sums_ps, qkv_ps, turn_ps = bank

        y_dram = nc.dram_tensor("y_scratch", [NG, P, T], F32, kind="Internal").ap()

        consts_ready, ident_ready, mask_filled = sem("consts_ready"), sem("ident_ready"), sem("mask_filled")
        tables_loaded = sem("tables_loaded")
        shift_steps = sem("shift_steps")
        x_loaded = [sem(f"x_loaded{n}") for n in range(4)]
        x_turned, xT_high, xT_low = sem("x_turned"), sem("xT_high"), sem("xT_low")
        w_loaded, w_high, w_low = sem("w_loaded"), sem("w_high"), sem("w_low")
        qkv_done, qkv_copied = sem("qkv_done"), sem("qkv_copied")
        norm_steps, inv_normed, sums_inverted = sem("norm_steps"), sem("inv_normed"), sem("sums_inverted")
        normed = sem("normed")
        q_products, k_products, q_roped, k_roped = sem("q_products"), sem("k_products"), sem("q_roped"), sem("k_roped")
        split_high, split_low = sem("split_high"), sem("split_low")
        turned, q_ready, k_ready = sem("turned"), sem("q_ready"), sem("k_ready")
        scores_ready, exp_done, pv_done = sem("scores_ready"), sem("exp_done"), sem("pv_done")
        sum_dve, sum_pool = sem("sum_dve"), sem("sum_pool")
        sums_done, sums_read = sem("sums_done"), sem("sums_read")
        y_copied, y_ready = sem("y_copied"), sem("y_ready")
        y_stored = [sem(f"y_stored{n}") for n in range(2)]


        x1T_h = at("x1T_h", 0, [P, KC, T], F32R)
        x1T_l = at("x1T_l", 32768, [P, KC, T], F32R)
        x1 = at("x1", 65536, [P, NT, D], F32)
        x_res = at("x_res", 193536, [P, 4, D], F32)
        rows = at("rows", 106496, [P, 4, D], F32)
        y_raw = at("y_raw", 114688, [P, 4, NG, P], F32)
        wo_l = at("wo_l", 122880, [P, NG, D], F32R)
        gw_raw = at("gw_raw", 131072, [P, KC, E], F32)
        gw_h = at("gw_h", 131200, [P, KC, E], F32R)
        gw_l = at("gw_l", 131328, [P, KC, E], F32R)
        wo_raw = at("wo_raw", 176128, [P, NG, D], F32)
        wo_h = at("wo_h", 185344, [P, NG, D], F32R)
        y_h = at("y_h", 98304, [P, 2, NG, P], F32R)
        y_l = at("y_l", 102400, [P, 2, NG, P], F32R)
        y_first = [at(f"y_first{n}", 8192 * (n // 2) + 4096 + 2048 * (n % 2), [P, NG, P], F32) for n in range(TPC)]
        x_first = [at(f"x_first{n}", 16384 + 8192 * (n // 2) + 4096 + 2048 * (n % 2), [P, D], F32) for n in range(TPC)]
        GATE, UP, DOWN = 0, 2 * KC * FH, 4 * KC * FH
        SLOT = 4 * KC * FH + 6 * D
        ffn_w = at("ffn_w", 98304, [P, 2, SLOT], F32R)
        raw = at("raw", 167936, [P, SLOT // 2], F32)
        silu = at("silu", 185344, [P, 2, CH], F32)
        hid_h = at("hid_h", 189440, [P, 3, CH], F32R)
        hid_l = at("hid_l", 195584, [P, 3, CH], F32R)
        stage = at("stage", 201728, [P, 2, D], F32)
        R0 = 179200
        logits = at("logits", R0, [P, NT, E], F32)
        shares = at("shares", R0 + 512, [P, NT, E], F32)
        top_values = at("top_values", R0 + 1024, [P, NT, E], F32)
        top_index = at("top_index", R0 + 1536, [P, NT, E], U32)
        ended = at("ended", R0, [P, MAX_TILES, E - 1], F32)
        chosen = at("chosen", R0 + 2048, [P, TOPK, NT, E], F32)
        place = at("place", R0 + 3072, [P, NT, E], F32)
        total = at("total", R0 + 3584, [P, NT, E], F32)
        before = at("before", R0 + 4096, [P, 2, NT, E], F32)
        product = at("product", R0 + 5120, [P, NT, E], F32)
        chosen_b = at("chosen_b", R0 + 5632, [P, NT, E], BF16)
        row_max = at("row_max", 205824, [P, NT], F32)
        row_sum = at("row_sum", 205888, [P, NT], F32)
        top_float = at("top_float", 205952, [P, NT, TOPK], F32)
        place_float = at("place_float", 206080, [P, TOPK, NT], F32)
        tiles_int = at("tiles_int", 206208, [P, E], I32)
        tiles_of = at("tiles_of", 206240, [P, E], F32)
        tile_end = at("tile_end", 206272, [P, 2, E], F32)
        tile_start = at("tile_start", 206336, [P, E], F32)
        tile_expert = at("tile_expert", 206368, [P, MAX_TILES], F32)
        weight = at("weight", 206528, [P, TOPK, NT], F32)
        x_tile = at("x_tile", 185344, [P, 2, D], F32)
        xt_h = at("xt_h", 189440, [P, KC, P], F32R)
        xt_l = at("xt_l", 191488, [P, KC, P], F32R)
        silu_t = at("silu_t", 193536, [P, FH], F32)
        hidden = at("hidden", 194944, [P, FH], F32)
        ht_h = at("ht_h", 196352, [P, 3, P], F32R)
        ht_l = at("ht_l", 197888, [P, 3, P], F32R)
        y_tile = at("y_tile", 199424, [P, 2, D], F32)
        extra = at("extra", 133120, [P, 4, 3, D], F32)
        stats = at("stats", 207360, [P, TPC, 6], F32)
        moments = at("moments", 207456, [P, TPC, 2], F32)
        var_eps = at("var_eps", 207488, [P, TPC], F32)
        rstd = at("rstd", 207520, [P, TPC], F32)
        mean_over = at("mean_over", 207584, [P, TPC], F32)
        ln_work = at("ln_work", 207552, [P, TPC], F32)
        place_int = at("place_int", 210784, [P, TOPK, NT], I32)
        tile_slot = at("tile_slot", 210912, [P, MAX_TILES], I32)
        tile_needs = at("tile_needs", 211072, [P, MAX_TILES], I32)
        tile_numbers = at("tile_numbers", 211392, [P, MAX_TILES], F32)
        tri_b = at("tri_b", 211584, [P, P], BF16)
        ones_b = at("ones_b", 211840, [P, P], BF16)
        start_int = at("start_int", 212096, [P, E], I32)
        zeros = at("zeros", 159744, [P, D], F32)

        HC = [(0, P), (P, P), (2 * P, FH - 2 * P)]
        xs_dram = nc.dram_tensor("x_sorted", [MAX_TILES * P, D], F32, kind="Internal").ap()
        ys_dram = nc.dram_tensor("y_sorted", [MAX_TILES * P, D], F32, kind="Internal").ap()
        half_dram = nc.dram_tensor("first_half", [T, D], F32, kind="Internal").ap()

        lot0_high, lot0_low, ln_ready = sem("lot0_high"), sem("lot0_low"), sem("ln_ready")
        half_added = sem("half_added")
        wo_loaded, wo_high, wo_low = sem("wo_loaded"), sem("wo_high"), sem("wo_low")
        y_loaded = [sem(f"y_loaded{n}") for n in range(4)]
        y_high, y_low = sem("y_high"), sem("y_low")
        projected, res_added, ln_steps, x1_ready = sem("projected"), sem("res_added"), sem("ln_steps"), sem("x1_ready")
        x1_turned, x1T_high, x1T_low = sem("x1_turned"), sem("x1T_high"), sem("x1T_low")
        logits_done, router_steps, router_exp, tables_made = sem("logits_done"), sem("router_steps"), sem("router_exp"), sem("tables_made")
        counted = sem("counted")
        ffn_loaded = [sem(f"ffn_loaded{n}") for n in range(3)]
        ffn_high, ffn_low = sem("ffn_high"), sem("ffn_low")
        gated, silu_done, product_done = sem("gated"), sem("silu_done"), sem("product_done")
        hid_high, hid_low, down_done, down_read = sem("hid_high"), sem("hid_low"), sem("down_done"), sem("down_read")
        half_stored = [sem(f"half_stored{n}") for n in range(2)]
        zero_made, zero_filled, scattered = sem("zero_made"), sem("zero_filled"), sem("scattered")
        xs_loaded = [sem(f"xs_loaded{n}") for n in range(2)]
        xs_turned, xt_high, xt_low = sem("xs_turned"), sem("xt_high"), sem("xt_low")
        tile_gated, tile_upped, tile_silu, tile_hidden = sem("tile_gated"), sem("tile_upped"), sem("tile_silu"), sem("tile_hidden")
        hid_turned, ht_high, ht_low = sem("hid_turned"), sem("ht_high"), sem("ht_low")
        tile_done, tile_copied = sem("tile_done"), sem("tile_copied")
        ys_stored = [sem(f"ys_stored{n}") for n in range(2)]
        half_loaded, gathered = [sem(f"half_loaded{n}") for n in range(4)], [sem(f"gathered{n}") for n in range(4)]
        extras_added = sem("extras_added")
        numbers_loaded = sem("numbers_loaded")
        out_ready, out_stored = sem("out_ready"), sem("out_stored")
        out_rows = out.rearrange("b s d -> (b s) d")
        z_ps = [scores[:, 0, 0], scores[:, 0, 1]]
        x1T_ps = [bank[0][:], bank[1][:]]

        def y_of(t):
            return y_raw[:, t % 4] if t >= TPC else y_first[t][:]

        def x_of(t):
            return x_res[:, t % 4] if t >= TPC else x_first[t][:]

        logits_ps, counts_ps = turn_ps, qkv_ps
        gate_tile, up_tile, xt_ps, ht_ps, out_tile = scores[:, 0, 0], scores[:, 0, 1], scores[:, 1, 0], scores[:, 1, 1], bank[0]

        LOTS = E + 2
        PIECES = 3
        RAW_AT = [0, KC * FH, 2 * KC * FH]

        def slot_of(lot):
            return (lot + 1) % 2

        def weights_of(lot):
            if 0 < lot < LOTS - 1:
                return w_gate[lot - 1], w_up[lot - 1], w_down[lot - 1]
            half = slice(0, FH) if lot == 0 else slice(FH, FS)
            return sw_gate[:, half], sw_up[:, half], sw_down[half, :]

        def areas_of(lot, piece):
            slot, first = slot_of(lot), (GATE, UP, DOWN)[piece]
            n = KC * FH if piece < 2 else 3 * D
            r, full = FH - 2 * P, 2 * D
            if piece < 2:
                cuts = [(P, 0, n)]
            else:
                cuts = [(P, 0, full), (r, full, n)]
            return [(raw[0:p, RAW_AT[piece] + a:RAW_AT[piece] + b],
                     [ffn_w[0:p, slot, first + low * n + a:first + low * n + b] for low in range(2)]) for p, a, b in cuts]

        def stationary(slot, at_, low, k, c0, cn):
            first = at_ + low * KC * FH + k * FH + c0
            return ffn_w[:, slot, first:first + cn]

        def load_y(sp, t):
            sp.dma_start(y_of(t), y_dram[:, :, t * P:(t + 1) * P].rearrange("g p t -> p g t")).then_inc(y_loaded[t % 4], 16)
            sp.dma_start(x_of(t), x_rows[t * P:(t + 1) * P, :]).then_inc(y_loaded[t % 4], 16)

        def load_piece(sp, lot, piece):
            if lot == 1:
                sp.wait_ge(lot0_low, piece + 1)
            if lot > 1:
                sp.wait_ge(ffn_low, PIECES * (lot - 2) + piece + 1)
            src, to = weights_of(lot)[piece], raw[:, RAW_AT[piece]:]
            if piece < 2:
                sp.dma_start(to[:, 0:KC * FH].rearrange("p (k n) -> p k n", k=KC), src.rearrange("(k p) n -> p k n", p=P)).then_inc(ffn_loaded[piece], 16)
            else:
                sp.dma_start(to[:, 0:2 * D].rearrange("p (k n) -> p k n", k=2), src[0:2 * P].rearrange("(k p) n -> p k n", p=P)).then_inc(ffn_loaded[piece], 16)
                sp.dma_start(to[0:FH - 2 * P, 2 * D:3 * D], src[2 * P:FH]).then_inc(ffn_loaded[piece], 16)

        def tail_sync(sp):
            sp.wait_ge(pv_done, SLOTS * NG)
            for n in range(2):
                sp.wait_ge(y_stored[n], 16 * NC * NG // 2)
            for t in range(TPC, NT):
                if t >= 2 * TPC:
                    sp.wait_ge(y_low, t - 3)
                    sp.wait_ge(y_high, t - 3)
                    sp.wait_ge(res_added, t - 3)
                load_y(sp, t)
                if t == 2 * TPC - 1:
                    sp.wait_ge(sums_done, 2 * NG)
                    for piece in range(PIECES):
                        load_piece(sp, 0, piece)
            for piece in range(2):
                load_piece(sp, 1, piece)

            def store_half(t):
                sp.wait_ge(down_read, t + 1)
                sp.dma_start(half_dram[t * P:(t + 1) * P, :], stage[:, t % 2]).then_inc(half_stored[t % 2], 16)

            for t in range(TPC):
                store_half(t)
            sp.wait_ge(router_steps, R_STEPS)
            load_piece(sp, 1, 2)
            for t in range(TPC, 2 * TPC):
                store_half(t)
            for piece in range(2):
                load_piece(sp, 2, piece)
            load_piece(sp, 2, 2)
            for t in range(2 * TPC, NT - TPC):
                store_half(t)
            sp.wait_ge(scattered, 16 * TOPK * NT)
            for j in range(2):
                sp.wait_ge(hid_low, 3 * NC - 1 + j)
                sp.dma_start(x_tile[:, j], xs_dram[j * P:(j + 1) * P, :]).then_inc(xs_loaded[j], 16)
            for t in range(NT - TPC, NT):
                store_half(t)
            for lot in range(3, LOTS):
                for piece in range(PIECES):
                    load_piece(sp, lot, piece)
            for n in range(2):
                sp.wait_ge(half_stored[n], 16 * NT // 2)
            sp.wait_ge(tile_done, MAX_TILES + 1)
            for t in range(NT):
                if t >= 4:
                    sp.wait_ge(half_added, t - 3)
                sp.dma_start(extra[:, t % 4, 0], half_dram[t * P:(t + 1) * P, :]).then_inc(half_loaded[t % 4], 16)
            for t in range(NT):
                sp.wait_ge(out_ready, t + 1)
                sp.dma_start(out_rows[t * P:(t + 1) * P, :], x1[:, t]).then_inc(out_stored, 16)
            sp.wait_ge(out_stored, 16 * NT)

        def tail_tensor(pe):
            pe.wait_ge(wo_high, 2)
            pe.wait_ge(wo_low, 2)
            for t in range(NT):
                pe.wait_ge(y_high, t + 1)
                pe.wait_ge(y_low, t + 1)
                if t >= 2:
                    pe.wait_ge(res_added, t - 1)
                for m, (ys, ws) in enumerate(((y_h, wo_h), (y_l, wo_h), (y_h, wo_l))):
                    for g in range(NG):
                        mm = nc.tensor.matmul(z_ps[t % 2], ys[:, t % 2, g, :], ws[:, g, :],
                                              start=(m == 0 and g == 0), stop=(m == 2 and g == NG - 1))
                mm.then_inc(projected, 1)
                if t >= TURN_LAG:
                    pe_turn_x1(pe, t - TURN_LAG)
                if t > TURN_LAG:
                    pe_logits(pe, t - TURN_LAG - 1)
            for s in range(NT - TURN_LAG, NT - TPC):
                pe_turn_x1(pe, s)
                pe_logits(pe, s - 1)
            pe_shared(pe, 0)
            pe.wait_ge(router_steps, R_STEPS)
            pe.wait_ge(product_done, 3 * NC)
            pe.wait_ge(down_read, NT)
            pe.sem_inc(tile_done, 1)
            for j in range(MAX_TILES + 1):
                if 0 <= j < MAX_TILES:
                    needs = pe.value_load(tile_needs[0:1, j:j + 1], min_val=0, max_val=PIECES * LOTS)
                    slot = pe.value_load(tile_slot[0:1, j:j + 1], min_val=0, max_val=1)
                    pe.wait_ge(ffn_low, needs)
                    pe.wait_ge(xt_high, j + 1)
                    pe.wait_ge(xt_low, j + 1)
                    if j:
                        pe.wait_ge(tile_silu, j)
                        pe.wait_ge(tile_hidden, j)
                    for m, (xs, low) in enumerate(((xt_h, 0), (xt_l, 0), (xt_h, 1))):
                        for k in range(KC):
                            mm = nc.tensor.matmul(gate_tile[:, 0:FH], xs[:, k, :], moving(slot, GATE + (low * KC + k) * FH, FH),
                                                  start=(m == 0 and k == 0), stop=(m == 2 and k == KC - 1))
                    mm.then_inc(tile_gated, 1)
                if j >= 1:
                    i = j - 1
                    pe.wait_ge(tile_hidden, i + 1)
                    if i:
                        pe.wait_ge(ht_low, i)
                    for k, (k0, kn) in enumerate(HC):
                        mm = nc.tensor.transpose(ht_ps[0:kn, k * P:(k + 1) * P], hidden[:, k0:k0 + kn], ident[:])
                    mm.then_inc(hid_turned, 1)
                if 0 <= j < MAX_TILES:
                    for m, (xs, low) in enumerate(((xt_h, 0), (xt_l, 0), (xt_h, 1))):
                        for k in range(KC):
                            mm = nc.tensor.matmul(up_tile[:, 0:FH], xs[:, k, :], moving(slot, UP + (low * KC + k) * FH, FH),
                                                  start=(m == 0 and k == 0), stop=(m == 2 and k == KC - 1))
                    mm.then_inc(tile_upped, 1)
                if 0 <= j < MAX_TILES - 1:
                    turn_x_tile(pe, j + 1)
                if j >= 1:
                    i = j - 1
                    pe.wait_ge(ht_high, i + 1)
                    pe.wait_ge(ht_low, i + 1)
                    if i:
                        pe.wait_ge(tile_copied, i)
                    for m, (hs, low) in enumerate(((ht_h, 0), (ht_l, 0), (ht_h, 1))):
                        for k, (k0, kn) in enumerate(HC):
                            mm = nc.tensor.matmul(out_tile[:], hs[0:kn, k, :], moving(slot_before, DOWN + (low * 3 + k) * D, D, kn),
                                                  start=(m == 0 and k == 0), stop=(m == 2 and k == 2))
                    mm.then_inc(tile_done, 1)
                if 0 <= j < MAX_TILES:
                    slot_before = slot
            pe.wait_ge(tile_copied, MAX_TILES)
            pe_shared(pe, 1)

        def turn_x_tile(pe, i):
            pe.wait_ge(xs_loaded[i % 2], 16 * (i // 2 + 1))
            if i:
                pe.wait_ge(xt_low, i)
            else:
                pe.wait_ge(product_done, 3 * NC)
            for k in range(KC):
                mm = nc.tensor.transpose(xt_ps[:, k * P:(k + 1) * P], x_tile[:, i % 2, k * P:(k + 1) * P], ident[:])
            mm.then_inc(xs_turned, 1)

        def pe_turn_x1(pe, s):
            pe.wait_ge(x1_ready, s + 1)
            if s >= 2:
                pe.wait_ge(x1T_low, s - 1)
            for k in range(KC):
                mm = nc.tensor.transpose(x1T_ps[s % 2][:, k * P:(k + 1) * P], x1[:, s, k * P:(k + 1) * P], ident[:])
            mm.then_inc(x1_turned, 1)

        def pe_logits(pe, s):
            pe.wait_ge(x1T_high, s + 1)
            pe.wait_ge(x1T_low, s + 1)
            for m, (xs, ws) in enumerate(((x1T_h, gw_h), (x1T_h, gw_l), (x1T_l, gw_h))):
                for k in range(KC):
                    mm = nc.tensor.matmul(logits_ps[:, s * E:(s + 1) * E], xs[:, k, s * P:(s + 1) * P], ws[:, k, :],
                                          start=(m == 0 and k == 0), stop=(m == 2 and k == KC - 1))
            mm.then_inc(logits_done, 1)

        def moving(slot, first, n, rows_=P):
            return ffn_w[0:rows_, bass.ds(slot, 1), first:first + n].rearrange("p a n -> p (a n)")

        def pe_shared(pe, half):
            lot = half * (LOTS - 1)
            slot = slot_of(lot)
            if half == 0:
                pe.wait_ge(lot0_low, PIECES)
            else:
                pe.wait_ge(ffn_low, PIECES * lot)
            for c in range(NC + 1):
                for hc, (h0, hn) in enumerate(HC):
                    b = half * NC + c
                    if c < NC:
                        n = b * 3 + hc
                        if n >= 2:
                            pe.wait_ge(product_done, n - 1)
                        for which, at_ in enumerate((GATE, UP)):
                            for m, (xs, low) in enumerate(((x1T_h, 0), (x1T_l, 0), (x1T_h, 1))):
                                for k in range(KC):
                                    mm = nc.tensor.matmul(scores[0:hn, which, n % 2, :], stationary(slot, at_, low, k, h0, hn),
                                                          xs[:, k, c * CH:(c + 1) * CH],
                                                          start=(m == 0 and k == 0), stop=(m == 2 and k == KC - 1))
                            mm.then_inc(gated, 1)
                        if half == 0 and n == 0:
                            pe_logits(pe, NT - TPC - 1)
                        if half == 0 and n < 2:
                            for s in range(NT - TPC + 2 * n, NT - TPC + 2 * n + 2):
                                pe_turn_x1(pe, s)
                        if half == 0 and 1 <= n < 3:
                            for s in range(NT - TPC + 2 * n - 2, NT - TPC + 2 * n):
                                pe_logits(pe, s)
                        if half == 0 and n == COUNT_AT:
                            pe.wait_ge(router_steps, CHOSEN_STEPS)
                            pe.wait_ge(tables_made, 1)
                            flat = chosen_b[:].rearrange("p t e -> p (t e)")
                            nc.tensor.matmul(counts_ps[:, 0:NT * E], tri_b[:], flat, start=True, stop=True)
                            nc.tensor.matmul(counts_ps[:, NT * E:2 * NT * E], ones_b[:], flat, start=True, stop=True).then_inc(counted, 1)
                    if half == 0 and c == NC and hc == 0:
                        turn_x_tile(pe, 0)
                    if hc == 0 and c:
                        b -= 1
                        pe.wait_ge(hid_high, 3 * (b + 1))
                        pe.wait_ge(hid_low, 3 * (b + 1))
                        for tt in range(TPC):
                            n = 4 * b + tt
                            if n >= 2:
                                pe.wait_ge(down_read, n - 1)
                            for m, (hs, low) in enumerate(((hid_h, 0), (hid_l, 0), (hid_h, 1))):
                                for k, (k0, kn) in enumerate(HC):
                                    first = DOWN + (low * 3 + k) * D
                                    mm = nc.tensor.matmul(bank[n % 2][:], hs[0:kn, k, tt * P:(tt + 1) * P], ffn_w[0:kn, slot, first:first + D],
                                                          start=(m == 0 and k == 0), stop=(m == 2 and k == 2))
                            mm.then_inc(down_done, 1)

        def tail_scalar(act):
            def act_split_y(t):
                act.wait_ge(y_loaded[t % 4], 32 * (t // 4 + 1))
                if t >= 2:
                    act.wait_ge(projected, t - 1)
                nc.scalar.copy(y_h[:, t % 2], y_of(t)).then_inc(y_high, 1)

            act_split_y(0)
            for t in range(NT + 2):
                if t + 1 < NT:
                    act_split_y(t + 1)
                if t % 4 == 1 and 4 < t < NT:
                    act_norm(act, t // 4 - 1, lambda i: rows[:, i], x1_ready)
                if t in LOT0_HIGH_AT:
                    piece = LOT0_HIGH_AT.index(t)
                    act.wait_ge(ffn_loaded[piece], 16 if piece < 2 else 32)
                    if piece == 0:
                        act.wait_ge(pv_done, SLOTS * NG)
                    for src, (high, low) in areas_of(0, piece):
                        last = nc.scalar.copy(high, src)
                    last.then_inc(lot0_high, 1)
                if t >= TURN_LAG:
                    act_x1T(act, t - TURN_LAG)
            act_shared(act, 0)
            for j in range(-1, MAX_TILES + 1):
                if 0 <= j < MAX_TILES:
                    act.wait_ge(tile_gated, j + 1)
                    if j:
                        act.wait_ge(tile_hidden, j)
                    nc.scalar.activation(silu_t[:], gate_tile[:, 0:FH], ACT.Silu).then_inc(tile_silu, 1)
                if j >= 1:
                    i = j - 1
                    act.wait_ge(hid_turned, i + 1)
                    if i:
                        act.wait_ge(tile_done, i + 1)
                    nc.scalar.copy(ht_h[:, 0:2], ht_ps[:, 0:2 * P].rearrange("p (k n) -> p k n", k=2))
                    nc.scalar.copy(ht_h[0:FH - 2 * P, 2], ht_ps[0:FH - 2 * P, 2 * P:3 * P]).then_inc(ht_high, 1)
                if j + 1 < MAX_TILES:
                    i = j + 1
                    act.wait_ge(xs_turned, i + 1)
                    if i + 2 < MAX_TILES:
                        act.dma_start(x_tile[:, i % 2], xs_dram[(i + 2) * P:(i + 3) * P, :]).then_inc(xs_loaded[i % 2], 16)
                    if i:
                        act.wait_ge(tile_upped, i)
                    else:
                        act.wait_ge(down_done, NT)
                    nc.scalar.copy(xt_h[:], xt_ps.rearrange("p (k n) -> p k n", k=KC)).then_inc(xt_high, 1)
                if j >= 1:
                    i = j - 1
                    act.wait_ge(tile_done, i + 2)
                    if i >= 2:
                        act.wait_ge(ys_stored[i % 2], 16 * (i // 2))
                    elif i == 0:
                        for n in range(2):
                            act.wait_ge(half_stored[n], 16 * NT // 2)
                    nc.scalar.copy(y_tile[:, i % 2], out_tile[:]).then_inc(tile_copied, 1)
                    act.wait_ge(tile_copied, i + 1)
                    act.dma_start(ys_dram[i * P:(i + 1) * P, :], y_tile[:, i % 2]).then_inc(ys_stored[i % 2], 16)
            act_shared(act, 1)
            act_norm(act, NC - 1, lambda i: x1[:, TPC * (NC - 1) + i], out_ready)

        def act_norm(act, c, src, done):
            act.wait_ge(ln_ready, c + 1 if done is x1_ready else NC + c + 1)
            for i in range(TPC):
                nc.scalar.activation(x1[:, TPC * c + i], src(i), ACT.Identity, bias=mean_over[:, i:i + 1], scale=rstd[:, i:i + 1]).then_inc(done, 1)

        def act_x1T(act, s):
            act.wait_ge(x1_turned, s + 1)
            nc.scalar.copy(x1T_h[:, :, s * P:(s + 1) * P],
                           x1T_ps[s % 2].rearrange("p (k n) -> p k n", k=KC)).then_inc(x1T_high, 1)

        def act_shared(act, half):
            for c in range(NC):
                b = half * NC + c
                for hc, (h0, hn) in enumerate(HC):
                    n = b * 3 + hc
                    act.wait_ge(gated, 2 * n + 1)
                    if n >= 2:
                        act.wait_ge(hid_low, n - 1)
                    if half == 1 and n == 3 * NC:
                        act.wait_ge(ht_low, MAX_TILES)
                        for i in range(2):
                            act.wait_ge(ys_stored[i], 16 * ((MAX_TILES + 1 - i) // 2))
                    nc.scalar.activation(silu[0:hn, n % 2], scores[0:hn, 0, n % 2, :], ACT.Silu).then_inc(silu_done, 1)
                    act.wait_ge(product_done, n + 1)
                    if b:
                        act.wait_ge(down_done, 4 * b)
                    nc.scalar.copy(hid_h[0:hn, hc], silu[0:hn, n % 2]).then_inc(hid_high, 1)
                    if half == 0 and n == 0:
                        act_norm(act, NC - 1, lambda i: rows[:, i], x1_ready)
                    if half == 0 and n < 2:
                        for s in range(NT - TPC + 2 * n, NT - TPC + 2 * n + 2):
                            act_x1T(act, s)
                    if half == 1 and hc == 1 and c:
                        act_norm(act, c - 1, lambda i: x1[:, TPC * (c - 1) + i], out_ready)
                    if half == 0 and n == ROUTER_AT[0]:
                        act.wait_ge(router_steps, 3)
                        nc.scalar.activation(shares[:], shares[:], ACT.Exp).then_inc(router_exp, 1)

        def layernorm(n, c):
            for i in range(TPC):
                nc.vector.bn_aggr(moments[:, i], stats[:, i]).then_inc(ln_steps, 1)
            nc.vector.wait_ge(ln_steps, n + 4)
            nc.vector.tensor_scalar(var_eps[:], moments[:, :, 1], LN_EPS, None, ALU.add).then_inc(ln_steps, 1)
            nc.vector.wait_ge(ln_steps, n + 5)
            if c:
                nc.vector.wait_ge(x1_ready, min(TPC * c, NT))
            if c > NC:
                nc.vector.wait_ge(out_ready, TPC * (c - NC))
            dve_rsqrt(rstd[:], ln_work[:], var_eps[:], ln_steps, n + 5)
            nc.vector.scalar_tensor_tensor(mean_over[:], moments[:, :, 0], -1.0, rstd[:], ALU.mult, ALU.mult).then_inc(ln_ready, 1)

        LN_STEPS = 4 + 4 + 1 + 11
        CHOSEN_STEPS = 9
        TURN_LAG = 6
        LOT0_HIGH_AT = [9, 11, 13]
        LOT0_LOW_AT = [9, 11, 13]

        def tail_vector(dve):
            for t in range(NT + 2):
                if t < NT:
                    dve.wait_ge(projected, t + 1)
                    if t >= 4:
                        dve.wait_ge(x1_ready, t - 3)
                    if t % 4 == 0 and t:
                        dve.wait_ge(ln_ready, t // 4)
                    nc.vector.tensor_tensor(rows[:, t % 4], z_ps[t % 2], x_of(t), ALU.add).then_inc(res_added, 1)
                    dve.wait_ge(res_added, t + 1)
                    nc.vector.bn_stats(stats[:, t % TPC], rows[:, t % 4]).then_inc(ln_steps, 1)
                if t < NT and t % TPC == TPC - 1:
                    c = t // TPC
                    dve.wait_ge(ln_steps, LN_STEPS * c + 4)
                    layernorm(LN_STEPS * c + 4, c)
                if t >= TURN_LAG:
                    dve_x1T(dve, t - TURN_LAG)
                if t in LOT0_LOW_AT:
                    piece = LOT0_LOW_AT.index(t)
                    dve.wait_ge(lot0_high, piece + 1)
                    for src, (high, low) in areas_of(0, piece):
                        last = nc.vector.tensor_tensor(low, src, high.bitcast(F32), ALU.subtract)
                    last.then_inc(lot0_low, 1)
            dve_shared(dve, 0)
            for j in range(-1, MAX_TILES + 1):
                if j >= 1:
                    i = j - 1
                    dve.wait_ge(ht_high, i + 1)
                    nc.vector.tensor_tensor(ht_l[:, 0:2], ht_ps[:, 0:2 * P].rearrange("p (k n) -> p k n", k=2),
                                            ht_h[:, 0:2].bitcast(F32), ALU.subtract)
                    nc.vector.tensor_tensor(ht_l[0:FH - 2 * P, 2], ht_ps[0:FH - 2 * P, 2 * P:3 * P],
                                            ht_h[0:FH - 2 * P, 2].bitcast(F32), ALU.subtract).then_inc(ht_low, 1)
                if 0 <= j < MAX_TILES:
                    dve.wait_ge(tile_silu, j + 1)
                    dve.wait_ge(tile_upped, j + 1)
                    if j:
                        dve.wait_ge(hid_turned, j)
                    nc.vector.tensor_tensor(hidden[:], silu_t[:], up_tile[:, 0:FH], ALU.mult).then_inc(tile_hidden, 1)
                if j + 1 < MAX_TILES:
                    i = j + 1
                    dve.wait_ge(xt_high, i + 1)
                    nc.vector.tensor_tensor(xt_l[:], xt_ps.rearrange("p (k n) -> p k n", k=KC), xt_h[:].bitcast(F32),
                                            ALU.subtract).then_inc(xt_low, 1)
            dve_shared(dve, 1)
            final_norm(dve, NC - 1)

        def final_norm(dve, c):
            dve.wait_ge(down_read, 4 * NC + 4 * (c + 1))
            for i in range(TPC):
                nc.vector.bn_stats(stats[:, i], x1[:, TPC * c + i]).then_inc(ln_steps, 1)
            n = LN_STEPS * (NC + c) + 4
            dve.wait_ge(ln_steps, n)
            layernorm(n, NC + c)

        def dve_x1T(dve, s):
            dve.wait_ge(x1T_high, s + 1)
            nc.vector.tensor_tensor(x1T_l[:, :, s * P:(s + 1) * P],
                                    x1T_ps[s % 2].rearrange("p (k n) -> p k n", k=KC),
                                    x1T_h[:, :, s * P:(s + 1) * P].bitcast(F32), ALU.subtract).then_inc(x1T_low, 1)

        def dve_shared(dve, half):
            for c in range(NC):
                b = half * NC + c
                for hc, (h0, hn) in enumerate(HC):
                    n = b * 3 + hc
                    dve.wait_ge(gated, 2 * n + 2)
                    dve.wait_ge(silu_done, n + 1)
                    nc.vector.tensor_tensor(silu[0:hn, n % 2], silu[0:hn, n % 2], scores[0:hn, 1, n % 2, :], ALU.mult).then_inc(product_done, 1)
                    dve.wait_ge(product_done, n + 1)
                    dve.wait_ge(hid_high, n + 1)
                    nc.vector.tensor_tensor(hid_l[0:hn, hc], silu[0:hn, n % 2], hid_h[0:hn, hc].bitcast(F32), ALU.subtract).then_inc(hid_low, 1)
                    if half == 0 and n < 2:
                        for s in range(NT - TPC + 2 * n, NT - TPC + 2 * n + 2):
                            dve_x1T(dve, s)
                    for part, at_ in enumerate(ROUTER_AT):
                        if half == 0 and n == at_:
                            router(dve, part)
                    if half == 1 and hc == 0 and c:
                        final_norm(dve, c - 1)
                    if half == 1 and hc:
                        for tt in range(2 * hc - 2, 2 * hc):
                            add_extras(dve, 4 * c + tt)
                for tt in range(TPC):
                    n = 4 * b + tt
                    dve.wait_ge(down_done, n + 1)
                    if half == 0:
                        if n >= 2:
                            dve.wait_ge(half_stored[n % 2], 16 * (n // 2))
                        nc.vector.tensor_copy(stage[:, n % 2], bank[n % 2][:]).then_inc(down_read, 1)
                    else:
                        t = n - NT
                        nc.vector.tensor_tensor(x1[:, t], bank[n % 2][:], x1[:, t], ALU.add).then_inc(down_read, 1)

        def add_extras(dve, t):
            dve.wait_ge(gathered[t % 4], 32 * (t // 4 + 1))
            dve.wait_ge(half_added, t + 1)
            for k in range(TOPK):
                nc.vector.scalar_tensor_tensor(x1[:, t], extra[:, t % 4, 1 + k], weight[:, k, t:t + 1], x1[:, t],
                                               ALU.mult, ALU.add).then_inc(extras_added, 1)
                dve.wait_ge(extras_added, TOPK * t + k + 1)

        ROUTER_AT = [2, 2, 3, 4]
        COUNT_AT = 3
        PLACE_STEPS = 37
        R_STEPS = 53
        step = [0]

        def done(inst):
            inst.then_inc(router_steps, 1)
            step[0] += 1
            nc.vector.wait_ge(router_steps, step[0])

        def router(dve, part):
            ve = nc.vector
            wide = [P, NT, E]
            if part == 0:
                dve.wait_ge(logits_done, NT)
                done(ve.tensor_copy(logits[:], logits_ps[:, 0:NT * E].rearrange("p (t e) -> p t e", e=E)))
                done(ve.tensor_reduce(row_max[:], logits[:], AX, ALU.max))
                done(ve.tensor_tensor(shares[:], logits[:], row_max[:].unsqueeze(2).broadcast_to(wide), ALU.subtract))
                for t in range(NT):
                    top = ve.max(top_values[:, t], logits[:, t])
                done(top)
            elif part == 1:
                for t in range(NT):
                    top = ve.max_index(top_index[:, t], top_values[:, t], logits[:, t])
                done(top)
                done(ve.tensor_copy(top_float[:], top_index[:, :, 0:TOPK]))
                dve.wait_ge(numbers_loaded, 16)
                for k in range(TOPK):
                    done(ve.tensor_tensor(chosen[:, k], tile_numbers[:, 0:E].unsqueeze(1).broadcast_to(wide),
                                          top_float[:, :, k:k + 1].broadcast_to(wide), ALU.is_equal))
                done(ve.tensor_tensor(chosen_b[:], chosen[:, 0], chosen[:, 1], ALU.add))
                assert step[0] == CHOSEN_STEPS
            elif part == 2:
                dve.wait_ge(counted, 1)
                done(ve.tensor_copy(total[:], counts_ps[:, NT * E:2 * NT * E].rearrange("p (t e) -> p t e", e=E)))
                src = total[:]
                for n, far in enumerate((1, 2, 4, 8)):
                    to = before[:, n % 2]
                    done(ve.tensor_copy(to[:, 0:far], src[:, 0:far]))
                    done(ve.tensor_tensor(to[:, far:NT], src[:, far:NT], src[:, 0:NT - far], ALU.add))
                    src = to
                done(ve.tensor_tensor(before[:, 0], before[:, 1], total[:], ALU.subtract))
                done(ve.tensor_scalar(tiles_of[:], before[:, 1, NT - 1], P - 1.0, None, ALU.add))
                done(ve.tensor_copy(tiles_int[:], tiles_of[:]))
                done(ve.tensor_scalar(tiles_int[:], tiles_int[:], 7, None, ALU.arith_shift_right))
                done(ve.tensor_copy(tiles_of[:], tiles_int[:]))
                src = tiles_of[:]
                for n, far in enumerate((1, 2, 4)):
                    to = tile_end[:, n % 2]
                    done(ve.tensor_copy(to[:, 0:far], src[:, 0:far]))
                    done(ve.tensor_tensor(to[:, far:E], src[:, far:E], src[:, 0:E - far], ALU.add))
                    src = to
                done(ve.tensor_tensor(tile_start[:], src, tiles_of[:], ALU.subtract))
                done(ve.scalar_tensor_tensor(place[:], tile_start[:].unsqueeze(1).broadcast_to(wide), float(P), before[:, 0], ALU.mult, ALU.add))
                done(ve.tensor_tensor(place[:], place[:], counts_ps[:, 0:NT * E].rearrange("p (t e) -> p t e", e=E), ALU.add))
                for k in range(TOPK):
                    done(ve.tensor_tensor(product[:], chosen[:, k], place[:], ALU.mult))
                    done(ve.tensor_reduce(place_float[:, k], product[:], AX, ALU.add))
                done(ve.tensor_copy(place_int[:], place_float[:]))
                assert step[0] == PLACE_STEPS, step[0]
            else:
                dve.wait_ge(router_exp, 1)
                done(ve.tensor_reduce(row_sum[:], shares[:], AX, ALU.add))
                done(ve.reciprocal(row_sum[:], row_sum[:]))
                for k in range(TOPK):
                    done(ve.tensor_tensor(product[:], chosen[:, k], shares[:], ALU.mult))
                    done(ve.tensor_reduce(weight[:, k], product[:], AX, ALU.add))
                    done(ve.tensor_tensor(weight[:, k], weight[:, k], row_sum[:], ALU.mult))
                done(ve.tensor_scalar(tile_start[:], tile_start[:], 1.0, None, ALU.add))
                done(ve.tensor_copy(start_int[:], tile_start[:]))
                shape = [P, MAX_TILES, E - 1]
                done(ve.tensor_tensor(ended[:], tile_end[:, 0, 0:E - 1].unsqueeze(1).broadcast_to(shape),
                                      tile_numbers[:].unsqueeze(2).broadcast_to(shape), ALU.is_le))
                done(ve.tensor_reduce(tile_expert[:], ended[:], AX, ALU.add))
                done(ve.tensor_copy(tile_slot[:], tile_expert[:]))
                done(ve.tensor_scalar(tile_slot[:], tile_slot[:], 1, None, ALU.bitwise_and))
                done(ve.tensor_scalar(tile_expert[:], tile_expert[:], 1.0, float(PIECES), ALU.add, ALU.mult))
                done(ve.tensor_copy(tile_needs[:], tile_expert[:]))
                assert step[0] == R_STEPS, step[0]

        def split_piece(pool, lot, piece):
            m = PIECES * (lot - 1) + piece
            pool.wait_ge(ffn_loaded[piece], (16 if piece < 2 else 32) * (lot + 1))
            areas = areas_of(lot, piece)
            for src, (high, low) in areas:
                one = ones[0:src.shape[0], 0:1].broadcast_to(list(src.shape))
                last = nc.gpsimd.tensor_tensor(high, src, one, ALU.mult)
            last.then_inc(ffn_high, 1)
            pool.wait_ge(ffn_high, m + 1)
            for src, (high, low) in areas:
                last = nc.gpsimd.tensor_tensor(low, src, high.bitcast(F32), ALU.subtract)
            last.then_inc(ffn_low, 1)

        def pool_split_wo(pool):
            pool.wait_ge(wo_loaded, 32)
            nc.gpsimd.tensor_tensor(wo_h[:], wo_raw[:], ones[:, 0:1].unsqueeze(2).broadcast_to([P, NG, D]), ALU.mult).then_inc(wo_high, 1)
            nc.gpsimd.tensor_tensor(gw_h[:], gw_raw[:], ones[:, 0:1].unsqueeze(2).broadcast_to([P, KC, E]), ALU.mult).then_inc(wo_high, 1)
            pool.wait_ge(wo_high, 2)
            nc.gpsimd.tensor_tensor(wo_l[:], wo_raw[:], wo_h[:].bitcast(F32), ALU.subtract).then_inc(wo_low, 1)
            nc.gpsimd.tensor_tensor(gw_l[:], gw_raw[:], gw_h[:].bitcast(F32), ALU.subtract).then_inc(wo_low, 1)

        def tail_gpsimd(pool):
            for t in range(NT):
                pool.wait_ge(y_high, t + 1)
                if t >= 2:
                    pool.wait_ge(projected, t - 1)
                nc.gpsimd.tensor_tensor(y_l[:, t % 2], y_of(t), y_h[:, t % 2].bitcast(F32), ALU.subtract).then_inc(y_low, 1)
            pool.wait_ge(x1_ready, NT)
            pool.wait_ge(logits_done, NT)
            for piece in range(2):
                split_piece(pool, 1, piece)
            pool.wait_ge(router_steps, PLACE_STEPS)
            pool.wait_ge(zero_filled, 16)
            for t in range(NT):
                for k in range(TOPK):
                    nc.gpsimd.indirect_dma_start(out=xs_dram, out_offset=bass.IndirectOffsetOnAxis(ap=place_int[:, k, t:t + 1], axis=0),
                                                 in_=x1[:, t], in_offset=None).then_inc(scattered, 16)
            split_piece(pool, 1, 2)
            pool.wait_ge(router_steps, R_STEPS)
            pool.wait_ge(down_done, NT)
            for lot in range(2, LOTS):
                if lot >= 3:
                    pool.wait_ge(tile_done, pool.value_load(start_int[0:1, lot - 2:lot - 1], min_val=0, max_val=MAX_TILES))
                for piece in range(PIECES):
                    split_piece(pool, lot, piece)
            pool.wait_ge(tile_done, MAX_TILES + 1)
            for i in range(2):
                pool.wait_ge(ys_stored[i], 16 * ((MAX_TILES + 1 - i) // 2))
            for t in range(NT):
                if t >= 4:
                    pool.wait_ge(extras_added, TOPK * (t - 3))
                for k in range(TOPK):
                    nc.gpsimd.indirect_dma_start(out=extra[:, t % 4, 1 + k], out_offset=None, in_=ys_dram,
                                                 in_offset=bass.IndirectOffsetOnAxis(ap=place_int[:, k, t:t + 1], axis=0)).then_inc(gathered[t % 4], 16)
                pool.wait_ge(half_loaded[t % 4], 16 * (t // 4 + 1))
                nc.gpsimd.tensor_tensor(x1[:, t], x1[:, t], extra[:, t % 4, 0], ALU.add).then_inc(half_added, 1)

        x_rows = x.rearrange("b s d -> (b s) d")
        block = ctx.enter_context(nc.Block())

        def added(g, slot):
            return (SLOTS - len(DIRECT)) * g + sum(n not in DIRECT for n in range(slot + 1))

        def load_w(sp, g):
            for part in range(3):
                col = part * D + g * P
                sp.dma_start(wqkv_raw[:, :, part * P:(part + 1) * P],
                             w_qkv.rearrange("(k p) n -> p k n", p=P)[:, :, col:col + P]).then_inc(w_loaded, 16)

        @block.sync
        def _(sp):
            for t in range(NT):
                if t >= 4:
                    sp.wait_ge(x_turned, t - 3)
                sp.dma_start(x_in[:, t % 4, :], x_rows[t * P:(t + 1) * P, :]).then_inc(x_loaded[t % 4], 16)
                if t == 3:
                    load_w(sp, 0)
                    sp.dma_start(tile_numbers[:], numbers.rearrange("(a h) -> a h", a=1).broadcast_to([P, MAX_TILES])).then_inc(numbers_loaded, 16)
                    for to, of in ((cos, rope_cos), (sin, rope_sin)):
                        for c in range(NC):
                            sp.dma_start(to[:, c], of[c * CH:(c + 1) * CH, :].rearrange("(t p) f -> p t f", p=P)).then_inc(tables_loaded, 16)
                    sp.dma_start(gain[:], q_gain.rearrange("(a h) -> a h", a=1).broadcast_to([P, HEADS])).then_inc(tables_loaded, 16)
            sp.wait_ge(zero_made, 1)
            sp.dma_start(xs_dram.rearrange("(j p) d -> p j d", p=P), zeros[:].unsqueeze(1).broadcast_to([P, MAX_TILES, D])).then_inc(zero_filled, 16)
            for g in range(NG):
                for i in range(NC):
                    if i == 2:
                        sp.wait_ge(split_high, 4 * g + 4)
                        sp.wait_ge(split_low, 2 * (4 * g + 4))
                        if g + 1 < NG:
                            load_w(sp, g + 1)
                        else:
                            sp.dma_start(wo_raw[:], w_out.rearrange("(g p) n -> p g n", p=P)).then_inc(wo_loaded, 16)
                            sp.dma_start(gw_raw[:], gate_w.rearrange("(k p) n -> p k n", p=P)).then_inc(wo_loaded, 16)
                            sp.wait_ge(y_stored[0], 16 * (NC * g + i) // 2)
                            for t in range(TPC):
                                load_y(sp, t)
                    step = NC * g + i
                    sp.wait_ge(y_ready, step + 1)
                    sp.dma_start(y_dram[g, :, i * CH:(i + 1) * CH], y_norm[:, step % 2, :]).then_inc(y_stored[step % 2], 16)
            tail_sync(sp)

        def pe_project(g, c, tt):
            n = 4 * (NC * g + c) + tt
            if tt == 0 and c == 0:
                nc.tensor.wait_ge(w_high, g + 1)
                nc.tensor.wait_ge(w_low, g + 1)
            if n >= 1:
                nc.tensor.wait_ge(qkv_copied, n)
            tok = slice((TPC * c + tt) * P, (TPC * c + tt + 1) * P)
            parts = [(xT_h, wqkv_h), (xT_h, wqkv_l), (xT_l, wqkv_h)]
            for m, (xs, ws) in enumerate(parts):
                for k in range(KC):
                    mm = nc.tensor.matmul(qkv_ps[:, 0:3 * P], xs[:, k, tok], ws[:, k, :],
                                          start=(m == 0 and k == 0), stop=(m == 2 and k == KC - 1))
            mm.then_inc(qkv_done, 1)

        def pe_turn(g, c, h, which):
            C = NC * g + c
            if h == 0 and which:
                nc.tensor.wait_ge(split_high, C + 1)
                nc.tensor.wait_ge(split_low, 2 * (C + 1))
            if not which:
                nc.tensor.wait_ge(k_ready, 4 * C + h + 1)
            elif 4 * C + h > 0:
                nc.tensor.wait_ge(q_ready, 4 * C + h)
            for tt in range(TPC):
                mm = nc.tensor.matmul(turn_ps[0:3 * HD, tt * P:(tt + 1) * P],
                                      split[:, which, tt, h, :, :].rearrange("p s d -> p (s d)"), ident_r[:],
                                      start=True, stop=True)
            mm.then_inc(turned, 1)

        def pe_scores(g, slot):
            i, j = step_of(slot)
            n = SLOTS * g + slot
            if j == 0:
                nc.tensor.wait_ge(q_ready, 4 * (NC * g + i + 1))
                nc.tensor.wait_ge(k_ready, 4 * (NC * g + i + 1))
            lo = max(0, (j - TPC * i) * P)
            for p in range(2):
                if n >= 1:
                    nc.tensor.wait_ge(exp_done, 2 * n + p - 1)
                for hh in range(2):
                    h = 2 * p + hh
                    diagonal = j >= TPC * i
                    mm = nc.tensor.matmul(scores[:, p, hh, lo:CH], k_stack[0:3 * HD, h, j * P:(j + 1) * P],
                                          q_stack[0:3 * HD, i % 2, h, lo:CH], start=True, stop=not diagonal)
                    if diagonal:
                        mm = nc.tensor.matmul(scores[:, p, hh, lo:lo + P], ident_b[:], mask_b[:],
                                              start=False, stop=True)
                mm.then_inc(scores_ready, 1)

        def pe_values(g, slot):
            i, j = step_of(slot)
            n, step = SLOTS * g + slot, NC * g + i
            if i >= 2 and slot == STEP_AT[i + 1] - 1:
                pe_sums(g, i)
            nc.tensor.wait_ge(exp_done, 2 * n + 2)
            if j == 0 and step >= 1:
                nc.tensor.wait_ge(y_copied, step)
            lo = max(0, (j - TPC * i) * P)
            last = TPC * (i + 1) - 1
            if slot in DIRECT:
                first = min(DIRECT & set(range(STEP_AT[i], STEP_AT[i + 1]))) == slot
                if first and step >= 1:
                    nc.tensor.wait_ge(sums_read, step)
                for h in range(HG):
                    nc.tensor.matmul(sums_ps[HD * h:HD * (h + 1), lo:CH], ones[:], probs[:, n % 4, h, lo:CH],
                                     start=first, stop=(j == last))
            for h in range(HG):
                mm = nc.tensor.matmul(y_ps[HD * h:HD * (h + 1), lo:CH],
                                      v_sb[:, j, HD * h:HD * (h + 1)], probs[:, n % 4, h, lo:CH],
                                      start=(j == 0), stop=(j == last))
            mm.then_inc(pv_done, 1)

        def pe_sums(g, i):
            nc.tensor.wait_ge(sum_dve, added(g, STEP_AT[i + 1] - 1))
            nc.tensor.wait_ge(sum_pool, added(g, STEP_AT[i + 1] - 1))
            for h in range(HG):
                mm = nc.tensor.matmul(sums_ps[HD * h:HD * (h + 1), :], ones[:], key_sum[:, h, :], start=False, stop=False)
            mm.then_inc(sums_done, 1)

        @block.tensor
        def _(pe):
            pe.wait_ge(consts_ready, 1)
            for t in range(NT):
                pe.wait_ge(x_loaded[t % 4], 16 * (t // 4 + 1))
                if t >= 4:
                    pe.wait_ge(xT_low, t - 3)
                for k in range(KC):
                    mm = nc.tensor.transpose(scores[:, (t % 4) // 2, t % 2, k * P:(k + 1) * P],
                                             x_in[:, t % 4, k * P:(k + 1) * P], ident[:])
                mm.then_inc(x_turned, 1)
                if t == TPC + 1:
                    pe.wait_ge(xT_low, TPC)
                    pe.wait_ge(xT_high, TPC)
                    pe.wait_ge(ident_ready, 1)
                    for tt in range(TPC):
                        pe_project(0, 0, tt)
            pe.wait_ge(xT_low, NT)
            pe.wait_ge(xT_high, NT)
            for h in range(HG):
                pe_turn(0, 0, h, 1)
                pe_turn(0, 0, h, 0)
                pe_project(0, 1, h)
            for g in range(NG):
                for slot in range(SLOTS):
                    pe_scores(g, slot)
                    for work in work_at(PROJECT_AT, slot, g):
                        pe_project(*work)
                    turns = list(work_at(TURN_AT, slot, g))
                    for n, work in enumerate(turns):
                        pe_turn(*work, 1)
                        if n + 1 < len(turns):
                            pe_turn(*work, 0)
                    if slot or g:
                        pe_values(g if slot else g - 1, (slot - 1) % SLOTS)
                    for work in turns[-1:]:
                        pe_turn(*work, 0)
            pe_values(NG - 1, SLOTS - 1)
            tail_tensor(pe)

        def act_copy_qkv(g, c, tt):
            C = NC * g + c
            n = 4 * C + tt
            nc.scalar.wait_ge(qkv_done, n + 1)
            if tt == 0 and C >= 1:
                nc.scalar.wait_ge(split_high, C)
                nc.scalar.wait_ge(split_low, 2 * C)
            if tt == 0 and c == 0:
                nc.scalar.wait_ge(w_high, g + 1)
                nc.scalar.wait_ge(w_low, g + 1)
            rows = qkv_ps[:, 0:2 * P].rearrange("p (w h d) -> p w h d", w=2, h=HG)
            nc.scalar.copy(qk[:, :, tt], rows)
            if tt == 0 and C >= 1:
                nc.scalar.wait_ge(q_roped, 2 * C)
                nc.scalar.wait_ge(k_roped, 2 * C)
            nc.scalar.activation(squares[:, :, tt], rows, ACT.Square)
            if g >= 1:
                nc.scalar.wait_ge(pv_done, SLOTS * (g - 1) + STEP_AT[3] + 4 * c + tt + 1)
            nc.scalar.copy(v_sb[:, TPC * c + tt, :], qkv_ps[:, 2 * P:3 * P]).then_inc(qkv_copied, 1)

        def act_copy_q(g, c, h):
            C = NC * g + c
            nc.scalar.wait_ge(turned, 8 * C + 2 * h + 2)
            if C >= 2 and h == 0:
                nc.scalar.wait_ge(scores_ready, 2 * (SLOTS * ((C - 2) // 4) + STEP_AT[(C - 2) % 4 + 1]))
            nc.scalar.copy(q_stack[0:3 * HD, c % 2, h, :], turn_ps[0:3 * HD, :]).then_inc(q_ready, 1)

        def act_copy_y(g, i):
            step = NC * g + i
            nc.scalar.wait_ge(pv_done, SLOTS * g + STEP_AT[i + 1])
            if step >= 2:
                nc.scalar.wait_ge(y_stored[step % 2], 16 * (step // 2))
            nc.scalar.copy(y_norm[:, step % 2, :], y_ps[:]).then_inc(y_copied, 1)

        def act_exp(g, slot):
            i, j = step_of(slot)
            n = SLOTS * g + slot
            lo = max(0, (j - TPC * i) * P)
            if n == 3:
                nc.scalar.wait_ge(zero_filled, 16)
            if n == 0:
                nc.scalar.wait_ge(shift_steps, 5)
                nc.scalar.wait_ge(x_turned, NT)
            if n >= 4:
                nc.scalar.wait_ge(pv_done, n - 3)
                before = added((n - 4) // SLOTS, (n - 4) % SLOTS)
                if before:
                    nc.scalar.wait_ge(sum_dve, before)
                    nc.scalar.wait_ge(sum_pool, before)
            for p in range(2):
                nc.scalar.wait_ge(scores_ready, 2 * n + p + 1)
                nc.scalar.activation(probs[:, n % 4, 2 * p:2 * p + 2, lo:CH], scores[:, p, :, lo:CH], ACT.Exp,
                                     bias=shift[:, 2 * g + p:2 * g + p + 1]).then_inc(exp_done, 1)

        @block.scalar
        def _(act):
            for t in range(NT):
                act.wait_ge(x_turned, t + 1)
                nc.scalar.copy(xT_h[:, :, t * P:(t + 1) * P],
                               scores[:, (t % 4) // 2, t % 2, :].rearrange("p (k n) -> p k n", k=KC)).then_inc(xT_high, 1)
                if t == TPC + 1:
                    for tt in range(TPC):
                        act_copy_qkv(0, 0, tt)
            for h in range(HG):
                act_copy_q(0, 0, h)
                act_copy_qkv(0, 1, h)
            for g in range(NG):
                for slot in range(SLOTS):
                    act_exp(g, slot)
                    if slot in STEP_AT and (slot or g):
                        i = STEP_AT.index(slot)
                        act_copy_y(g if i else g - 1, (i - 1) % NC)
                    for work in work_at(PROJECT_AT, slot, g):
                        act_copy_qkv(*work)
                    for work in work_at(TURN_AT, slot, g):
                        act_copy_q(*work)
            act_copy_y(NG - 1, NC - 1)
            tail_scalar(act)

        def dve_split_w(g):
            nc.vector.wait_ge(w_loaded, 48 * (g + 1))
            if g:
                nc.vector.wait_ge(qkv_done, 16 * g)
            nc.vector.tensor_copy(wqkv_h[:], wqkv_raw[:]).then_inc(w_high, 1)

        def dve_rsqrt(out, work, arg, ready, steps):
            n = steps
            for do in range(2):
                if do == 0:
                    nc.vector.tensor_scalar(out.bitcast(I32), arg.bitcast(I32), 1, None, ALU.arith_shift_right).then_inc(ready, 1)
                else:
                    nc.vector.tensor_scalar(out.bitcast(I32), out.bitcast(I32), -1.0, RSQRT_GUESS, ALU.mult, ALU.add).then_inc(ready, 1)
                n += 1
                nc.vector.wait_ge(ready, n)
            for _ in range(3):
                nc.vector.scalar_tensor_tensor(work, out, -0.5, out, ALU.mult, ALU.mult).then_inc(ready, 1)
                nc.vector.wait_ge(ready, n + 1)
                nc.vector.tensor_tensor(work, work, arg, ALU.mult).then_inc(ready, 1)
                nc.vector.wait_ge(ready, n + 2)
                nc.vector.scalar_tensor_tensor(out, work, 1.5, out, ALU.add, ALU.mult).then_inc(ready, 1)
                nc.vector.wait_ge(ready, n + 3)
                n += 3

        def dve_norms(g, c):
            C = NC * g + c
            nc.vector.wait_ge(qkv_copied, 4 * (C + 1))
            nc.vector.tensor_reduce(sq_sum[:], squares[:], AX, ALU.add).then_inc(norm_steps, 1)
            nc.vector.wait_ge(norm_steps, 13 * C + 1)
            nc.vector.tensor_scalar(sq_sum[:], sq_sum[:], UNIT_EPS, None, ALU.add).then_inc(norm_steps, 1)
            nc.vector.wait_ge(norm_steps, 13 * C + 2)
            if C:
                nc.vector.wait_ge(normed, C)
            dve_rsqrt(inv_norm[:], newton[:], sq_sum[:], norm_steps, 13 * C + 2)
            nc.vector.tensor_tensor(inv_norm[:, 0], inv_norm[:, 0],
                                    gain[:, HG * g:HG * (g + 1)].unsqueeze(1).broadcast_to([P, TPC, HG]),
                                    ALU.mult).then_inc(inv_normed, 1)
            nc.vector.wait_ge(inv_normed, C + 1)
            rows = qk[:].rearrange("p w t h d -> p (w t h) d")
            nc.vector.tensor_tensor(rows, rows, inv_norm[:].rearrange("p w t h -> p (w t h)").unsqueeze(2)
                                    .broadcast_to([P, 2 * TPC * HG, HD]), ALU.mult).then_inc(normed, 1)
            rotate(nc.vector, 0, C, c, q_products, q_roped)

        def rotate(engine, which, C, c, products, done):
            half, shape = HD // 2, [P, TPC, HG // 2, HD // 2]
            even, prod = qk[:, which, :, 0::2, :], rope_prod[:, which]
            first, second = even[:, :, :, 0:half], even[:, :, :, half:HD]
            cs, sn = [table[:, c].unsqueeze(2).broadcast_to(shape) for table in (cos, sin)]
            engine.wait_ge(normed, C + 1)
            engine.tensor_tensor(prod[:, 0], first, cs, ALU.mult)
            engine.tensor_tensor(prod[:, 1], second, sn, ALU.mult)
            engine.tensor_tensor(prod[:, 2], first, sn, ALU.mult)
            engine.tensor_tensor(prod[:, 3], second, cs, ALU.mult).then_inc(products, 1)
            engine.wait_ge(products, C + 1)
            engine.tensor_tensor(first, prod[:, 0], prod[:, 1], ALU.subtract).then_inc(done, 1)
            engine.tensor_tensor(second, prod[:, 2], prod[:, 3], ALU.add).then_inc(done, 1)

        def dve_split(g, c):
            C = NC * g + c
            nc.vector.wait_ge(q_roped, 2 * (C + 1))
            nc.vector.wait_ge(k_roped, 2 * (C + 1))
            if C:
                nc.vector.wait_ge(turned, 8 * C)
            rows = [qk[:, w].rearrange("p t h d -> p (t h) d") for w in range(2)]
            parts = [split[:, w].rearrange("p t h s d -> p (t h) s d") for w in range(2)]
            twice = [r.unsqueeze(2).broadcast_to([P, TPC * HG, 2, HD]) for r in rows]
            nc.vector.tensor_copy(parts[0][:, :, 0:2, :], twice[0])
            nc.vector.tensor_copy(parts[1][:, :, 0::2, :], twice[1]).then_inc(split_high, 1)
            nc.vector.wait_ge(split_high, C + 1)
            for w, low in ((0, 2), (1, 1)):
                nc.vector.tensor_tensor(parts[w][:, :, low, :], rows[w], parts[w][:, :, 0, :].bitcast(F32),
                                        ALU.subtract).then_inc(split_low, 1)

        def dve_copy_k(g, c, h):
            C = NC * g + c
            nc.vector.wait_ge(turned, 8 * C + 2 * h + 1)
            if g and h == 0:
                nc.vector.wait_ge(scores_ready, 2 * (SLOTS * (g - 1) + STEP_AT[3] + TPC * (c + 1)))
            nc.vector.tensor_copy(k_stack[0:3 * HD, h, c * CH:(c + 1) * CH], turn_ps[0:3 * HD, :]).then_inc(k_ready, 1)

        def dve_add_keys(g, slot):
            i, j = step_of(slot)
            n = SLOTS * g + slot
            lo = max(0, (j - TPC * i) * P)
            nc.vector.wait_ge(exp_done, 2 * n + 2)
            if added(g, slot) > 1:
                nc.vector.wait_ge(sum_dve, added(g, slot) - 1)
            if j == 0:
                if 2 * g + i > 2:
                    nc.vector.wait_ge(sums_done, 2 * g + i - 2)
                nc.vector.tensor_copy(key_sum[:, 0:3, :], probs[:, n % 4, 0:3, :]).then_inc(sum_dve, 1)
            else:
                nc.vector.tensor_tensor(key_sum[:, 0:3, lo:CH], key_sum[:, 0:3, lo:CH], probs[:, n % 4, 0:3, lo:CH],
                                        ALU.add).then_inc(sum_dve, 1)

        def dve_outputs(g, i):
            step = NC * g + i
            nc.vector.wait_ge(pv_done, SLOTS * g + STEP_AT[i + 1])
            if step:
                nc.vector.wait_ge(y_ready, step)
            nc.vector.transpose(inv_sum[:], sums_ps[:]).then_inc(sums_read, 1)
            nc.vector.wait_ge(sums_read, step + 1)
            nc.vector.reciprocal(inv_col[:], inv_sum[:].rearrange("p (b n) -> p b n", n=32)[:, :, 0]).then_inc(sums_inverted, 1)
            nc.vector.wait_ge(sums_inverted, 2 * step + 1)
            nc.vector.transpose(inv_sum[:], inv_col[:].unsqueeze(2).broadcast_to([P, CH // 32, 32])).then_inc(sums_inverted, 1)
            nc.vector.wait_ge(sums_inverted, 2 * step + 2)
            nc.vector.wait_ge(y_copied, step + 1)
            nc.vector.tensor_tensor(y_norm[:, step % 2, :], y_norm[:, step % 2, :], inv_sum[:], ALU.mult).then_inc(y_ready, 1)

        @block.vector
        def _(dve):
            dve.wait_ge(consts_ready, 1)
            nc.vector.tensor_copy(ident_r[:], ident[:]).then_inc(ident_ready, 1)
            dve.wait_ge(tables_loaded, 16 * (2 * NC + 1))
            nc.vector.tensor_scalar(gain_abs[:], gain[:], -1.0, None, ALU.mult).then_inc(shift_steps, 1)
            dve.wait_ge(shift_steps, 1)
            nc.vector.tensor_tensor(gain_abs[:], gain_abs[:], gain[:], ALU.max).then_inc(shift_steps, 1)
            dve.wait_ge(shift_steps, 2)
            pairs = gain_abs[:].rearrange("p (a b) -> p a b", b=2)
            nc.vector.tensor_tensor(shift[:], pairs[:, :, 0], pairs[:, :, 1], ALU.max).then_inc(shift_steps, 1)
            dve.wait_ge(shift_steps, 3)
            nc.vector.tensor_scalar(shift[:], shift[:], EXP_SAFE, 0.0, ALU.subtract, ALU.max).then_inc(shift_steps, 1)
            dve.wait_ge(shift_steps, 4)
            nc.vector.tensor_scalar(shift[:], shift[:], -1.0, None, ALU.mult).then_inc(shift_steps, 1)
            for t in range(NT):
                dve.wait_ge(xT_high, t + 1)
                nc.vector.tensor_tensor(xT_l[:, :, t * P:(t + 1) * P],
                                        scores[:, (t % 4) // 2, t % 2, :].rearrange("p (k n) -> p k n", k=KC),
                                        xT_h[:, :, t * P:(t + 1) * P].bitcast(F32), ALU.subtract).then_inc(xT_low, 1)
                if t == 3:
                    dve_split_w(0)
                if t == 2 * TPC + 1:
                    dve_norms(0, 0)
                if t == NT - 1:
                    dve_split(0, 0)
            for h in range(HG):
                dve_copy_k(0, 0, h)
            dve_norms(0, 1)
            dve_split(0, 1)
            for g in range(NG):
                for slot in range(SLOTS):
                    for work in work_at(TURN_AT, slot, g):
                        dve_copy_k(*work)
                    if slot in STEP_AT and (slot or g):
                        i = STEP_AT.index(slot)
                        dve_outputs(g if i else g - 1, (i - 1) % NC)
                    if slot not in DIRECT:
                        dve_add_keys(g, slot)
                    for gg, c, stage in work_at(NORMALISE_AT, slot, g):
                        if stage == 0:
                            dve_norms(gg, c)
                        if stage == 2:
                            dve_split(gg, c)
                    if slot == SPLIT_W_AT and g + 1 < NG:
                        dve_split_w(g + 1)
            dve_outputs(NG - 1, NC - 1)
            tail_vector(dve)

        def pool_split_w(g):
            nc.gpsimd.wait_ge(w_high, g + 1)
            nc.gpsimd.tensor_tensor(wqkv_l[:], wqkv_raw[:], wqkv_h[:].bitcast(F32), ALU.subtract).then_inc(w_low, 1)

        def pool_rotate(g, c):
            rotate(nc.gpsimd, 1, NC * g + c, c, k_products, k_roped)

        def pool_add_keys(g, slot):
            i, j = step_of(slot)
            n = SLOTS * g + slot
            lo = max(0, (j - TPC * i) * P)
            nc.gpsimd.wait_ge(exp_done, 2 * n + 2)
            if added(g, slot) > 1:
                nc.gpsimd.wait_ge(sum_pool, added(g, slot) - 1)
            if j == 0 and 2 * g + i > 2:
                nc.gpsimd.wait_ge(sums_done, 2 * g + i - 2)
            new = probs[:, n % 4, 3, lo:CH]
            if j == 0:
                nc.gpsimd.tensor_tensor(key_sum[:, 3, :], new, ones[:, 0:1].broadcast_to([P, CH]), ALU.mult).then_inc(sum_pool, 1)
            else:
                nc.gpsimd.tensor_tensor(key_sum[:, 3, lo:CH], key_sum[:, 3, lo:CH], new, ALU.add).then_inc(sum_pool, 1)

        @block.gpsimd
        def _(pool):
            nc.gpsimd.memset(zeros[:], 0.0).then_inc(zero_made, 1)
            nc.gpsimd.memset(ones_b[:], 1.0)
            nc.gpsimd.memset(ident[:], 0.0)
            nc.gpsimd.memset(mask_b[:], 0.0)
            nc.gpsimd.memset(ident_b[:], 0.0)
            nc.gpsimd.memset(ones[:], 1.0).then_inc(mask_filled, 1)
            pool.wait_ge(mask_filled, 1)
            for m in (ident_b, ident):
                nc.gpsimd.affine_select(out=m[:], in_=m[:], compare_op=ALU.not_equal, fill=1.0, base=0,
                                        pattern=[[-1, P]], channel_multiplier=1)
            nc.gpsimd.affine_select(out=tri_b[:], in_=ones_b[:], compare_op=ALU.is_gt, fill=0.0, base=0,
                                    pattern=[[1, P]], channel_multiplier=-1).then_inc(tables_made, 1)
            nc.gpsimd.affine_select(out=mask_b[:], in_=mask_b[:], compare_op=ALU.is_ge, fill=MASKED, base=0,
                                    pattern=[[1, P]], channel_multiplier=-1).then_inc(consts_ready, 1)
            pool.wait_ge(tables_loaded, 16 * (2 * NC + 1))
            pool_split_w(0)
            for c in range(2):
                pool_rotate(0, c)
            for g in range(NG):
                for slot in range(SLOTS):
                    if slot not in DIRECT:
                        pool_add_keys(g, slot)
                    for gg, c, stage in work_at(NORMALISE_AT, slot, g):
                        if stage == 1:
                            pool_rotate(gg, c)
                    if slot == SPLIT_W_AT and g + 1 < NG:
                        pool_split_w(g + 1)
                    if slot == SPLIT_WO_AT and g + 1 == NG:
                        pool_split_wo(pool)
            tail_gpsimd(pool)


def kernel(L0_attn_x, L0_attn_w_qkv, L0_attn_w_out, L0_attn_q_gain, L0_ffn_gate_w, L0_ffn_w_gate, L0_ffn_w_up,
           L0_ffn_w_down, L0_ffn_sw_gate, L0_ffn_sw_up, L0_ffn_sw_down):
    import concourse.bacc as bacc
    from concourse.bass_utils import run_bass_kernel_spmd

    half = HD // 2
    inv_freq = np.float32(10000.0) ** (-np.arange(half, dtype=np.float32) / np.float32(half))
    theta = np.arange(T, dtype=np.float32)[:, None] * inv_freq.astype(np.float32)[None, :]
    arrays = dict(x=L0_attn_x, w_qkv=L0_attn_w_qkv, w_out=L0_attn_w_out, q_gain=L0_attn_q_gain,
                  gate_w=L0_ffn_gate_w, w_gate=L0_ffn_w_gate, w_up=L0_ffn_w_up, w_down=L0_ffn_w_down,
                  sw_gate=L0_ffn_sw_gate, sw_up=L0_ffn_sw_up, sw_down=L0_ffn_sw_down,
                  rope_cos=np.cos(theta), rope_sin=np.sin(theta), numbers=np.arange(MAX_TILES, dtype=np.float32))
    arrays = {name: np.ascontiguousarray(a) for name, a in arrays.items()}
    nc = bacc.Bacc("TRN2", target_bir_lowering=False, num_devices=1)
    args = [nc.dram_tensor(name, a.shape, mybir.dt.from_np(a.dtype), kind="ExternalInput").ap()
            for name, a in arrays.items()]
    out = nc.dram_tensor("out", L0_attn_x.shape, F32, kind="ExternalOutput").ap()
    build(nc, *args, out)
    result = run_bass_kernel_spmd(nc, [arrays], core_ids=[0])
    return result.results[0]["out"]
```

```python
from contextlib import ExitStack

import numpy as np

import concourse.bass as bass
import concourse.mybir as mybir

F32 = mybir.dt.float32
F32R = mybir.dt.float32r
BF16 = mybir.dt.bfloat16
I32 = mybir.dt.int32
U32 = mybir.dt.uint32
ALU = mybir.AluOpType
ACT = mybir.ActivationFunctionType
AX = mybir.AxisListType.X

P = 128
T, D = 2048, 512
NT, KC = T // P, D // P
HEADS, HD = 16, 32
HG = 4
NG = HEADS // HG
CH = 512
NC, TPC = T // CH, CH // P
E, TOPK, FH, FS = 8, 2, 352, 704
MAX_TILES = TOPK * T // P + E - 1
UNIT_EPS, LN_EPS = 1e-6, 1e-5
MASKED = -1.0e30
RSQRT_GUESS = float(0x5F3759DF)
EXP_SAFE = 80.0

STEP_AT = [0, 4, 12, 24, 40]
SLOTS = STEP_AT[-1]
PROJECT_AT = {(2, 0): 0, (2, 1): 1, (2, 2): 3, (2, 3): 4,
              (3, 0): 7, (3, 1): 9, (3, 2): 10, (3, 3): 11,
              (0, 0): 25, (0, 1): 26, (0, 2): 27, (0, 3): 28,
              (1, 0): 32, (1, 1): 32, (1, 2): 34, (1, 3): 35}
NORMALISE_AT = {(2, 0): 4, (2, 1): 5, (2, 2): 7,
                (3, 0): 11, (3, 1): 13, (3, 2): 15,
                (0, 0): 29, (0, 1): 30, (0, 2): 30,
                (1, 0): 36, (1, 1): 37, (1, 2): 39}
TURN_AT = {(2, 0): 8, (2, 1): 9, (2, 2): 10, (2, 3): 11,
           (3, 0): 17, (3, 1): 18, (3, 2): 19, (3, 3): 20,
           (0, 0): 32, (0, 1): 33, (0, 2): 34, (0, 3): 35,
           (1, 0): 0, (1, 1): 1, (1, 2): 2, (1, 3): 3}
SPLIT_W_AT = 22
SPLIT_WO_AT = 26
DIRECT = set(range(STEP_AT[1])) | {4, 5, 6, 10, 11, 14, 15, 23, 28, 29, 30, 36, 38, 39}
ADDING = [i for i in range(NC) if any(n not in DIRECT for n in range(STEP_AT[i], STEP_AT[i + 1]))]
NORM_AFTER, SPLIT_AFTER = 7, 11
FIRST_AFTER = 5
LATE_AT = {(False, 2, 1): 0}


def first_added(i):
    return min(n for n in range(STEP_AT[i], STEP_AT[i + 1]) if n not in DIRECT)


def work_at(table, slot, g):
    for (c, part), at in table.items():
        if isinstance(g, int) and g == 0 and c in (1, 2) and at < 4 and table is not NORMALISE_AT:
            at = LATE_AT.get((table is TURN_AT, c, part), at)
        ahead = c < 2 and slot >= STEP_AT[3]
        if at == slot and (not isinstance(g, int) or g + ahead < NG):
            yield g + ahead, c, part


def step_of(slot):
    i = max(n for n in range(NC) if STEP_AT[n] <= slot)
    return i, slot - STEP_AT[i]


def build(nc, x, w_qkv, w_out, q_gain, gate_w, w_gate, w_up, w_down, sw_gate, sw_up, sw_down,
          rope_cos, rope_sin, numbers, out):
    with ExitStack() as ctx:
        def sem(name):
            return ctx.enter_context(nc.semaphore(name))

        BASE = -(-nc.sbuf_base // 32) * 32
        TOP = 229344

        def at(name, offset, shape, dt):
            size = int(np.prod(shape[1:])) * (2 if dt == BF16 else 4)
            assert BASE + offset + size <= TOP, (name, offset, size)
            return nc.alloc_sbuf_tensor_at(name, shape, dt, offset=BASE + offset)

        xT_h = at("xT_h", 0, [P, KC, T], F32R)
        xT_l = at("xT_l", 32768, [P, KC, T], F32R)
        k_stack = at("k_stack", 65536, [P, HG, T], F32R)
        q_stack = at("q_stack", 98304, [P, 2, HG, CH], F32R)
        v_sb = at("v_sb", 114688, [P, NT, P], F32)
        wqkv_h = at("wqkv_h", 122880, [P, KC, 3 * P], F32R)
        wqkv_l = at("wqkv_l", 129024, [P, KC, 3 * P], F32R)
        probs = at("probs", 135168, [P, 4, HG, CH], F32)
        x_in = at("x_in", 135168, [P, 4, D], F32)
        key_sum = at("key_sum", 167936, [P, HG, CH], F32)
        qk = at("qk", 176128, [P, 2, TPC, HG, HD], F32)
        squares = at("squares", 180224, [P, 2, TPC, HG, HD], F32)
        rope_prod = at("rope_prod", 180224, [P, 2, 4, TPC, HG // 2, HD // 2], F32)
        wqkv_raw = at("wqkv_raw", 176128, [P, KC, 3 * P], F32)
        split = at("split", 184320, [P, 2, TPC, HG, 3, HD], F32R)
        y_norm = at("y_norm", 196608, [P, 2, CH], F32)
        inv_sum = at("inv_sum", 200704, [P, CH], F32)
        cos = at("cos", 202752, [P, NC, TPC, HD // 2], F32)
        sin = at("sin", 204800, [P, NC, TPC, HD // 2], F32)
        ident = at("ident", 208896, [P, P], F32)
        ident_r = at("ident_r", 206848, [P, P], F32R)
        ident_b = at("ident_b", 209408, [P, P], BF16)
        mask_b = at("mask_b", 209664, [P, P], BF16)
        ones = at("ones", 209920, [P, HD], F32)
        gain = at("gain", 210048, [P, HEADS], F32)
        gain_abs = at("gain_abs", 210112, [P, HEADS], F32)
        shift = at("shift", 210176, [P, HEADS // 2], F32)
        sq_sum = at("sq_sum", 210208, [P, 2, TPC, HG], F32)
        inv_norm = at("inv_norm", 210464, [P, 2, TPC, HG], F32)
        newton = at("newton", 210592, [P, 2, TPC, HG], F32)
        shift_now = at("shift_now", 212128, [P, 2], F32)
        inv_col = at("inv_col", 210720, [P, CH // 32], F32)

        scores = ctx.enter_context(nc.psum_tensor("scores", [P, 2, 2, CH], F32))
        bank = [ctx.enter_context(nc.psum_tensor(f"bank{n}", [P, CH], F32)) for n in range(4)]
        y_ps, sums_ps, qkv_ps, turn_ps = bank

        y_dram = nc.dram_tensor("y_scratch", [NG, P, T], F32, kind="Internal").ap()

        consts_ready, ident_ready, mask_filled = sem("consts_ready"), sem("ident_ready"), sem("mask_filled")
        tables_loaded = sem("tables_loaded")
        shift_steps, shift_copied = sem("shift_steps"), sem("shift_copied")
        x_loaded = [sem(f"x_loaded{n}") for n in range(4)]
        x_turned, xT_high, xT_low = sem("x_turned"), sem("xT_high"), sem("xT_low")
        w_loaded, w_high, w_low = sem("w_loaded"), sem("w_high"), sem("w_low")
        qkv_done, qkv_copied = sem("qkv_done"), sem("qkv_copied")
        norm_steps, inv_normed, sums_inverted = sem("norm_steps"), sem("inv_normed"), sem("sums_inverted")
        normed = sem("normed")
        q_products, k_products, q_roped, k_roped = sem("q_products"), sem("k_products"), sem("q_roped"), sem("k_roped")
        split_high, split_low = sem("split_high"), sem("split_low")
        turned, q_ready, k_ready = sem("turned"), sem("q_ready"), sem("k_ready")
        scores_ready, exp_done, pv_done = sem("scores_ready"), sem("exp_done"), sem("pv_done")
        sum_dve, sum_pool = sem("sum_dve"), sem("sum_pool")
        sums_done, sums_read = sem("sums_done"), sem("sums_read")
        y_copied, y_ready = sem("y_copied"), sem("y_ready")
        y_stored = [sem(f"y_stored{n}") for n in range(2)]


        x1T_h = at("x1T_h", 0, [P, KC, T], F32R)
        x1T_l = at("x1T_l", 32768, [P, KC, T], F32R)
        x1 = at("x1", 65536, [P, NT, D], F32)
        x_res = at("x_res", 193536, [P, 4, D], F32)
        rows = at("rows", 106496, [P, 4, D], F32)
        y_raw = at("y_raw", 114688, [P, 4, NG, P], F32)
        wo_l = at("wo_l", 122880, [P, NG, D], F32R)
        gw_raw = at("gw_raw", 131072, [P, KC, E], F32)
        gw_split = at("gw_split", 131200, [P, KC, 2 * E], F32R)
        wo_raw = at("wo_raw", 176128, [P, NG, D], F32)
        wo_h = at("wo_h", 185344, [P, NG, D], F32R)
        y_h = at("y_h", 98304, [P, 2, NG, P], F32R)
        y_l = at("y_l", 102400, [P, 2, NG, P], F32R)
        y_first = [at(f"y_first{n}", 8192 * (n // 2) + 4096 + 2048 * (n % 2), [P, NG, P], F32) for n in range(TPC)]
        x_first = [at(f"x_first{n}", 16384 + 8192 * (n // 2) + 4096 + 2048 * (n % 2), [P, D], F32) for n in range(TPC)]
        GATE, UP, DOWN = 0, 2 * KC * FH, 4 * KC * FH
        SLOT = 4 * KC * FH + 6 * D
        ffn_w = at("ffn_w", 98304, [P, 2, SLOT], F32R)
        raw = at("raw", 167936, [P, SLOT // 2], F32)
        silu = at("silu", 185344, [P, 2, CH], F32)
        hid_h = at("hid_h", 189440, [P, 3, CH], F32R)
        hid_l = at("hid_l", 195584, [P, 3, CH], F32R)
        stage = at("stage", 201728, [P, 2, D], F32)
        R0 = 179200
        logits = at("logits", R0, [P, NT, E], F32)
        shares = at("shares", R0 + 512, [P, NT, E], F32)
        top_values = at("top_values", R0 + 1024, [P, NT, E], F32)
        top_index = at("top_index", R0 + 1536, [P, NT, E], U32)
        ended = at("ended", R0, [P, MAX_TILES, E - 1], F32)
        chosen = at("chosen", R0 + 2048, [P, TOPK, NT, E], F32)
        place = at("place", R0 + 3072, [P, NT, E], F32)
        total = at("total", R0 + 3584, [P, NT, E], F32)
        before = at("before", R0 + 4096, [P, 2, NT, E], F32)
        product = at("product", R0 + 5120, [P, NT, E], F32)
        chosen_b = at("chosen_b", R0 + 5632, [P, NT, E], BF16)
        row_max = at("row_max", 205824, [P, NT], F32)
        row_sum = at("row_sum", 205888, [P, NT], F32)
        top_float = at("top_float", 205952, [P, NT, TOPK], F32)
        place_float = at("place_float", 206080, [P, TOPK, NT], F32)
        tiles_int = at("tiles_int", 206208, [P, E], I32)
        tiles_of = at("tiles_of", 206240, [P, E], F32)
        tile_end = at("tile_end", 206272, [P, 2, E], F32)
        tile_start = at("tile_start", 206336, [P, E], F32)
        tile_expert = at("tile_expert", 206368, [P, MAX_TILES], F32)
        weight = at("weight", 206528, [P, TOPK, NT], F32)
        x_tile = at("x_tile", 185344, [P, 2, D], F32)
        xt_h = at("xt_h", 189440, [P, KC, P], F32R)
        xt_l = at("xt_l", 191488, [P, KC, P], F32R)
        silu_t = at("silu_t", 193536, [P, FH], F32)
        hidden = at("hidden", 194944, [P, FH], F32)
        ht_h = at("ht_h", 196352, [P, 3, P], F32R)
        ht_l = at("ht_l", 197888, [P, 3, P], F32R)
        y_tile = at("y_tile", 199424, [P, 2, D], F32)
        extra = at("extra", 133120, [P, 4, 3, D], F32)
        stats = at("stats", 207360, [P, TPC, 6], F32)
        moments = at("moments", 207456, [P, TPC, 2], F32)
        var_eps = at("var_eps", 207488, [P, TPC], F32)
        rstd = at("rstd", 207520, [P, TPC], F32)
        mean_over = at("mean_over", 207584, [P, TPC], F32)
        ln_work = at("ln_work", 207552, [P, TPC], F32)
        place_int = at("place_int", 210784, [P, TOPK, NT], I32)
        tile_slot = at("tile_slot", 210912, [P, MAX_TILES], I32)
        tile_needs = at("tile_needs", 211072, [P, MAX_TILES], I32)
        tile_numbers = at("tile_numbers", 211392, [P, MAX_TILES], F32)
        tri_b = at("tri_b", 211584, [P, P], BF16)
        ones_b = at("ones_b", 211840, [P, P], BF16)
        start_int = at("start_int", 212096, [P, E], I32)
        zeros = at("zeros", 159744, [P, D], F32)

        HC = [(0, P), (P, P), (2 * P, FH - 2 * P)]
        xs_dram = nc.dram_tensor("x_sorted", [MAX_TILES * P, D], F32, kind="Internal").ap()
        ys_dram = nc.dram_tensor("y_sorted", [MAX_TILES * P, D], F32, kind="Internal").ap()
        half_dram = nc.dram_tensor("first_half", [T, D], F32, kind="Internal").ap()

        lot0_high, lot0_low, ln_ready = sem("lot0_high"), sem("lot0_low"), sem("ln_ready")
        half_added = sem("half_added")
        wo_loaded, wo_high, wo_low = sem("wo_loaded"), sem("wo_high"), sem("wo_low")
        y_loaded = [sem(f"y_loaded{n}") for n in range(4)]
        y_high, y_low = sem("y_high"), sem("y_low")
        projected, res_added, ln_steps, x1_ready = sem("projected"), sem("res_added"), sem("ln_steps"), sem("x1_ready")
        x1_turned, x1T_high, x1T_low = sem("x1_turned"), sem("x1T_high"), sem("x1T_low")
        logits_done, router_steps, router_exp, tables_made = sem("logits_done"), sem("router_steps"), sem("router_exp"), sem("tables_made")
        counted = sem("counted")
        ffn_loaded = [sem(f"ffn_loaded{n}") for n in range(3)]
        ffn_high, ffn_low = sem("ffn_high"), sem("ffn_low")
        gated, silu_done, product_done = sem("gated"), sem("silu_done"), sem("product_done")
        hid_high, hid_low, down_done, down_read = sem("hid_high"), sem("hid_low"), sem("down_done"), sem("down_read")
        half_stored = [sem(f"half_stored{n}") for n in range(2)]
        zero_made, zero_filled, scattered = sem("zero_made"), sem("zero_filled"), sem("scattered")
        xs_first_loaded = [sem(f"xs_first_loaded{n}") for n in range(2)]
        xs_loaded = [sem(f"xs_loaded{n}") for n in range(2)]
        xs_turned, xt_high, xt_low = sem("xs_turned"), sem("xt_high"), sem("xt_low")
        tile_gated, tile_upped, tile_silu, tile_hidden = sem("tile_gated"), sem("tile_upped"), sem("tile_silu"), sem("tile_hidden")
        hid_turned, ht_high, ht_low = sem("hid_turned"), sem("ht_high"), sem("ht_low")
        tile_done, tile_copied = sem("tile_done"), sem("tile_copied")
        ys_stored = [sem(f"ys_stored{n}") for n in range(2)]
        half_loaded, gathered = [sem(f"half_loaded{n}") for n in range(4)], [sem(f"gathered{n}") for n in range(4)]
        extras_added = sem("extras_added")
        numbers_loaded = sem("numbers_loaded")
        out_ready, last_ready, out_stored = sem("out_ready"), sem("last_ready"), sem("out_stored")
        out_rows = out.rearrange("b s d -> (b s) d")
        z_ps = [scores[:, 0, 0], scores[:, 0, 1]]
        x1T_ps = [bank[0][:], bank[1][:]]

        def y_of(t):
            return y_raw[:, t % 4] if t >= TPC else y_first[t][:]

        def x_of(t):
            return x_res[:, t % 4] if t >= TPC else x_first[t][:]

        logits_ps, counts_ps = turn_ps, qkv_ps
        gate_tile, up_tile, xt_ps, ht_ps, out_tile = scores[:, 0, 0], scores[:, 0, 1], scores[:, 1, 0], scores[:, 1, 1], bank[0]

        LOTS = E + 2
        PIECES = 3
        RAW_AT = [0, KC * FH, 2 * KC * FH]

        def slot_of(lot):
            return (lot + 1) % 2

        def weights_of(lot):
            if 0 < lot < LOTS - 1:
                return w_gate[lot - 1], w_up[lot - 1], w_down[lot - 1]
            half = slice(0, FH) if lot == 0 else slice(FH, FS)
            return sw_gate[:, half], sw_up[:, half], sw_down[half, :]

        def areas_of(lot, piece):
            slot, first = slot_of(lot), (GATE, UP, DOWN)[piece]
            n = KC * FH if piece < 2 else 3 * D
            r, full = FH - 2 * P, 2 * D
            if piece < 2:
                cuts = [(P, 0, n)]
            else:
                cuts = [(P, 0, full), (r, full, n)]
            return [(raw[0:p, RAW_AT[piece] + a:RAW_AT[piece] + b],
                     [ffn_w[0:p, slot, first + low * n + a:first + low * n + b] for low in range(2)]) for p, a, b in cuts]

        def stationary(slot, at_, low, k, c0, cn):
            first = at_ + low * KC * FH + k * FH + c0
            return ffn_w[:, slot, first:first + cn]

        def load_y(sp, t):
            sp.dma_start(y_of(t), y_dram[:, :, t * P:(t + 1) * P].rearrange("g p t -> p g t")).then_inc(y_loaded[t % 4], 16)
            sp.dma_start(x_of(t), x_rows[t * P:(t + 1) * P, :]).then_inc(y_loaded[t % 4], 16)

        def load_piece(sp, lot, piece):
            if lot == 1:
                sp.wait_ge(lot0_low, piece + 1)
            if lot > 1:
                sp.wait_ge(ffn_low, PIECES * (lot - 2) + piece + 1)
            src, to = weights_of(lot)[piece], raw[:, RAW_AT[piece]:]
            if piece < 2:
                sp.dma_start(to[:, 0:KC * FH].rearrange("p (k n) -> p k n", k=KC), src.rearrange("(k p) n -> p k n", p=P)).then_inc(ffn_loaded[piece], 16)
            else:
                sp.dma_start(to[:, 0:2 * D].rearrange("p (k n) -> p k n", k=2), src[0:2 * P].rearrange("(k p) n -> p k n", p=P)).then_inc(ffn_loaded[piece], 16)
                sp.dma_start(to[0:FH - 2 * P, 2 * D:3 * D], src[2 * P:FH]).then_inc(ffn_loaded[piece], 16)

        def tail_sync(sp):
            sp.wait_ge(pv_done, SLOTS * NG)
            for n in range(2):
                sp.wait_ge(y_stored[n], 16 * NC * NG // 2)
            for t in range(TPC, NT):
                if t >= 2 * TPC:
                    sp.wait_ge(y_low, t - 3)
                    sp.wait_ge(y_high, t - 3)
                    sp.wait_ge(res_added, t - 3)
                load_y(sp, t)
                if t == 2 * TPC - 1:
                    sp.wait_ge(sums_done, len(ADDING) * NG)
                    for piece in range(PIECES):
                        load_piece(sp, 0, piece)
            for piece in range(2):
                load_piece(sp, 1, piece)

            def store_half(t):
                sp.wait_ge(down_read, t + 1)
                sp.dma_start(half_dram[t * P:(t + 1) * P, :], stage[:, t % 2]).then_inc(half_stored[t % 2], 16)

            for t in range(TPC):
                store_half(t)
            sp.wait_ge(router_steps, R_STEPS)
            load_piece(sp, 1, 2)
            for t in range(TPC, 2 * TPC):
                store_half(t)
            for piece in range(2):
                load_piece(sp, 2, piece)
            for t in range(2 * TPC, NT):
                store_half(t)
            load_piece(sp, 2, 2)
            for lot in range(3, LOTS):
                for piece in range(PIECES):
                    load_piece(sp, lot, piece)
            for n in range(2):
                sp.wait_ge(half_stored[n], 16 * NT // 2)
            sp.wait_ge(tile_done, MAX_TILES + 1)
            for t in range(NT):
                if t >= 4:
                    sp.wait_ge(half_added, t - 3)
                sp.dma_start(extra[:, t % 4, 0], half_dram[t * P:(t + 1) * P, :]).then_inc(half_loaded[t % 4], 16)
            for t in range(NT):
                if t < NT - TPC // 2:
                    sp.wait_ge(out_ready, t + 1)
                else:
                    sp.wait_ge(last_ready, t + 1 - (NT - TPC // 2))
                sp.dma_start(out_rows[t * P:(t + 1) * P, :], x1[:, t]).then_inc(out_stored, 16)
            sp.wait_ge(out_stored, 16 * NT)

        def tail_tensor(pe):
            pe.wait_ge(wo_high, 2)
            pe.wait_ge(wo_low, 2)
            for t in range(NT):
                pe.wait_ge(y_high, t + 1)
                pe.wait_ge(y_low, t + 1)
                if t >= 2:
                    pe.wait_ge(res_added, t - 1)
                for m, (ys, ws) in enumerate(((y_h, wo_h), (y_l, wo_h), (y_h, wo_l))):
                    for g in range(NG):
                        mm = nc.tensor.matmul(z_ps[t % 2], ys[:, t % 2, g, :], ws[:, g, :],
                                              start=(m == 0 and g == 0), stop=(m == 2 and g == NG - 1))
                mm.then_inc(projected, 1)
                if t >= TURN_LAG:
                    pe_turn_x1(pe, t - TURN_LAG)
                if t > TURN_LAG:
                    pe_logits(pe, t - TURN_LAG - 1)
            for s in range(NT - TURN_LAG, NT - TPC):
                pe_turn_x1(pe, s)
            pe_logits(pe, NT - TURN_LAG - 1)
            pe_shared(pe, 0)
            pe.wait_ge(router_steps, R_STEPS)
            pe.wait_ge(product_done, 3 * NC)
            pe.wait_ge(down_read, NT)
            pe.sem_inc(tile_done, 1)
            each_tile(pe, pe_tile)
            pe_shared(pe, 1)

        def each_tile(engine, step):
            for j in range(3):
                step(engine, j, (j + 1) // 2, j % 2)
            pairs = (MAX_TILES - 7) // 2
            with engine.Fori(0, pairs) as pair:
                for odd in range(2):
                    step(engine, 2 * pair + (3 + odd), pair + 2, 1 - odd)
            for j in range(3 + 2 * pairs, MAX_TILES + 1):
                step(engine, j, (j + 1) // 2, j % 2)

        def is_tile(j):
            return not isinstance(j, int) or j < MAX_TILES

        def has_last(j):
            return not isinstance(j, int) or j > 0

        def has_next(j):
            return not isinstance(j, int) or j + 1 < MAX_TILES

        def pe_tile(pe, j, half, odd):
            if is_tile(j):
                needs = pe.value_load(tile_needs[0:1, bass.ds(j, 1)], min_val=1, max_val=PIECES * LOTS)
                slot = pe.value_load(tile_slot[0:1, bass.ds(j, 1)], min_val=0, max_val=1)
                pe.wait_ge(ffn_low, needs)
                pe.wait_ge(xt_high, j + 1)
                pe.wait_ge(xt_low, j + 1)
                if has_last(j):
                    pe.wait_ge(tile_silu, j)
                    pe.wait_ge(tile_hidden, j)
                tile_product(gate_tile, slot, GATE).then_inc(tile_gated, 1)
            if has_last(j):
                pe.wait_ge(tile_hidden, j)
                if not isinstance(j, int) or j > 1:
                    pe.wait_ge(ht_low, j - 1)
                for k, (k0, kn) in enumerate(HC):
                    mm = nc.tensor.transpose(ht_ps[0:kn, k * P:(k + 1) * P], hidden[:, k0:k0 + kn], ident[:])
                mm.then_inc(hid_turned, 1)
            if is_tile(j):
                tile_product(up_tile, slot, UP).then_inc(tile_upped, 1)
            if has_next(j):
                turn_x_tile(pe, j + 1, half, 1 - odd)
            if has_last(j) and is_tile(j):
                pe_tile_down(pe, j)

        def pe_tile_down(pe, j):
            slot_before = pe.value_load(tile_slot[0:1, bass.ds(j - 1, 1)], min_val=0, max_val=1)
            pe.wait_ge(ht_high, j)
            pe.wait_ge(ht_low, j)
            if not isinstance(j, int) or j > 1:
                pe.wait_ge(tile_copied, j - 1)
            for m, (hs, low) in enumerate(((ht_h, 0), (ht_l, 0), (ht_h, 1))):
                for k, (k0, kn) in enumerate(HC):
                    mm = nc.tensor.matmul(out_tile[:], hs[0:kn, k, :], moving(slot_before, DOWN + (low * 3 + k) * D, D, kn),
                                          start=(m == 0 and k == 0), stop=(m == 2 and k == 2))
            mm.then_inc(tile_done, 1)

        def tile_product(to, slot, first):
            for m, (xs, low) in enumerate(((xt_h, 0), (xt_l, 0), (xt_h, 1))):
                for k in range(KC):
                    mm = nc.tensor.matmul(to[:, 0:FH], xs[:, k, :], moving(slot, first + (low * KC + k) * FH, FH),
                                          start=(m == 0 and k == 0), stop=(m == 2 and k == KC - 1))
            return mm

        def turn_x_tile(pe, i, half, odd):
            if isinstance(i, int) and i < 2:
                pe.wait_ge(xs_first_loaded[i], 16)
            else:
                pe.wait_ge(xs_loaded[odd], 16 * half)
            if not isinstance(i, int) or i:
                pe.wait_ge(xt_low, i)
            else:
                pe.wait_ge(product_done, 3 * NC)
            for k in range(KC):
                mm = nc.tensor.transpose(xt_ps[:, k * P:(k + 1) * P], x_tile[:, odd, k * P:(k + 1) * P], ident[:])
            mm.then_inc(xs_turned, 1)

        def pe_turn_x1(pe, s):
            pe.wait_ge(x1_ready, s + 1)
            if s >= 2:
                pe.wait_ge(x1T_low, s - 1)
            for k in range(KC):
                mm = nc.tensor.transpose(x1T_ps[s % 2][:, k * P:(k + 1) * P], x1[:, s, k * P:(k + 1) * P], ident[:])
            mm.then_inc(x1_turned, 1)

        def pe_logits(pe, s):
            pe.wait_ge(x1T_high, s + 1)
            pe.wait_ge(x1T_low, s + 1)
            first = 2 * E * s
            for m, (xs, n) in enumerate(((x1T_h, 2 * E), (x1T_l, E))):
                for k in range(KC):
                    mm = nc.tensor.matmul(logits_ps[:, first:first + n], xs[:, k, s * P:(s + 1) * P], gw_split[:, k, 0:n],
                                          start=(m == 0 and k == 0), stop=(m == 1 and k == KC - 1))
            mm.then_inc(logits_done, 1)

        def moving(slot, first, n, rows_=P):
            return ffn_w[0:rows_, bass.ds(slot, 1), first:first + n].rearrange("p a n -> p (a n)")

        def pe_shared(pe, half):
            lot = half * (LOTS - 1)
            slot = slot_of(lot)
            if half == 0:
                pe.wait_ge(lot0_low, PIECES)
            else:
                pe.wait_ge(ffn_low, PIECES * lot)
            for c in range(NC + 1):
                for hc, (h0, hn) in enumerate(HC):
                    b = half * NC + c
                    if c < NC:
                        n = b * 3 + hc
                        if n >= 2:
                            pe.wait_ge(product_done, n - 1)
                        for which, at_ in enumerate((GATE, UP)):
                            for m, (xs, low) in enumerate(((x1T_h, 0), (x1T_l, 0), (x1T_h, 1))):
                                for k in range(KC):
                                    mm = nc.tensor.matmul(scores[0:hn, which, n % 2, :], stationary(slot, at_, low, k, h0, hn),
                                                          xs[:, k, c * CH:(c + 1) * CH],
                                                          start=(m == 0 and k == 0), stop=(m == 2 and k == KC - 1))
                            mm.then_inc(gated, 1)
                        if half == 1 and c == 0 and hc == 0:
                            pe_tile_down(pe, MAX_TILES)
                        if half == 0 and n == 0:
                            for s in range(NT - TURN_LAG, NT - TPC):
                                pe_logits(pe, s)
                        if half == 0 and n < 2:
                            for s in range(NT - TPC + 2 * n, NT - TPC + 2 * n + 2):
                                pe_turn_x1(pe, s)
                        if half == 0 and 1 <= n < 3:
                            for s in range(NT - TPC + 2 * n - 2, NT - TPC + 2 * n):
                                pe_logits(pe, s)
                        if half == 0 and n == COUNT_AT:
                            pe.wait_ge(router_steps, CHOSEN_STEPS)
                            pe.wait_ge(tables_made, 1)
                            flat = chosen_b[:].rearrange("p t e -> p (t e)")
                            nc.tensor.matmul(counts_ps[:, 0:NT * E], tri_b[:], flat, start=True, stop=True)
                            nc.tensor.matmul(counts_ps[:, NT * E:2 * NT * E], ones_b[:], flat, start=True, stop=True).then_inc(counted, 1)
                    if half == 0 and c == NC and hc == 0:
                        turn_x_tile(pe, 0, 0, 0)
                    if half == 1 and hc == 0 and c == 1:
                        pe.wait_ge(tile_copied, MAX_TILES)
                    if hc == 0 and c:
                        b -= 1
                        pe.wait_ge(hid_high, 3 * (b + 1))
                        pe.wait_ge(hid_low, 3 * (b + 1))
                        for tt in range(TPC):
                            n = 4 * b + tt
                            if n >= 2:
                                pe.wait_ge(down_read, n - 1)
                            for m, (hs, low) in enumerate(((hid_h, 0), (hid_l, 0), (hid_h, 1))):
                                for k, (k0, kn) in enumerate(HC):
                                    first = DOWN + (low * 3 + k) * D
                                    mm = nc.tensor.matmul(bank[n % 2][:], hs[0:kn, k, tt * P:(tt + 1) * P], ffn_w[0:kn, slot, first:first + D],
                                                          start=(m == 0 and k == 0), stop=(m == 2 and k == 2))
                            mm.then_inc(down_done, 1)

        def tail_scalar(act):
            def act_split_y(t):
                act.wait_ge(y_loaded[t % 4], 32 * (t // 4 + 1))
                if t >= 2:
                    act.wait_ge(projected, t - 1)
                nc.scalar.copy(y_h[:, t % 2], y_of(t)).then_inc(y_high, 1)

            act_split_y(0)
            for t in range(NT + 2):
                if t + 1 < NT:
                    act_split_y(t + 1)
                if t % 4 == 1 and 4 < t < NT:
                    act_norm(act, t // 4 - 1, lambda i: rows[:, i], x1_ready)
                if t in LOT0_HIGH_AT:
                    piece = LOT0_HIGH_AT.index(t)
                    act.wait_ge(ffn_loaded[piece], 16 if piece < 2 else 32)
                    if piece == 0:
                        act.wait_ge(pv_done, SLOTS * NG)
                    for src, (high, low) in areas_of(0, piece):
                        last = nc.scalar.copy(high, src)
                    last.then_inc(lot0_high, 1)
                if t >= TURN_LAG:
                    act_x1T(act, t - TURN_LAG)
            act_shared(act, 0)
            act_split_x(act, 0, 0)
            each_tile(act, act_tile)
            act_shared(act, 1)
            act_norm(act, NC - 1, lambda i: x1[:, TPC * (NC - 1) + i], out_ready, TPC // 2)

        def act_split_x(act, i, odd):
            act.wait_ge(xs_turned, i + 1)
            if not isinstance(i, int) or i:
                act.wait_ge(tile_upped, i)
            else:
                act.wait_ge(down_done, NT)
            nc.scalar.copy(xt_h[:], xt_ps.rearrange("p (k n) -> p k n", k=KC)).then_inc(xt_high, 1)
            if not isinstance(i, int) or i + 2 < MAX_TILES:
                act.dma_start(x_tile[:, odd], xs_dram[bass.ds((i + 2) * P, P), :]).then_inc(xs_loaded[odd], 16)

        def act_tile(act, j, half, odd):
            if is_tile(j):
                act.wait_ge(tile_gated, j + 1)
                if has_last(j):
                    act.wait_ge(tile_hidden, j)
                nc.scalar.activation(silu_t[:], gate_tile[:, 0:FH], ACT.Silu).then_inc(tile_silu, 1)
            if has_last(j):
                act.wait_ge(hid_turned, j)
                if not isinstance(j, int) or j > 1:
                    act.wait_ge(tile_done, j)
                nc.scalar.copy(ht_h[:, 0:2], ht_ps[:, 0:2 * P].rearrange("p (k n) -> p k n", k=2))
                nc.scalar.copy(ht_h[0:FH - 2 * P, 2], ht_ps[0:FH - 2 * P, 2 * P:3 * P]).then_inc(ht_high, 1)
            if has_next(j):
                act_split_x(act, j + 1, 1 - odd)
            if has_last(j):
                act.wait_ge(tile_done, j + 1)
                if not isinstance(j, int) or j > 2:
                    act.wait_ge(ys_stored[1 - odd], 16 * half - 16)
                elif j == 1:
                    for n in range(2):
                        act.wait_ge(half_stored[n], 16 * NT // 2)
                nc.scalar.copy(y_tile[:, 1 - odd], out_tile[:]).then_inc(tile_copied, 1)
                act.wait_ge(tile_copied, j)
                act.dma_start(ys_dram[bass.ds((j - 1) * P, P), :], y_tile[:, 1 - odd]).then_inc(ys_stored[1 - odd], 16)

        def act_norm(act, c, src, done, tiles=TPC):
            act.wait_ge(ln_ready, c + 1 if done is x1_ready else NC + c + 1)
            for i in range(tiles):
                nc.scalar.activation(x1[:, TPC * c + i], src(i), ACT.Identity, bias=mean_over[:, i:i + 1], scale=rstd[:, i:i + 1]).then_inc(done, 1)

        def act_x1T(act, s):
            act.wait_ge(x1_turned, s + 1)
            nc.scalar.copy(x1T_h[:, :, s * P:(s + 1) * P],
                           x1T_ps[s % 2].rearrange("p (k n) -> p k n", k=KC)).then_inc(x1T_high, 1)

        def act_shared(act, half):
            for c in range(NC):
                b = half * NC + c
                for hc, (h0, hn) in enumerate(HC):
                    n = b * 3 + hc
                    act.wait_ge(gated, 2 * n + 1)
                    if n >= 2:
                        act.wait_ge(hid_low, n - 1)
                    if half == 1 and n == 3 * NC:
                        act.wait_ge(ht_low, MAX_TILES)
                        for i in range(2):
                            act.wait_ge(ys_stored[i], 16 * ((MAX_TILES + 1 - i) // 2))
                    nc.scalar.activation(silu[0:hn, n % 2], scores[0:hn, 0, n % 2, :], ACT.Silu).then_inc(silu_done, 1)
                    act.wait_ge(product_done, n + 1)
                    if b:
                        act.wait_ge(down_done, 4 * b)
                    nc.scalar.copy(hid_h[0:hn, hc], silu[0:hn, n % 2]).then_inc(hid_high, 1)
                    if half == 0 and n == 0:
                        act_norm(act, NC - 1, lambda i: rows[:, i], x1_ready)
                    if half == 0 and n < 2:
                        for s in range(NT - TPC + 2 * n, NT - TPC + 2 * n + 2):
                            act_x1T(act, s)
                    if half == 1 and hc == 2 and c:
                        act_norm(act, c - 1, lambda i: x1[:, TPC * (c - 1) + i], out_ready)
                    if half == 0 and n == ROUTER_AT[0]:
                        act.wait_ge(router_steps, 4)
                        nc.scalar.activation(shares[:], shares[:], ACT.Exp).then_inc(router_exp, 1)

        def layernorm(n, c):
            for i in range(TPC):
                nc.vector.bn_aggr(moments[:, i], stats[:, i]).then_inc(ln_steps, 1)
            nc.vector.wait_ge(ln_steps, n + 4)
            nc.vector.tensor_scalar(var_eps[:], moments[:, :, 1], LN_EPS, None, ALU.add).then_inc(ln_steps, 1)
            nc.vector.wait_ge(ln_steps, n + 5)
            if c:
                nc.vector.wait_ge(x1_ready, min(TPC * c, NT))
            if c > NC:
                nc.vector.wait_ge(out_ready, TPC * (c - NC))
            dve_rsqrt(rstd[:], ln_work[:], var_eps[:], ln_steps, n + 5)
            nc.vector.scalar_tensor_tensor(mean_over[:], moments[:, :, 0], -1.0, rstd[:], ALU.mult, ALU.mult).then_inc(ln_ready, 1)

        LN_STEPS = 4 + 4 + 1 + 11
        CHOSEN_STEPS = 10
        TURN_LAG = 6
        EXTRAS_AT = [(), (0, 1), (2, 3), (), (4, 5), (6, 7, 8), (), (9, 10, 11), (12, 13, 14), (), (15,), ()]
        LOT0_HIGH_AT = [9, 11, 13]
        LOT0_LOW_AT = [9, 11, 13]

        def tail_vector(dve):
            for t in range(NT + 2):
                if t < NT:
                    dve.wait_ge(projected, t + 1)
                    if t >= 4:
                        dve.wait_ge(x1_ready, t - 3)
                    if t % 4 == 0 and t:
                        dve.wait_ge(ln_ready, t // 4)
                    nc.vector.tensor_tensor(rows[:, t % 4], z_ps[t % 2], x_of(t), ALU.add).then_inc(res_added, 1)
                    dve.wait_ge(res_added, t + 1)
                    nc.vector.bn_stats(stats[:, t % TPC], rows[:, t % 4]).then_inc(ln_steps, 1)
                if t >= TURN_LAG:
                    dve_x1T(dve, t - TURN_LAG)
                if t < NT and t % TPC == TPC - 1:
                    c = t // TPC
                    dve.wait_ge(ln_steps, LN_STEPS * c + 4)
                    layernorm(LN_STEPS * c + 4, c)
                if t in LOT0_LOW_AT:
                    piece = LOT0_LOW_AT.index(t)
                    dve.wait_ge(lot0_high, piece + 1)
                    for src, (high, low) in areas_of(0, piece):
                        last = nc.vector.tensor_tensor(low, src, high.bitcast(F32), ALU.subtract)
                    last.then_inc(lot0_low, 1)
            dve_shared(dve, 0)
            dve_split_x(dve, 0)
            each_tile(dve, dve_tile)
            dve_shared(dve, 1)
            final_norm(dve, NC - 1)
            dve.wait_ge(ln_ready, 2 * NC)
            for i in range(TPC // 2, TPC):
                t = NT - TPC + i
                nc.vector.tensor_scalar(x1[:, t], x1[:, t], moments[:, i, 0:1], rstd[:, i:i + 1],
                                        ALU.subtract, ALU.mult).then_inc(last_ready, 1)

        def dve_split_x(dve, i):
            dve.wait_ge(xt_high, i + 1)
            nc.vector.tensor_tensor(xt_l[:], xt_ps.rearrange("p (k n) -> p k n", k=KC), xt_h[:].bitcast(F32),
                                    ALU.subtract).then_inc(xt_low, 1)

        def dve_tile(dve, j, half, odd):
            if has_last(j):
                dve.wait_ge(ht_high, j)
                nc.vector.tensor_tensor(ht_l[:, 0:2], ht_ps[:, 0:2 * P].rearrange("p (k n) -> p k n", k=2),
                                        ht_h[:, 0:2].bitcast(F32), ALU.subtract)
                nc.vector.tensor_tensor(ht_l[0:FH - 2 * P, 2], ht_ps[0:FH - 2 * P, 2 * P:3 * P],
                                        ht_h[0:FH - 2 * P, 2].bitcast(F32), ALU.subtract).then_inc(ht_low, 1)
            if is_tile(j):
                dve.wait_ge(tile_silu, j + 1)
                dve.wait_ge(tile_upped, j + 1)
                if has_last(j):
                    dve.wait_ge(hid_turned, j)
                nc.vector.tensor_tensor(hidden[:], silu_t[:], up_tile[:, 0:FH], ALU.mult).then_inc(tile_hidden, 1)
            if has_next(j):
                dve_split_x(dve, j + 1)

        def final_norm(dve, c):
            n = LN_STEPS * (NC + c) + 4
            dve.wait_ge(ln_steps, n)
            layernorm(n, NC + c)

        def dve_x1T(dve, s):
            dve.wait_ge(x1T_high, s + 1)
            nc.vector.tensor_tensor(x1T_l[:, :, s * P:(s + 1) * P],
                                    x1T_ps[s % 2].rearrange("p (k n) -> p k n", k=KC),
                                    x1T_h[:, :, s * P:(s + 1) * P].bitcast(F32), ALU.subtract).then_inc(x1T_low, 1)

        def dve_shared(dve, half):
            for c in range(NC):
                b = half * NC + c
                for hc, (h0, hn) in enumerate(HC):
                    n = b * 3 + hc
                    dve.wait_ge(gated, 2 * n + 2)
                    dve.wait_ge(silu_done, n + 1)
                    nc.vector.tensor_tensor(silu[0:hn, n % 2], silu[0:hn, n % 2], scores[0:hn, 1, n % 2, :], ALU.mult).then_inc(product_done, 1)
                    dve.wait_ge(product_done, n + 1)
                    dve.wait_ge(hid_high, n + 1)
                    nc.vector.tensor_tensor(hid_l[0:hn, hc], silu[0:hn, n % 2], hid_h[0:hn, hc].bitcast(F32), ALU.subtract).then_inc(hid_low, 1)
                    if half == 0 and n < 2:
                        for s in range(NT - TPC + 2 * n, NT - TPC + 2 * n + 2):
                            dve_x1T(dve, s)
                    for part, at_ in enumerate(ROUTER_AT):
                        if half == 0 and n == at_:
                            router(dve, part)
                    if half == 1 and hc == 0 and c:
                        final_norm(dve, c - 1)
                    if half == 1:
                        for t in EXTRAS_AT[3 * c + hc]:
                            add_extras(dve, t)
                for tt in range(TPC):
                    n = 4 * b + tt
                    dve.wait_ge(down_done, n + 1)
                    if half == 0:
                        if n >= 2:
                            dve.wait_ge(half_stored[n % 2], 16 * (n // 2))
                        nc.vector.tensor_copy(stage[:, n % 2], bank[n % 2][:]).then_inc(down_read, 1)
                    else:
                        t = n - NT
                        nc.vector.tensor_tensor(x1[:, t], bank[n % 2][:], x1[:, t], ALU.add).then_inc(down_read, 1)
                        dve.wait_ge(down_read, n + 1)
                        nc.vector.bn_stats(stats[:, tt], x1[:, t]).then_inc(ln_steps, 1)

        def add_extras(dve, t):
            dve.wait_ge(gathered[t % 4], 32 * (t // 4 + 1))
            dve.wait_ge(half_added, t + 1)
            for k in range(TOPK):
                nc.vector.scalar_tensor_tensor(x1[:, t], extra[:, t % 4, 1 + k], weight[:, k, t:t + 1], x1[:, t],
                                               ALU.mult, ALU.add).then_inc(extras_added, 1)
                dve.wait_ge(extras_added, TOPK * t + k + 1)

        ROUTER_AT = [2, 2, 3, 5]
        COUNT_AT = 3
        PLACE_STEPS = 38
        R_STEPS = 54
        step = [0]

        def done(inst):
            inst.then_inc(router_steps, 1)
            step[0] += 1
            nc.vector.wait_ge(router_steps, step[0])

        def router(dve, part):
            ve = nc.vector
            wide = [P, NT, E]
            if part == 0:
                dve.wait_ge(logits_done, NT)
                both = logits_ps[:, 0:NT * 2 * E].rearrange("p (t n) -> p t n", n=2 * E)
                done(ve.tensor_copy(logits[:], both[:, :, 0:E]))
                done(ve.tensor_tensor(logits[:], logits[:], both[:, :, E:2 * E], ALU.add))
                done(ve.tensor_reduce(row_max[:], logits[:], AX, ALU.max))
                done(ve.tensor_tensor(shares[:], logits[:], row_max[:].unsqueeze(2).broadcast_to(wide), ALU.subtract))
                for t in range(NT):
                    top = ve.max(top_values[:, t], logits[:, t])
                done(top)
            elif part == 1:
                for t in range(NT):
                    top = ve.max_index(top_index[:, t], top_values[:, t], logits[:, t])
                done(top)
                done(ve.tensor_copy(top_float[:], top_index[:, :, 0:TOPK]))
                dve.wait_ge(numbers_loaded, 16)
                for k in range(TOPK):
                    done(ve.tensor_tensor(chosen[:, k], tile_numbers[:, 0:E].unsqueeze(1).broadcast_to(wide),
                                          top_float[:, :, k:k + 1].broadcast_to(wide), ALU.is_equal))
                done(ve.tensor_tensor(chosen_b[:], chosen[:, 0], chosen[:, 1], ALU.add))
                assert step[0] == CHOSEN_STEPS
            elif part == 2:
                dve.wait_ge(counted, 1)
                done(ve.tensor_copy(total[:], counts_ps[:, NT * E:2 * NT * E].rearrange("p (t e) -> p t e", e=E)))
                src = total[:]
                for n, far in enumerate((1, 2, 4, 8)):
                    to = before[:, n % 2]
                    done(ve.tensor_copy(to[:, 0:far], src[:, 0:far]))
                    done(ve.tensor_tensor(to[:, far:NT], src[:, far:NT], src[:, 0:NT - far], ALU.add))
                    src = to
                done(ve.tensor_tensor(before[:, 0], before[:, 1], total[:], ALU.subtract))
                done(ve.tensor_scalar(tiles_of[:], before[:, 1, NT - 1], P - 1.0, None, ALU.add))
                done(ve.tensor_copy(tiles_int[:], tiles_of[:]))
                done(ve.tensor_scalar(tiles_int[:], tiles_int[:], 7, None, ALU.arith_shift_right))
                done(ve.tensor_copy(tiles_of[:], tiles_int[:]))
                src = tiles_of[:]
                for n, far in enumerate((1, 2, 4)):
                    to = tile_end[:, n % 2]
                    done(ve.tensor_copy(to[:, 0:far], src[:, 0:far]))
                    done(ve.tensor_tensor(to[:, far:E], src[:, far:E], src[:, 0:E - far], ALU.add))
                    src = to
                done(ve.tensor_tensor(tile_start[:], src, tiles_of[:], ALU.subtract))
                done(ve.scalar_tensor_tensor(place[:], tile_start[:].unsqueeze(1).broadcast_to(wide), float(P), before[:, 0], ALU.mult, ALU.add))
                done(ve.tensor_tensor(place[:], place[:], counts_ps[:, 0:NT * E].rearrange("p (t e) -> p t e", e=E), ALU.add))
                for k in range(TOPK):
                    done(ve.tensor_tensor(product[:], chosen[:, k], place[:], ALU.mult))
                    done(ve.tensor_reduce(place_float[:, k], product[:], AX, ALU.add))
                done(ve.tensor_copy(place_int[:], place_float[:]))
                assert step[0] == PLACE_STEPS, step[0]
            else:
                dve.wait_ge(router_exp, 1)
                done(ve.tensor_reduce(row_sum[:], shares[:], AX, ALU.add))
                done(ve.reciprocal(row_sum[:], row_sum[:]))
                for k in range(TOPK):
                    done(ve.tensor_tensor(product[:], chosen[:, k], shares[:], ALU.mult))
                    done(ve.tensor_reduce(weight[:, k], product[:], AX, ALU.add))
                    done(ve.tensor_tensor(weight[:, k], weight[:, k], row_sum[:], ALU.mult))
                done(ve.tensor_scalar(tile_start[:], tile_start[:], 1.0, None, ALU.add))
                done(ve.tensor_copy(start_int[:], tile_start[:]))
                shape = [P, MAX_TILES, E - 1]
                done(ve.tensor_tensor(ended[:], tile_end[:, 0, 0:E - 1].unsqueeze(1).broadcast_to(shape),
                                      tile_numbers[:].unsqueeze(2).broadcast_to(shape), ALU.is_le))
                done(ve.tensor_reduce(tile_expert[:], ended[:], AX, ALU.add))
                done(ve.tensor_copy(tile_slot[:], tile_expert[:]))
                done(ve.tensor_scalar(tile_slot[:], tile_slot[:], 1, None, ALU.bitwise_and))
                done(ve.tensor_scalar(tile_expert[:], tile_expert[:], 1.0, float(PIECES), ALU.add, ALU.mult))
                done(ve.tensor_copy(tile_needs[:], tile_expert[:]))
                assert step[0] == R_STEPS, step[0]

        def split_piece(pool, lot, piece):
            m = PIECES * (lot - 1) + piece
            pool.wait_ge(ffn_loaded[piece], (16 if piece < 2 else 32) * (lot + 1))
            areas = areas_of(lot, piece)
            for src, (high, low) in areas:
                one = ones[0:src.shape[0], 0:1].broadcast_to(list(src.shape))
                last = nc.gpsimd.tensor_tensor(high, src, one, ALU.mult)
            last.then_inc(ffn_high, 1)
            pool.wait_ge(ffn_high, m + 1)
            for src, (high, low) in areas:
                last = nc.gpsimd.tensor_tensor(low, src, high.bitcast(F32), ALU.subtract)
            last.then_inc(ffn_low, 1)

        def pool_split_wo(pool):
            pool.wait_ge(wo_loaded, 32)
            nc.gpsimd.tensor_tensor(wo_h[:], wo_raw[:], ones[:, 0:1].unsqueeze(2).broadcast_to([P, NG, D]), ALU.mult).then_inc(wo_high, 1)
            nc.gpsimd.tensor_tensor(gw_split[:, :, 0:E], gw_raw[:], ones[:, 0:1].unsqueeze(2).broadcast_to([P, KC, E]), ALU.mult).then_inc(wo_high, 1)
            pool.wait_ge(wo_high, 2)
            nc.gpsimd.tensor_tensor(wo_l[:], wo_raw[:], wo_h[:].bitcast(F32), ALU.subtract).then_inc(wo_low, 1)
            nc.gpsimd.tensor_tensor(gw_split[:, :, E:2 * E], gw_raw[:], gw_split[:, :, 0:E].bitcast(F32), ALU.subtract).then_inc(wo_low, 1)

        def tail_gpsimd(pool):
            for t in range(NT):
                pool.wait_ge(y_high, t + 1)
                if t >= 2:
                    pool.wait_ge(projected, t - 1)
                nc.gpsimd.tensor_tensor(y_l[:, t % 2], y_of(t), y_h[:, t % 2].bitcast(F32), ALU.subtract).then_inc(y_low, 1)
            pool.wait_ge(x1_ready, NT)
            pool.wait_ge(logits_done, NT)
            for piece in range(2):
                split_piece(pool, 1, piece)
            pool.wait_ge(router_steps, PLACE_STEPS)
            pool.wait_ge(zero_filled, 16)
            for t in range(NT):
                for k in range(TOPK):
                    nc.gpsimd.indirect_dma_start(out=xs_dram, out_offset=bass.IndirectOffsetOnAxis(ap=place_int[:, k, t:t + 1], axis=0),
                                                 in_=x1[:, t], in_offset=None).then_inc(scattered, 16)
            split_piece(pool, 1, 2)
            pool.wait_ge(scattered, 16 * TOPK * NT)
            for j in range(2):
                pool.wait_ge(hid_low, 3 * NC - 1 + j)
                pool.dma_start(x_tile[:, j], xs_dram[j * P:(j + 1) * P, :]).then_inc(xs_first_loaded[j], 16)
            pool.wait_ge(router_steps, R_STEPS)
            pool.wait_ge(down_done, NT)
            for lot in range(2, LOTS):
                if lot >= 3:
                    pool.wait_ge(tile_done, pool.value_load(start_int[0:1, lot - 2:lot - 1], min_val=1, max_val=MAX_TILES + 1))
                for piece in range(PIECES):
                    split_piece(pool, lot, piece)
            pool.wait_ge(tile_done, MAX_TILES + 1)
            for i in range(2):
                pool.wait_ge(ys_stored[i], 16 * ((MAX_TILES + 1 - i) // 2))
            for t in range(NT):
                if t >= 4:
                    pool.wait_ge(extras_added, TOPK * (t - 3))
                for k in range(TOPK):
                    nc.gpsimd.indirect_dma_start(out=extra[:, t % 4, 1 + k], out_offset=None, in_=ys_dram,
                                                 in_offset=bass.IndirectOffsetOnAxis(ap=place_int[:, k, t:t + 1], axis=0)).then_inc(gathered[t % 4], 16)
                pool.wait_ge(half_loaded[t % 4], 16 * (t // 4 + 1))
                nc.gpsimd.tensor_tensor(x1[:, t], x1[:, t], extra[:, t % 4, 0], ALU.add).then_inc(half_added, 1)

        x_rows = x.rearrange("b s d -> (b s) d")
        block = ctx.enter_context(nc.Block())

        def later(g):
            return not isinstance(g, int) or g > 0

        def sums_before(g, i):
            return len(ADDING) * g + ADDING.index(i)

        def has_following(g):
            return not isinstance(g, int) or g + 1 < NG

        def each_group(engine, group):
            group(0)
            with engine.Fori(1, NG - 1) as g:
                group(g)
            group(NG - 1)

        def added(g, slot):
            return (SLOTS - len(DIRECT)) * g + sum(n not in DIRECT for n in range(slot + 1))

        def load_w(sp, g):
            for part in range(3):
                col = part * D + g * P
                sp.dma_start(wqkv_raw[:, :, part * P:(part + 1) * P],
                             w_qkv.rearrange("(k p) n -> p k n", p=P)[:, :, col:col + P]).then_inc(w_loaded, 16)

        @block.sync
        def _(sp):
            for t in range(NT):
                if t >= 4:
                    sp.wait_ge(x_turned, t - 3)
                sp.dma_start(x_in[:, t % 4, :], x_rows[t * P:(t + 1) * P, :]).then_inc(x_loaded[t % 4], 16)
                if t == 3:
                    load_w(sp, 0)
                    sp.dma_start(tile_numbers[:], numbers.rearrange("(a h) -> a h", a=1).broadcast_to([P, MAX_TILES])).then_inc(numbers_loaded, 16)
                    for to, of in ((cos, rope_cos), (sin, rope_sin)):
                        for c in range(NC):
                            sp.dma_start(to[:, c], of[c * CH:(c + 1) * CH, :].rearrange("(t p) f -> p t f", p=P)).then_inc(tables_loaded, 16)
                    sp.dma_start(gain[:], q_gain.rearrange("(a h) -> a h", a=1).broadcast_to([P, HEADS])).then_inc(tables_loaded, 16)
            sp.wait_ge(zero_made, 1)
            sp.dma_start(xs_dram.rearrange("(j p) d -> p j d", p=P), zeros[:].unsqueeze(1).broadcast_to([P, MAX_TILES, D])).then_inc(zero_filled, 16)
            def group(g):
                for i in range(NC):
                    if i == 2:
                        sp.wait_ge(split_high, 4 * g + 4)
                        sp.wait_ge(split_low, 2 * (4 * g + 4))
                        if has_following(g):
                            load_w(sp, g + 1)
                        else:
                            sp.dma_start(wo_raw[:], w_out.rearrange("(g p) n -> p g n", p=P)).then_inc(wo_loaded, 16)
                            sp.dma_start(gw_raw[:], gate_w.rearrange("(k p) n -> p k n", p=P)).then_inc(wo_loaded, 16)
                            sp.wait_ge(y_stored[0], 16 * (NC * g + i) // 2)
                            for t in range(TPC):
                                load_y(sp, t)
                    step = NC * g + i
                    sp.wait_ge(y_ready, step + 1)
                    sp.dma_start(y_dram[g, :, i * CH:(i + 1) * CH], y_norm[:, i % 2, :]).then_inc(y_stored[i % 2], 16)

            for g in range(NG):
                group(g)
            tail_sync(sp)

        def pe_project(g, c, tt):
            n = 4 * (NC * g + c) + tt
            if tt == 0 and c == 0:
                nc.tensor.wait_ge(w_high, g + 1)
            if later(g) or c or tt:
                nc.tensor.wait_ge(qkv_copied, n)
            tok = slice((TPC * c + tt) * P, (TPC * c + tt + 1) * P)
            for m, (xs, ws) in enumerate(((xT_h, wqkv_h), (xT_l, wqkv_h), (xT_h, wqkv_l))):
                if tt == 0 and c == 0 and m == 2:
                    nc.tensor.wait_ge(w_low, g + 1)
                for k in range(KC):
                    mm = nc.tensor.matmul(qkv_ps[:, 0:3 * P], xs[:, k, tok], ws[:, k, :],
                                          start=(m == 0 and k == 0), stop=(m == 2 and k == KC - 1))
            mm.then_inc(qkv_done, 1)

        def pe_turn(g, c, h, which):
            C = NC * g + c
            if h == 0 and which:
                nc.tensor.wait_ge(split_high, C + 1)
                nc.tensor.wait_ge(split_low, 2 * (C + 1))
            if not which:
                nc.tensor.wait_ge(k_ready, 4 * C + h + 1)
            elif later(g) or c or h:
                nc.tensor.wait_ge(q_ready, 4 * C + h)
            for tt in range(TPC):
                mm = nc.tensor.matmul(turn_ps[0:3 * HD, tt * P:(tt + 1) * P],
                                      split[:, which, tt, h, :, :].rearrange("p s d -> p (s d)"), ident_r[:],
                                      start=True, stop=True)
            mm.then_inc(turned, 1)

        def pe_scores(g, slot):
            i, j = step_of(slot)
            n = SLOTS * g + slot
            if j == 0:
                nc.tensor.wait_ge(q_ready, 4 * (NC * g + i + 1))
                nc.tensor.wait_ge(k_ready, 4 * (NC * g + i + 1))
            lo = max(0, (j - TPC * i) * P)
            for p in range(2):
                if later(g) or slot:
                    nc.tensor.wait_ge(exp_done, 2 * n + p - 1)
                for hh in range(2):
                    h = 2 * p + hh
                    diagonal = j >= TPC * i
                    mm = nc.tensor.matmul(scores[:, p, hh, lo:CH], k_stack[0:3 * HD, h, j * P:(j + 1) * P],
                                          q_stack[0:3 * HD, i % 2, h, lo:CH], start=True, stop=not diagonal)
                    if diagonal:
                        mm = nc.tensor.matmul(scores[:, p, hh, lo:lo + P], ident_b[:], mask_b[:],
                                              start=False, stop=True)
                mm.then_inc(scores_ready, 1)

        def pe_values(g, slot):
            i, j = step_of(slot)
            n, step = SLOTS * g + slot, NC * g + i
            if i in ADDING and slot == STEP_AT[i + 1] - 1:
                pe_sums(g, i)
            nc.tensor.wait_ge(exp_done, 2 * n + 2)
            if j == 0 and (later(g) or i):
                nc.tensor.wait_ge(y_copied, step)
            lo = max(0, (j - TPC * i) * P)
            last = TPC * (i + 1) - 1
            if slot in DIRECT:
                first = min(DIRECT & set(range(STEP_AT[i], STEP_AT[i + 1]))) == slot
                if first and (later(g) or i):
                    nc.tensor.wait_ge(sums_read, step)
                for h in range(HG):
                    nc.tensor.matmul(sums_ps[HD * h:HD * (h + 1), lo:CH], ones[:], probs[:, slot % 4, h, lo:CH],
                                     start=first, stop=(j == last))
            for h in range(HG):
                mm = nc.tensor.matmul(y_ps[HD * h:HD * (h + 1), lo:CH],
                                      v_sb[:, j, HD * h:HD * (h + 1)], probs[:, slot % 4, h, lo:CH],
                                      start=(j == 0), stop=(j == last))
            mm.then_inc(pv_done, 1)

        def pe_sums(g, i):
            nc.tensor.wait_ge(sum_dve, added(g, STEP_AT[i + 1] - 1))
            nc.tensor.wait_ge(sum_pool, added(g, STEP_AT[i + 1] - 1))
            for h in range(HG):
                mm = nc.tensor.matmul(sums_ps[HD * h:HD * (h + 1), :], ones[:], key_sum[:, h, :], start=False, stop=False)
            mm.then_inc(sums_done, 1)

        @block.tensor
        def _(pe):
            pe.wait_ge(consts_ready, 1)
            for t in range(NT):
                pe.wait_ge(x_loaded[t % 4], 16 * (t // 4 + 1))
                if t >= 4:
                    pe.wait_ge(xT_low, t - 3)
                for k in range(KC):
                    mm = nc.tensor.transpose(scores[:, (t % 4) // 2, t % 2, k * P:(k + 1) * P],
                                             x_in[:, t % 4, k * P:(k + 1) * P], ident[:])
                mm.then_inc(x_turned, 1)
                if 0 <= t - FIRST_AFTER < TPC:
                    pe.wait_ge(xT_low, TPC)
                    pe.wait_ge(xT_high, TPC)
                    pe.wait_ge(ident_ready, 1)
                    pe_project(0, 0, t - FIRST_AFTER)
            pe.wait_ge(xT_low, NT)
            pe.wait_ge(xT_high, NT)
            for h in range(HG):
                pe_turn(0, 0, h, 1)
                pe_turn(0, 0, h, 0)
                pe_project(0, 1, h)
            def group(g):
                for slot in range(SLOTS):
                    pe_scores(g, slot)
                    for work in work_at(PROJECT_AT, slot, g):
                        pe_project(*work)
                    turns = list(work_at(TURN_AT, slot, g))
                    for n, work in enumerate(turns):
                        pe_turn(*work, 1)
                        if n + 1 < len(turns):
                            pe_turn(*work, 0)
                    if slot or later(g):
                        pe_values(g if slot else g - 1, (slot - 1) % SLOTS)
                    for work in turns[-1:]:
                        pe_turn(*work, 0)

            each_group(pe, group)
            pe_values(NG - 1, SLOTS - 1)
            tail_tensor(pe)

        def act_copy_qkv(g, c, tt):
            C = NC * g + c
            n = 4 * C + tt
            nc.scalar.wait_ge(qkv_done, n + 1)
            if tt == 0 and (later(g) or c):
                nc.scalar.wait_ge(split_high, C)
                nc.scalar.wait_ge(split_low, 2 * C)
            if tt == 0 and c == 0:
                nc.scalar.wait_ge(w_high, g + 1)
                nc.scalar.wait_ge(w_low, g + 1)
            rows = qkv_ps[:, 0:2 * P].rearrange("p (w h d) -> p w h d", w=2, h=HG)
            nc.scalar.copy(qk[:, :, tt], rows)
            if tt == 0 and (later(g) or c):
                nc.scalar.wait_ge(q_roped, 2 * C)
                nc.scalar.wait_ge(k_roped, 2 * C)
            nc.scalar.activation(squares[:, :, tt], rows, ACT.Square)
            if later(g):
                nc.scalar.wait_ge(pv_done, SLOTS * (g - 1) + STEP_AT[3] + 4 * c + tt + 1)
            nc.scalar.copy(v_sb[:, TPC * c + tt, :], qkv_ps[:, 2 * P:3 * P]).then_inc(qkv_copied, 1)

        def act_copy_q(g, c, h):
            C = NC * g + c
            nc.scalar.wait_ge(turned, 8 * C + 2 * h + 2)
            if h == 0 and (later(g) or c >= 2):
                there = g if c >= 2 else g - 1
                nc.scalar.wait_ge(scores_ready, 2 * (SLOTS * there + STEP_AT[(c - 2) % 4 + 1]))
            nc.scalar.copy(q_stack[0:3 * HD, c % 2, h, :], turn_ps[0:3 * HD, :]).then_inc(q_ready, 1)

        def act_copy_y(g, i):
            step = NC * g + i
            nc.scalar.wait_ge(pv_done, SLOTS * g + STEP_AT[i + 1])
            if later(g) or i >= 2:
                nc.scalar.wait_ge(y_stored[i % 2], 16 * (NC // 2 * g + i // 2))
            nc.scalar.copy(y_norm[:, i % 2, :], y_ps[:]).then_inc(y_copied, 1)

        def act_exp(g, slot):
            i, j = step_of(slot)
            n = SLOTS * g + slot
            lo = max(0, (j - TPC * i) * P)
            if not later(g) and slot == 3:
                nc.scalar.wait_ge(zero_filled, 16)
            if not later(g) and slot == 0:
                nc.scalar.wait_ge(x_turned, NT)
            if later(g) or slot >= 4:
                nc.scalar.wait_ge(pv_done, n - 3)
                before = added(g if slot >= 4 else g - 1, (slot - 4) % SLOTS)
                if later(g) or before:
                    nc.scalar.wait_ge(sum_dve, before)
                    nc.scalar.wait_ge(sum_pool, before)
            for p in range(2):
                nc.scalar.wait_ge(scores_ready, 2 * n + p + 1)
                nc.scalar.activation(probs[:, slot % 4, 2 * p:2 * p + 2, lo:CH], scores[:, p, :, lo:CH], ACT.Exp,
                                     bias=shift_now[:, p:p + 1]).then_inc(exp_done, 1)

        @block.scalar
        def _(act):
            for t in range(NT):
                act.wait_ge(x_turned, t + 1)
                nc.scalar.copy(xT_h[:, :, t * P:(t + 1) * P],
                               scores[:, (t % 4) // 2, t % 2, :].rearrange("p (k n) -> p k n", k=KC)).then_inc(xT_high, 1)
                if 0 <= t - FIRST_AFTER < TPC:
                    act_copy_qkv(0, 0, t - FIRST_AFTER)
            for h in range(HG):
                act_copy_q(0, 0, h)
                act_copy_qkv(0, 1, h)
            def group(g):
                if not later(g):
                    nc.scalar.wait_ge(shift_steps, 5)
                else:
                    act.wait_ge(exp_done, 2 * SLOTS * g)
                nc.scalar.copy(shift_now[:], shift[:, bass.ds(2 * g, 2)]).then_inc(shift_copied, 1)
                act.wait_ge(shift_copied, g + 1)
                for slot in range(SLOTS):
                    act_exp(g, slot)
                    if slot in STEP_AT and (slot or later(g)):
                        i = STEP_AT.index(slot)
                        act_copy_y(g if i else g - 1, (i - 1) % NC)
                    for work in work_at(PROJECT_AT, slot, g):
                        act_copy_qkv(*work)
                    for work in work_at(TURN_AT, slot, g):
                        act_copy_q(*work)

            each_group(act, group)
            act_copy_y(NG - 1, NC - 1)
            tail_scalar(act)

        def dve_split_w(g):
            nc.vector.wait_ge(w_loaded, 48 * (g + 1))
            if later(g):
                nc.vector.wait_ge(qkv_done, 16 * g)
            nc.vector.tensor_copy(wqkv_h[:], wqkv_raw[:]).then_inc(w_high, 1)

        def dve_rsqrt(out, work, arg, ready, steps):
            n = steps
            for do in range(2):
                if do == 0:
                    nc.vector.tensor_scalar(out.bitcast(I32), arg.bitcast(I32), 1, None, ALU.arith_shift_right).then_inc(ready, 1)
                else:
                    nc.vector.tensor_scalar(out.bitcast(I32), out.bitcast(I32), -1.0, RSQRT_GUESS, ALU.mult, ALU.add).then_inc(ready, 1)
                n += 1
                nc.vector.wait_ge(ready, n)
            for _ in range(3):
                nc.vector.scalar_tensor_tensor(work, out, -0.5, out, ALU.mult, ALU.mult).then_inc(ready, 1)
                nc.vector.wait_ge(ready, n + 1)
                nc.vector.tensor_tensor(work, work, arg, ALU.mult).then_inc(ready, 1)
                nc.vector.wait_ge(ready, n + 2)
                nc.vector.scalar_tensor_tensor(out, work, 1.5, out, ALU.add, ALU.mult).then_inc(ready, 1)
                nc.vector.wait_ge(ready, n + 3)
                n += 3

        def dve_norms(g, c):
            C = NC * g + c
            nc.vector.wait_ge(qkv_copied, 4 * (C + 1))
            nc.vector.tensor_reduce(sq_sum[:], squares[:], AX, ALU.add).then_inc(norm_steps, 1)
            nc.vector.wait_ge(norm_steps, 13 * C + 1)
            nc.vector.tensor_scalar(sq_sum[:], sq_sum[:], UNIT_EPS, None, ALU.add).then_inc(norm_steps, 1)
            nc.vector.wait_ge(norm_steps, 13 * C + 2)
            if later(g) or c:
                nc.vector.wait_ge(normed, C)
            dve_rsqrt(inv_norm[:], newton[:], sq_sum[:], norm_steps, 13 * C + 2)
            nc.vector.tensor_tensor(inv_norm[:, 0], inv_norm[:, 0],
                                    gain[:, bass.ds(HG * g, HG)].unsqueeze(1).broadcast_to([P, TPC, HG]),
                                    ALU.mult).then_inc(inv_normed, 1)
            nc.vector.wait_ge(inv_normed, C + 1)
            rows = qk[:].rearrange("p w t h d -> p (w t h) d")
            nc.vector.tensor_tensor(rows, rows, inv_norm[:].rearrange("p w t h -> p (w t h)").unsqueeze(2)
                                    .broadcast_to([P, 2 * TPC * HG, HD]), ALU.mult).then_inc(normed, 1)
            rotate(nc.vector, 0, C, c, q_products, q_roped)

        def rotate(engine, which, C, c, products, done):
            half, shape = HD // 2, [P, TPC, HG // 2, HD // 2]
            even, prod = qk[:, which, :, 0::2, :], rope_prod[:, which]
            first, second = even[:, :, :, 0:half], even[:, :, :, half:HD]
            cs, sn = [table[:, c].unsqueeze(2).broadcast_to(shape) for table in (cos, sin)]
            engine.wait_ge(normed, C + 1)
            engine.tensor_tensor(prod[:, 0], first, cs, ALU.mult)
            engine.tensor_tensor(prod[:, 1], second, sn, ALU.mult)
            engine.tensor_tensor(prod[:, 2], first, sn, ALU.mult)
            engine.tensor_tensor(prod[:, 3], second, cs, ALU.mult).then_inc(products, 1)
            engine.wait_ge(products, C + 1)
            engine.tensor_tensor(first, prod[:, 0], prod[:, 1], ALU.subtract).then_inc(done, 1)
            engine.tensor_tensor(second, prod[:, 2], prod[:, 3], ALU.add).then_inc(done, 1)

        def dve_split(g, c):
            C = NC * g + c
            nc.vector.wait_ge(q_roped, 2 * (C + 1))
            nc.vector.wait_ge(k_roped, 2 * (C + 1))
            if later(g) or c:
                nc.vector.wait_ge(turned, 8 * C)
            rows = [qk[:, w].rearrange("p t h d -> p (t h) d") for w in range(2)]
            parts = [split[:, w].rearrange("p t h s d -> p (t h) s d") for w in range(2)]
            twice = [r.unsqueeze(2).broadcast_to([P, TPC * HG, 2, HD]) for r in rows]
            nc.vector.tensor_copy(parts[0][:, :, 0:2, :], twice[0])
            nc.vector.tensor_copy(parts[1][:, :, 0::2, :], twice[1]).then_inc(split_high, 1)
            nc.vector.wait_ge(split_high, C + 1)
            for w, low in ((0, 2), (1, 1)):
                nc.vector.tensor_tensor(parts[w][:, :, low, :], rows[w], parts[w][:, :, 0, :].bitcast(F32),
                                        ALU.subtract).then_inc(split_low, 1)

        def dve_copy_k(g, c, h):
            C = NC * g + c
            nc.vector.wait_ge(turned, 8 * C + 2 * h + 1)
            if later(g) and h == 0:
                nc.vector.wait_ge(scores_ready, 2 * (SLOTS * (g - 1) + STEP_AT[3] + TPC * (c + 1)))
            nc.vector.tensor_copy(k_stack[0:3 * HD, h, c * CH:(c + 1) * CH], turn_ps[0:3 * HD, :]).then_inc(k_ready, 1)

        def dve_add_keys(g, slot):
            i, j = step_of(slot)
            n = SLOTS * g + slot
            lo = max(0, (j - TPC * i) * P)
            nc.vector.wait_ge(exp_done, 2 * n + 2)
            if later(g) or added(g, slot) > 1:
                nc.vector.wait_ge(sum_dve, added(g, slot) - 1)
            if slot == first_added(i):
                if later(g) or i > ADDING[0]:
                    nc.vector.wait_ge(sums_done, sums_before(g, i))
                nc.vector.tensor_copy(key_sum[:, 0:3, :], probs[:, slot % 4, 0:3, :]).then_inc(sum_dve, 1)
            else:
                nc.vector.tensor_tensor(key_sum[:, 0:3, lo:CH], key_sum[:, 0:3, lo:CH], probs[:, slot % 4, 0:3, lo:CH],
                                        ALU.add).then_inc(sum_dve, 1)

        def dve_outputs(g, i):
            step = NC * g + i
            nc.vector.wait_ge(pv_done, SLOTS * g + STEP_AT[i + 1])
            if later(g) or i:
                nc.vector.wait_ge(y_ready, step)
            nc.vector.transpose(inv_sum[:], sums_ps[:]).then_inc(sums_read, 1)
            nc.vector.wait_ge(sums_read, step + 1)
            nc.vector.reciprocal(inv_col[:], inv_sum[:].rearrange("p (b n) -> p b n", n=32)[:, :, 0]).then_inc(sums_inverted, 1)
            nc.vector.wait_ge(sums_inverted, 2 * step + 1)
            nc.vector.transpose(inv_sum[:], inv_col[:].unsqueeze(2).broadcast_to([P, CH // 32, 32])).then_inc(sums_inverted, 1)
            nc.vector.wait_ge(sums_inverted, 2 * step + 2)
            nc.vector.wait_ge(y_copied, step + 1)
            nc.vector.tensor_tensor(y_norm[:, i % 2, :], y_norm[:, i % 2, :], inv_sum[:], ALU.mult).then_inc(y_ready, 1)

        @block.vector
        def _(dve):
            dve.wait_ge(consts_ready, 1)
            nc.vector.tensor_copy(ident_r[:], ident[:]).then_inc(ident_ready, 1)
            for t in range(NT):
                dve.wait_ge(xT_high, t + 1)
                nc.vector.tensor_tensor(xT_l[:, :, t * P:(t + 1) * P],
                                        scores[:, (t % 4) // 2, t % 2, :].rearrange("p (k n) -> p k n", k=KC),
                                        xT_h[:, :, t * P:(t + 1) * P].bitcast(F32), ALU.subtract).then_inc(xT_low, 1)
                if t == 3:
                    dve_split_w(0)
                if t == NORM_AFTER:
                    dve.wait_ge(tables_loaded, 16 * (2 * NC + 1))
                    nc.vector.tensor_scalar(gain_abs[:], gain[:], -1.0, None, ALU.mult).then_inc(shift_steps, 1)
                    dve.wait_ge(shift_steps, 1)
                    nc.vector.tensor_tensor(gain_abs[:], gain_abs[:], gain[:], ALU.max).then_inc(shift_steps, 1)
                    dve.wait_ge(shift_steps, 2)
                    pairs = gain_abs[:].rearrange("p (a b) -> p a b", b=2)
                    nc.vector.tensor_tensor(shift[:], pairs[:, :, 0], pairs[:, :, 1], ALU.max).then_inc(shift_steps, 1)
                    dve.wait_ge(shift_steps, 3)
                    nc.vector.tensor_scalar(shift[:], shift[:], EXP_SAFE, 0.0, ALU.subtract, ALU.max).then_inc(shift_steps, 1)
                    dve.wait_ge(shift_steps, 4)
                    nc.vector.tensor_scalar(shift[:], shift[:], -1.0, None, ALU.mult).then_inc(shift_steps, 1)
                    dve_norms(0, 0)
                if t == SPLIT_AFTER:
                    dve_split(0, 0)
            for h in range(HG):
                dve_copy_k(0, 0, h)
            dve_norms(0, 1)
            dve_split(0, 1)
            def group(g):
                for slot in range(SLOTS):
                    for work in work_at(TURN_AT, slot, g):
                        dve_copy_k(*work)
                    if slot in STEP_AT and (slot or later(g)):
                        i = STEP_AT.index(slot)
                        dve_outputs(g if i else g - 1, (i - 1) % NC)
                    if slot not in DIRECT:
                        dve_add_keys(g, slot)
                    for gg, c, stage in work_at(NORMALISE_AT, slot, g):
                        if stage == 0:
                            dve_norms(gg, c)
                        if stage == 2:
                            dve_split(gg, c)
                    if slot == SPLIT_W_AT and has_following(g):
                        dve_split_w(g + 1)

            each_group(dve, group)
            dve_outputs(NG - 1, NC - 1)
            tail_vector(dve)

        def pool_split_w(g):
            nc.gpsimd.wait_ge(w_high, g + 1)
            nc.gpsimd.tensor_tensor(wqkv_l[:], wqkv_raw[:], wqkv_h[:].bitcast(F32), ALU.subtract).then_inc(w_low, 1)

        def pool_rotate(g, c):
            rotate(nc.gpsimd, 1, NC * g + c, c, k_products, k_roped)

        def pool_add_keys(g, slot):
            i, j = step_of(slot)
            n = SLOTS * g + slot
            lo = max(0, (j - TPC * i) * P)
            nc.gpsimd.wait_ge(exp_done, 2 * n + 2)
            if later(g) or added(g, slot) > 1:
                nc.gpsimd.wait_ge(sum_pool, added(g, slot) - 1)
            if slot == first_added(i) and (later(g) or i > ADDING[0]):
                nc.gpsimd.wait_ge(sums_done, sums_before(g, i))
            new = probs[:, slot % 4, 3, lo:CH]
            if slot == first_added(i):
                nc.gpsimd.tensor_tensor(key_sum[:, 3, :], new, ones[:, 0:1].broadcast_to([P, CH]), ALU.mult).then_inc(sum_pool, 1)
            else:
                nc.gpsimd.tensor_tensor(key_sum[:, 3, lo:CH], key_sum[:, 3, lo:CH], new, ALU.add).then_inc(sum_pool, 1)

        @block.gpsimd
        def _(pool):
            nc.gpsimd.memset(zeros[:], 0.0).then_inc(zero_made, 1)
            nc.gpsimd.memset(ones_b[:], 1.0)
            nc.gpsimd.memset(ident[:], 0.0)
            nc.gpsimd.memset(mask_b[:], 0.0)
            nc.gpsimd.memset(ident_b[:], 0.0)
            nc.gpsimd.memset(ones[:], 1.0).then_inc(mask_filled, 1)
            pool.wait_ge(mask_filled, 1)
            for m in (ident_b, ident):
                nc.gpsimd.affine_select(out=m[:], in_=m[:], compare_op=ALU.not_equal, fill=1.0, base=0,
                                        pattern=[[-1, P]], channel_multiplier=1)
            nc.gpsimd.affine_select(out=tri_b[:], in_=ones_b[:], compare_op=ALU.is_gt, fill=0.0, base=0,
                                    pattern=[[1, P]], channel_multiplier=-1).then_inc(tables_made, 1)
            nc.gpsimd.affine_select(out=mask_b[:], in_=mask_b[:], compare_op=ALU.is_ge, fill=MASKED, base=0,
                                    pattern=[[1, P]], channel_multiplier=-1).then_inc(consts_ready, 1)
            pool.wait_ge(tables_loaded, 16 * (2 * NC + 1))
            pool_split_w(0)
            for c in range(2):
                pool_rotate(0, c)
            def group(g):
                for slot in range(SLOTS):
                    if slot not in DIRECT:
                        pool_add_keys(g, slot)
                    for gg, c, stage in work_at(NORMALISE_AT, slot, g):
                        if stage == 1:
                            pool_rotate(gg, c)
                    if slot == SPLIT_W_AT and has_following(g):
                        pool_split_w(g + 1)
                    if slot == SPLIT_WO_AT and not has_following(g):
                        pool_split_wo(pool)

            each_group(pool, group)
            tail_gpsimd(pool)


def kernel(L0_attn_x, L0_attn_w_qkv, L0_attn_w_out, L0_attn_q_gain, L0_ffn_gate_w, L0_ffn_w_gate, L0_ffn_w_up,
           L0_ffn_w_down, L0_ffn_sw_gate, L0_ffn_sw_up, L0_ffn_sw_down):
    import concourse.bacc as bacc
    from concourse.bass_utils import run_bass_kernel_spmd

    half = HD // 2
    inv_freq = np.float32(10000.0) ** (-np.arange(half, dtype=np.float32) / np.float32(half))
    theta = np.arange(T, dtype=np.float32)[:, None] * inv_freq.astype(np.float32)[None, :]
    arrays = dict(x=L0_attn_x, w_qkv=L0_attn_w_qkv, w_out=L0_attn_w_out, q_gain=L0_attn_q_gain,
                  gate_w=L0_ffn_gate_w, w_gate=L0_ffn_w_gate, w_up=L0_ffn_w_up, w_down=L0_ffn_w_down,
                  sw_gate=L0_ffn_sw_gate, sw_up=L0_ffn_sw_up, sw_down=L0_ffn_sw_down,
                  rope_cos=np.cos(theta), rope_sin=np.sin(theta), numbers=np.arange(MAX_TILES, dtype=np.float32))
    arrays = {name: np.ascontiguousarray(a) for name, a in arrays.items()}
    nc = bacc.Bacc("TRN2", target_bir_lowering=False, num_devices=1)
    args = [nc.dram_tensor(name, a.shape, mybir.dt.from_np(a.dtype), kind="ExternalInput").ap()
            for name, a in arrays.items()]
    out = nc.dram_tensor("out", L0_attn_x.shape, F32, kind="ExternalOutput").ap()
    build(nc, *args, out)
    result = run_bass_kernel_spmd(nc, [arrays], core_ids=[0])
    return result.results[0]["out"]
```
